# Optimizing a Trainium2 kernel written in Bass

```python
import numpy as np
import jax
import jax.numpy as jnp

def _softmax(x, axis=-1):
    return jax.nn.softmax(x, axis=axis)

def _gelu(x):
    return jax.nn.gelu(x, approximate=True)

def _silu(x):
    return jax.nn.silu(x)

def _sigmoid(x):
    return jax.nn.sigmoid(x)

def _layernorm(x, axis=-1, eps=1e-05):
    m = jnp.mean(x, axis=axis, keepdims=True)
    v = jnp.var(x, axis=axis, keepdims=True)
    return (x - m) / jnp.sqrt(v + eps)

def _scatter_add(tgt, idx, src, axis=0):
    return tgt.at[idx].add(src)

def _segment_sum(src, seg, n):
    return jax.ops.segment_sum(src, seg, n)
kernel_name = 'mk_gnn_ffn_d1_gnn_r8_94fa1a'

def setup_inputs(seed: int=0):
    np.random.seed(seed)
    _w = jnp.asarray

    def _rec_inputs():
        import jax
        import jax.numpy as jnp
        _gk = jax.random.key(seed)
        x = -0.0002117 + 1 * jax.random.normal(jax.random.fold_in(_gk, 1), (6250, 256), jnp.float32)
        _s = jax.random.randint(jax.random.fold_in(_gk, 2), (50000,), 0, 6250, jnp.int32)
        _d = jax.random.randint(jax.random.fold_in(_gk, 3), (50000,), 0, 6250, jnp.int32)
        _loop = jnp.arange(6250, dtype=jnp.int32)
        src = jnp.concatenate([_s, _d, _loop])
        dst = jnp.concatenate([_d, _s, _loop])
        _o = jnp.argsort(dst, stable=True)
        src = src[_o]
        dst = dst[_o]
        return (x, src, dst)
    x, src, dst = _rec_inputs()

    def _L0_gnn_setup():
        import jax, jax.numpy as jnp
        import numpy as np
        N = 12500
        E = 200000
        D = 256
        BN_EPS = 1e-05

        def _batchnorm(x, gamma, beta):
            mu = jnp.mean(x, axis=0)
            var = jnp.var(x, axis=0)
            return (x - mu) * jax.lax.rsqrt(var + BN_EPS) * gamma + beta

        def _gin_conv(x, src, dst, n, W1, b1, gamma, beta, W2, b2):
            agg = jax.ops.segment_sum(x[src], dst, num_segments=n)
            h = x + agg
            h = jax.nn.relu(_batchnorm(h @ W1 + b1, gamma, beta))
            return jax.nn.relu(h @ W2 + b2)
        key = jax.random.key(seed)
        ks = jax.random.split(key, 8)
        x = jax.random.normal(ks[0], (N, D), dtype=jnp.float32)
        edge_index = jax.random.randint(ks[1], (2, E), 0, N, dtype=jnp.int64)
        s = 0.02
        inp = {'x': x, 'edge_index': edge_index, 'g0': jnp.ones((D,), jnp.float32), 'b0': jnp.zeros((D,), jnp.float32), 'W1a': jax.random.normal(ks[2], (D, D), jnp.float32) * s, 'b1a': jnp.zeros((D,), jnp.float32), 'g1': jnp.ones((D,), jnp.float32), 'bt1': jnp.zeros((D,), jnp.float32), 'W1b': jax.random.normal(ks[3], (D, D), jnp.float32) * s, 'b1b': jnp.zeros((D,), jnp.float32), 'W2a': jax.random.normal(ks[4], (D, D), jnp.float32) * s, 'b2a': jnp.zeros((D,), jnp.float32), 'g2': jnp.ones((D,), jnp.float32), 'bt2': jnp.zeros((D,), jnp.float32), 'W2b': jax.random.normal(ks[5], (D, D), jnp.float32) * s, 'b2b': jnp.zeros((D,), jnp.float32)}
        return inp
    _L0_gnn_all = _L0_gnn_setup()
    _L0_gnn_in = {k: v for k, v in _L0_gnn_all.items() if k in ('g0', 'b0', 'W1a', 'b1a', 'g1', 'bt1', 'W1b', 'b1b', 'W2a', 'b2a', 'g2', 'bt2', 'W2b', 'b2b')}
    del _L0_gnn_all

    def _L0_ffn_setup():
        import jax, jax.numpy as jnp
        import numpy as np
        B, S, D, F, E, K = (8, 256, 256, 1024, 8, 2)
        key = jax.random.key(seed)
        ks = jax.random.split(key, 10)
        s = 0.02
        return {'x': jax.random.normal(ks[0], (B, S, D), dtype=jnp.float32), 'Wr': jax.random.normal(ks[1], (D, E), dtype=jnp.float32) * s, 'W1s': jax.random.normal(ks[2], (D, F), dtype=jnp.float32) * s, 'b1s': jnp.zeros((F,), dtype=jnp.float32), 'W2s': jax.random.normal(ks[3], (F, D), dtype=jnp.float32) * s, 'b2s': jnp.zeros((D,), dtype=jnp.float32), 'W1p': jax.random.normal(ks[4], (E, D, F), dtype=jnp.float32) * s, 'b1p': jnp.zeros((E, F), dtype=jnp.float32), 'W2p': jax.random.normal(ks[5], (E, F, D), dtype=jnp.float32) * s, 'b2p': jnp.zeros((E, D), dtype=jnp.float32)}
    _L0_ffn_all = _L0_ffn_setup()
    _L0_ffn_in = {k: v for k, v in _L0_ffn_all.items() if k in ('Wr', 'W1s', 'b1s', 'W2s', 'b2s', 'W1p', 'b1p', 'W2p', 'b2p')}
    del _L0_ffn_all
    return {'x': x, 'src': src, 'dst': dst, 'L0_gnn_g0': _L0_gnn_in['g0'], 'L0_gnn_b0': _L0_gnn_in['b0'], 'L0_gnn_W1a': _L0_gnn_in['W1a'], 'L0_gnn_b1a': _L0_gnn_in['b1a'], 'L0_gnn_g1': _L0_gnn_in['g1'], 'L0_gnn_bt1': _L0_gnn_in['bt1'], 'L0_gnn_W1b': _L0_gnn_in['W1b'], 'L0_gnn_b1b': _L0_gnn_in['b1b'], 'L0_gnn_W2a': _L0_gnn_in['W2a'], 'L0_gnn_b2a': _L0_gnn_in['b2a'], 'L0_gnn_g2': _L0_gnn_in['g2'], 'L0_gnn_bt2': _L0_gnn_in['bt2'], 'L0_gnn_W2b': _L0_gnn_in['W2b'], 'L0_gnn_b2b': _L0_gnn_in['b2b'], 'L0_ffn_Wr': _L0_ffn_in['Wr'], 'L0_ffn_W1s': _L0_ffn_in['W1s'], 'L0_ffn_b1s': _L0_ffn_in['b1s'], 'L0_ffn_W2s': _L0_ffn_in['W2s'], 'L0_ffn_b2s': _L0_ffn_in['b2s'], 'L0_ffn_W1p': _L0_ffn_in['W1p'], 'L0_ffn_b1p': _L0_ffn_in['b1p'], 'L0_ffn_W2p': _L0_ffn_in['W2p'], 'L0_ffn_b2p': _L0_ffn_in['b2p']}

def reference(x, src, dst, L0_gnn_g0, L0_gnn_b0, L0_gnn_W1a, L0_gnn_b1a, L0_gnn_g1, L0_gnn_bt1, L0_gnn_W1b, L0_gnn_b1b, L0_gnn_W2a, L0_gnn_b2a, L0_gnn_g2, L0_gnn_bt2, L0_gnn_W2b, L0_gnn_b2b, L0_ffn_Wr, L0_ffn_W1s, L0_ffn_b1s, L0_ffn_W2s, L0_ffn_b2s, L0_ffn_W1p, L0_ffn_b1p, L0_ffn_W2p, L0_ffn_b2p):
    import jax
    import jax.numpy as jnp

    def _L0_gnn_ref(x, edge_index, g0, b0, W1a, b1a, g1, bt1, W1b, b1b, W2a, b2a, g2, bt2, W2b, b2b):
        import jax, jax.numpy as jnp
        import numpy as np
        N = 12500
        E = 200000
        D = 256
        BN_EPS = 1e-05

        def _batchnorm(x, gamma, beta):
            mu = jnp.mean(x, axis=0)
            var = jnp.var(x, axis=0)
            return (x - mu) * jax.lax.rsqrt(var + BN_EPS) * gamma + beta

        def _gin_conv(x, src, dst, n, W1, b1, gamma, beta, W2, b2):
            agg = jax.ops.segment_sum(x[src], dst, num_segments=n)
            h = x + agg
            h = jax.nn.relu(_batchnorm(h @ W1 + b1, gamma, beta))
            return jax.nn.relu(h @ W2 + b2)
        n = x.shape[0]
        src, dst = (edge_index[0], edge_index[1])
        h = _batchnorm(x, g0, b0)
        h = _gin_conv(h, src, dst, n, W1a, b1a, g1, bt1, W1b, b1b)
        h = jax.nn.relu(h)
        h = _gin_conv(h, src, dst, n, W2a, b2a, g2, bt2, W2b, b2b)
        return jax.nn.relu(h)

    def _L0_ffn_ref(x, Wr, W1s, b1s, W2s, b2s, W1p, b1p, W2p, b2p):
        import jax, jax.numpy as jnp
        import numpy as np
        B, S, D, F, E, K = (8, 256, 256, 1024, 8, 2)
        gelu = lambda t: jax.nn.gelu(t, approximate=False)
        shared = gelu(x @ W1s + b1s) @ W2s + b2s
        rw = jax.nn.softmax(x @ Wr, axis=-1)
        topw, topi = jax.lax.top_k(rw, K)
        topw = topw / jnp.sum(topw, axis=-1, keepdims=True)
        mask = jnp.sum(jax.nn.one_hot(topi, E, dtype=topw.dtype) * topw[..., None], axis=-2)
        h = gelu(jnp.einsum('bsd,edf->bsef', x, W1p) + b1p)
        priv = jnp.einsum('bsef,efd->bsed', h, W2p) + b2p
        routed = jnp.einsum('bsed,bse->bsd', priv, mask)
        return shared + routed
    edge_index = jnp.stack([src, dst])
    x = x + _L0_gnn_ref(_layernorm(x, axis=-1), edge_index, L0_gnn_g0, L0_gnn_b0, L0_gnn_W1a, L0_gnn_b1a, L0_gnn_g1, L0_gnn_bt1, L0_gnn_W1b, L0_gnn_b1b, L0_gnn_W2a, L0_gnn_b2a, L0_gnn_g2, L0_gnn_bt2, L0_gnn_W2b, L0_gnn_b2b)
    x = x + _L0_ffn_ref(_layernorm(x, axis=-1)[None], L0_ffn_Wr, L0_ffn_W1s, L0_ffn_b1s, L0_ffn_W2s, L0_ffn_b2s, L0_ffn_W1p, L0_ffn_b1p, L0_ffn_W2p, L0_ffn_b2p)[0]
    return x

_drawn_inputs = setup_inputs


def setup_inputs(seed=0):
    import zlib

    import numpy as np

    out = dict(_drawn_inputs(seed))
    spreads = {'L0_gnn_g0': (1.0, 0.2),
     'L0_gnn_b0': (0.0, 0.463),
     'L0_gnn_b1a': (0.0, 0.8),
     'L0_gnn_g1': (1.0, 0.2),
     'L0_gnn_bt1': (0.0, 0.392),
     'L0_gnn_b1b': (0.0, 0.1),
     'L0_gnn_b2a': (0.0, 0.8),
     'L0_gnn_g2': (1.0, 0.2),
     'L0_gnn_bt2': (0.0, 0.408),
     'L0_gnn_b2b': (0.0, 0.1),
     'L0_ffn_b1s': (0.0, 0.1),
     'L0_ffn_b2s': (0.0, 0.1),
     'L0_ffn_b1p': (0.0, 0.332),
     'L0_ffn_b2p': (0.0, 0.1)}
    factors = {}
    for name, (base, spread) in spreads.items():
        noise = np.random.default_rng([zlib.crc32(name.encode()), seed]).standard_normal(out[name].shape)
        drawn = base * np.exp(spread * noise) if base else spread * noise
        out[name] = jnp.asarray(drawn.astype(out[name].dtype))
    for name, factor in factors.items():
        out[name] = (out[name] * factor).astype(out[name].dtype)
    return out
```

```python
N, D, E = 6250, 256, 106250
NODE = 125
TILES = N // NODE
KD = D // 128
CH = 2 * NODE
CHUNKS = N // CH
PIECES = 5
GROUP = 4
RING = 4
EDGE_TILES = -(-E // (128 * GROUP * RING)) * GROUP * RING
GROUPS = EDGE_TILES // GROUP
ROUNDS = GROUPS // RING
F, NF, EXPERTS, TOPK = 1024, 1024 // 128, 8, 2
ROW = D + 1 + EXPERTS
SLOT_TILES = (TOPK * N + EXPERTS * 127) // 128 + 1
EPS = 1e-5
ROUND = 12582912.0
FAR = 1 << 20
VECS = 8


def build(nc, x, src, dst, vecs, w1a, w1b, w2a, w2b, rows, wr, w1s, w2s, b1, w1p, w2p, b2p, out):
    from contextlib import ExitStack

    import concourse.bass as bass
    from concourse import mybir

    F32, I32 = mybir.dt.float32, mybir.dt.int32
    ACT, ALU, AX = mybir.ActivationFunctionType, mybir.AluOpType, mybir.AxisListType
    ds = bass.ds

    with ExitStack() as ctx:
        def sb(name, shape, dt=F32):
            return ctx.enter_context(nc.sbuf_tensor(name, shape, dt))

        def sem(name):
            return ctx.enter_context(nc.semaphore(name))

        tables = [nc.dram_tensor(f"table{l}", (N, D), F32).ap() for l in range(2)]
        slots = nc.dram_tensor("slots", (SLOT_TILES * 128, ROW), F32).ap()

        XA = sb("X", [128, TILES, D])
        X = XA[0:NODE]
        HA = sb("H", [128, TILES, ROW])
        H = HA[0:NODE]
        FT = sb("FT", [128, KD * N])
        feat = FT[:, :].rearrange("p (k n) -> p k n", k=KD)
        E_ = sb("edge_arena", [128, 2 * EDGE_TILES + RING * GROUP * D + GROUP * NODE])
        G_ = sb("gnn_arena", [128, 4 * KD * D + 2 * KD * CH])

        def cut(arena, at, shape):
            size = 1
            for s in shape:
                size *= s
            v = arena[:, at:at + size]
            names = "abcd"[:len(shape)]
            if len(shape) > 1:
                v = v.rearrange(f"p ({' '.join(names)}) -> p {' '.join(names)}",
                                **{n: s for n, s in zip(names, shape)})
            return v

        SRC = cut(E_, 0, [EDGE_TILES]).bitcast(I32)
        DST = cut(E_, EDGE_TILES, [EDGE_TILES])
        GATHERED = cut(E_, 2 * EDGE_TILES, [RING, GROUP, D])
        ONEHOT = cut(E_, 2 * EDGE_TILES + RING * GROUP * D, [GROUP, NODE])
        W1S = cut(E_, 0, [KD, F])
        W2S = cut(E_, KD * F, [NF, D])
        GELU = cut(E_, KD * F + NF * D, [NF, CH])
        W = [[cut(G_, (2 * l + i) * KD * D, [KD, D]) for i in range(2)] for l in range(2)]
        RT = [cut(G_, 4 * KD * D + p * KD * CH, [KD, CH]) for p in range(2)]
        TE = TILES * EXPERTS
        LOGIT, TOP1, TOP2, CAND, POS, CUM, CUM2 = [
            cut(G_, i * TE, [TILES, EXPERTS])[0:NODE] for i in range(7)]
        DSTI = cut(FT, 0, [EDGE_TILES]).bitcast(I32)
        TILEOF = cut(FT, EDGE_TILES, [EDGE_TILES])
        RANGES = cut(FT, 2 * EDGE_TILES, [2, GROUPS])
        AT = 2 * EDGE_TILES + 2 * GROUPS
        EXTREMES = cut(FT, AT, [4])
        STEPS = cut(FT, AT + 4, [6, GROUPS])[0:1]
        DIAG = cut(FT, AT + 4 + 6 * GROUPS, [2 * KD, 128])
        SPREAD = cut(FT, AT + 4 + 6 * GROUPS + 512, [2, D])
        IOTAI = cut(FT, AT + 4 + 6 * GROUPS + 1024, [256]).bitcast(I32)
        assert AT + 4 + 6 * GROUPS + 1024 + 256 <= KD * N
        HX = HA[:, :, :].rearrange("p t r -> p (t r)")
        at, hx = 0, {}
        for name, shape in (("w1_0", [KD, F]), ("w1_1", [KD, F]), ("w2_0", [NF, D]), ("w2_1", [NF, D]),
                            ("b2", [EXPERTS, D]), ("meta", [SLOT_TILES, 1 + EXPERTS]), ("row", [ROW]),
                            ("feat", [KD, 128]), ("gelu", [NF, 128]), ("out", [D])):
            hx[name] = cut(HX, at, shape)
            size = 1
            for n in shape:
                size *= n
            at += size
        assert at <= TILES * ROW
        W1X, W2X = [hx["w1_0"], hx["w1_1"]], [hx["w2_0"], hx["w2_1"]]
        B2X, META, SLOTROW, SLOTFEAT = hx["b2"], hx["meta"], hx["row"], hx["feat"]
        SLOTGELU, SLOTOUT = hx["gelu"], hx["out"]
        TABLE = sb("TABLE", [1, 3, GROUPS], I32)
        IDX = sb("IDX", [128, RING, GROUP], I32)
        STAGE = sb("STAGE", [128, 2, 2, D])
        TMP = sb("TMP", [NODE, 2, 2, D])
        ROWS = sb("ROWS", [NODE, 3, D])
        IDENT = sb("IDENT", [128, 128])
        ONES = sb("ONES", [128, 128])
        TRI = sb("TRI", [NODE, NODE])
        IOTA = sb("IOTA", [128, NODE])
        NEG = sb("NEG", [128, TILES])
        MISC = sb("MISC", [128, 64])
        VEC = sb("VEC", [128, VECS, KD])
        B1 = sb("B1", [128, 1 + EXPERTS, NF])
        WR = sb("WR", [128, KD, EXPERTS])
        LNSTAT = sb("LNSTAT", [NODE, TILES, 6])
        LN = sb("LN", [NODE, 4, TILES])
        MV = sb("MV", [NODE, TILES, 2])
        BNSTAT = sb("BNSTAT", [128, KD, CHUNKS, 6])
        BN = sb("BN", [128, 6, KD, 2])
        FILL = cut(G_, 4 * KD * D, [ROW])
        POSI = sb("POSI", [NODE, TOPK, TILES], I32)
        OFFI = sb("OFFI", [1, 16], I32)
        EPST = MISC[:, 0:1]
        OFFF = MISC[:, 8:32].rearrange("p (a b) -> p a b", a=3)
        DOWN = MISC[0:NODE, 40:48]
        assert 7 * TE + 4 * TILES <= 4 * KD * D + 2 * KD * CH
        S0, S1, S2, S3 = [cut(G_, 7 * TE + i * TILES, [TILES])[0:NODE] for i in range(4)]
        POS32 = sb("POS32", [NODE, 2, TOPK], I32)
        TOKEN = sb("TOKEN", [128, 1], I32)
        SENDROW = [cut(STAGE[:, :, :, :].rearrange("p a b d -> p (a b d)"), p * 2 * D, [ROW])[0:NODE]
                   for p in range(2)]
        SLOTSUM = cut(STAGE[:, :, :, :].rearrange("p a b d -> p (a b d)"), 0, [D])

        PS = ctx.enter_context(nc.psum_tensor("PS", [128, 8, 512], F32))

        x_in = [sem(f"x_in{i}") for i in range(PIECES)]
        edges_in, vec_in, rows_in, gnnw_in, ffn_small_in = map(
            sem, ("edges_in", "vec_in", "rows_in", "gnnw_in", "ffn_small_in"))
        pool_const, const_ready, dve_chain = map(sem, ("pool_const", "const_ready", "dve_chain"))
        ln_stats, moments_in, ln_std, ln_ready = map(sem, ("ln_stats", "moments_in", "ln_std", "ln_ready"))
        staged0, turned0, bn0_counted = map(sem, ("staged0", "turned0", "bn0_counted"))
        bn_std, bn_ready = map(sem, ("bn_std", "bn_ready"))
        dve_bn = sem("bn_moments")
        diag_ready, spread_done, spread_ready = map(sem, ("diag_ready", "spread_done", "spread_ready"))
        centred, h0_ready = map(sem, ("centred", "h0_ready"))
        range_ready, range_turned, row_ready, row_turned, table_ready = map(
            sem, ("range_ready", "range_turned", "row_ready", "row_turned", "table_ready"))
        stored = [sem(f"stored{l}") for l in range(2)]
        index_ready = sem("index_ready")
        gathered = [sem(f"gathered{r}") for r in range(RING)]
        group_used = sem("group_used")
        onehot_ready = [sem(f"onehot_ready{l}") for l in range(2)]
        multiplied = [sem(f"multiplied{l}") for l in range(2)]
        added = [sem(f"added{l}") for l in range(2)]
        agg_done = sem("agg_done")
        staged, turned, feat_ready, z_ready, z_kept, bn_counted = map(
            sem, ("staged", "turned", "feat_ready", "z_ready", "z_kept", "bn_counted"))
        relu_ready, y_ready, y_taken, h1_ready, x2_ready, x2_stats = map(
            sem, ("relu_ready", "y_ready", "y_taken", "h1_ready", "x2_ready", "x2_stats"))
        moments_mid, ln2_std, ln2_ready, row_norm = map(sem, ("moments_mid", "ln2_std", "ln2_ready", "row_norm"))
        staged2, turned2, feat2, half2, logit_done, logit_kept = map(
            sem, ("staged2", "turned2", "feat2", "half2", "logit_done", "logit_kept"))
        logit_max, exp_ready, mask_ready, counted, pos_ready, off_ready = map(
            sem, ("logit_max", "exp_ready", "mask_ready", "counted", "pos_ready", "off_ready"))
        shared_in, hidden, gelu_done, ffn_done, ffn_taken, out_ready, out_stored, spare_zero = map(
            sem, ("shared_in", "hidden", "gelu_done", "ffn_done", "ffn_taken", "out_ready",
                  "out_stored", "spare_zero"))
        filled, row_copied = map(sem, ("filled", "row_copied"))
        scattered = [sem(f"scattered{p}") for p in range(2)]
        scatter_end = sem("scatter_end")
        wait_carrier = sem("wait_carrier")
        expert_in = [sem(f"expert_in{q}") for q in range(2)]
        b2_in, slot_in, slot_turned, slot_feat, slot_meta = map(
            sem, ("b2_in", "slot_in", "slot_turned", "slot_feat", "slot_meta"))
        slot_hidden, slot_gelu, slot_ffn, slot_taken, slot_row, slot_added = map(
            sem, ("slot_hidden", "slot_gelu", "slot_ffn", "slot_taken", "slot_row", "slot_added"))
        slot_free = sem("slot_free")

        def wait_count(eng, semaphore, value):
            if isinstance(value, int) and value <= 0:
                return
            eng.wait_ge(semaphore, value)

        def chunks(eng, body):
            body(0, 0)
            body(1, 1)
            with eng.Fori(1, CHUNKS // 2) as i:
                body(2 * i, 0)
                body(2 * i + 1, 1)
            body(CHUNKS - 1, 0)

        def last(c):
            return isinstance(c, int) and c == CHUNKS - 1

        PARTS = ((0, 112), (112, NODE))

        def by_tile(dram):
            return dram[0:N, :].rearrange("(t p) d -> p t d", p=NODE)

        turn_psum = [PS[:, p, 0:KD * CH].rearrange("q (k n) -> q k n", k=KD) for p in range(2)]
        z_psum = [PS[:, 2 + p, 0:KD * CH].rearrange("q (k n) -> q k n", k=KD) for p in range(2)]
        y_psum = [PS[0:NODE, 4 + p, :].rearrange("q (i d) -> q i d", i=2) for p in range(2)]
        logit_psum = [PS[0:NODE, 6 + p, 0:2 * EXPERTS].rearrange("q (i e) -> q i e", i=2) for p in range(2)]
        hidden_psum = [PS[:, f % 4, 0:CH] for f in range(NF)]
        ffn_psum = PS[0:NODE, 4, :].rearrange("q (i d) -> q i d", i=2)
        slot_turn_psum = PS[:, 5, 0:KD * 128].rearrange("q (k n) -> q k n", k=KD)
        slot_hidden_psum = [PS[:, f % 4, 0:128] for f in range(NF)]
        slot_ffn_psum = PS[:, 6, 0:D]


        block = ctx.enter_context(nc.Block())

        @block.sync
        def _(sp):
            for i in range(PIECES):
                t = slice(i * TILES // PIECES, (i + 1) * TILES // PIECES)
                for a, b in PARTS:
                    sp.dma_start(X[a:b, t, :], by_tile(x)[a:b, t, :]).then_inc(x_in[i], 16)

            def store_table(layer, source_ready, base):
                def store(c, p):
                    wait_count(sp, source_ready, base * (c + 1))
                    for a, b in PARTS:
                        sp.dma_start(by_tile(tables[layer])[a:b, ds(2 * c, 2), :],
                                     H[a:b, ds(2 * c, 2), 0:D]).then_inc(stored[layer], 16)
                return store

            chunks(sp, store_table(0, h0_ready, 2))
            chunks(sp, store_table(1, h1_ready, 1))

            sp.wait_ge(agg_done, 2)
            sp.dma_start(W1S, w1s.rearrange("(k p) f -> p k f", p=128)).then_inc(shared_in, 16)
            sp.dma_start(W2S, w2s.rearrange("(f p) d -> p f d", p=128)).then_inc(shared_in, 16)

            def store_out(c, p):
                sp.wait_ge(out_ready, c + 2)
                for a, b in PARTS:
                    sp.dma_start(by_tile(out)[a:b, ds(2 * c, 2), :],
                                 X[a:b, ds(2 * c, 2), :]).then_inc(out_stored, 16)

            def load_expert(e, q):
                sp.dma_start(W1X[q], w1p[ds(e, 1)].rearrange("o (k p) f -> p (o k) f", p=128))\
                    .then_inc(expert_in[q], 16)
                sp.dma_start(W2X[q], w2p[ds(e, 1)].rearrange("o (f p) d -> p (o f) d", p=128))\
                    .then_inc(expert_in[q], 16)

            def load_slots(s):
                sp.dma_start(SLOTROW, slots[ds(128 * s, 128), :]).then_inc(slot_in, 16)

            with sp.Fori(0, CHUNKS) as c:
                store_out(c, 0)
            sp.wait_ge(scatter_end, 1)
            sp.dma_start(B2X, b2p.partition_broadcast(128)).then_inc(b2_in, 16)
            load_expert(0, 0)
            load_slots(0)

            def expert(e, q):
                first = sp.value_load(OFFI[0:1, ds(e, 1)], min_val=0, max_val=SLOT_TILES - 1)
                end = sp.value_load(OFFI[0:1, ds(e + 1, 1)], min_val=1, max_val=SLOT_TILES - 1)
                if not (isinstance(e, int) and e == EXPERTS - 1):
                    sp.wait_ge(slot_ffn, first + 1)
                    load_expert(e + 1, 1 - q)
                with sp.Fori(first, end) as s:
                    sp.wait_ge(slot_turned, s + 1)
                    sp.wait_ge(slot_meta, s + 1)
                    load_slots(s + 1)

            with sp.Fori(0, EXPERTS // 2 - 1) as i:
                expert(2 * i, 0)
                expert(2 * i + 1, 1)
            expert(EXPERTS - 2, 0)
            expert(EXPERTS - 1, 1)

        @block.gpsimd
        def _(pool):
            nc.gpsimd.memset(IDENT[:, :], 0.0).then_inc(pool_const, 1)
            nc.gpsimd.memset(TRI[:, :], 1.0).then_inc(pool_const, 1)
            nc.gpsimd.memset(ONES[:, :], 1.0).then_inc(pool_const, 1)
            nc.gpsimd.memset(FILL[:, :], 0.0).then_inc(pool_const, 1)
            nc.gpsimd.memset(EPST, EPS).then_inc(pool_const, 1)
            nc.gpsimd.iota(IOTAI[:, 0:NODE], [[1, NODE]], base=0, channel_multiplier=0)\
                .then_inc(pool_const, 1)
            nc.gpsimd.iota(IOTAI[:, 128:128 + TILES], [[-NODE, TILES]], base=0, channel_multiplier=0)\
                .then_inc(pool_const, 1)
            nc.gpsimd.iota(IOTAI[:, 180:181], [[1, 1]], base=N, channel_multiplier=1)\
                .then_inc(pool_const, 1)
            nc.gpsimd.iota(IOTAI[:, 184:192], [[-1, EXPERTS]], base=EXPERTS, channel_multiplier=0)\
                .then_inc(pool_const, 1)
            nc.gpsimd.iota(IOTAI[:, 192:192 + TILES], [[NODE, TILES]], base=0, channel_multiplier=1)\
                .then_inc(pool_const, 1)
            pool.wait_ge(pool_const, 10)
            nc.gpsimd.affine_select(out=IDENT[:, :], in_=IDENT[:, :], compare_op=ALU.not_equal, fill=1.0,
                                    base=0, pattern=[[-1, 128]], channel_multiplier=1)\
                .then_inc(const_ready, 1)
            nc.gpsimd.affine_select(out=TRI[:, :], in_=TRI[:, :], compare_op=ALU.is_gt, fill=0.0,
                                    base=0, pattern=[[1, NODE]], channel_multiplier=-1)\
                .then_inc(const_ready, 1)

            for layer in range(2):
                pool.wait_ge(stored[layer], 32 * CHUNKS)

                def gather(i, layer=layer):
                    for r in range(RING):
                        g = RING * i + r + layer * GROUPS
                        wait_count(pool, group_used, g - RING + 1)
                        pool.wait_ge(index_ready, g + 1)
                        pool.sem_inc(wait_carrier, 1)
                        for k in range(GROUP):
                            nc.gpsimd.indirect_dma_start(
                                out=GATHERED[:, r, k, :], out_offset=None, in_=tables[layer],
                                in_offset=bass.IndirectOffsetOnAxis(ap=IDX[:, r, k:k + 1], axis=0))\
                                .then_inc(gathered[r], 16)

                gather(0)
                with pool.Fori(1, ROUNDS) as i:
                    gather(i)

            pool.wait_ge(pos_ready, 1)
            pool.wait_ge(filled, 32)

            def scatter(t, p):
                wait_count(pool, scattered[p], 32 * (t // 2) if isinstance(t, int) else 16 * (t - p))
                nc.gpsimd.tensor_copy(SENDROW[p].unsqueeze(1), H[:, ds(t, 1), :]).then_inc(row_copied, 1)
                nc.gpsimd.tensor_copy(POS32[:, p, :].unsqueeze(2), POSI[:, :, ds(t, 1)])\
                    .then_inc(row_copied, 1)
                pool.wait_ge(row_copied, 2 * t + 2)
                pool.sem_inc(wait_carrier, 1)
                for k in range(TOPK):
                    nc.gpsimd.indirect_dma_start(
                        out=slots, out_offset=bass.IndirectOffsetOnAxis(ap=POS32[:, p, k:k + 1], axis=0),
                        in_=SENDROW[p], in_offset=None).then_inc(scattered[p], 16)

            scatter(0, 0)
            scatter(1, 1)
            with pool.Fori(1, TILES // 2) as i:
                scatter(2 * i, 0)
                scatter(2 * i + 1, 1)
            for p in range(2):
                pool.wait_ge(scattered[p], 32 * TILES // 2)
            pool.sem_inc(scatter_end, 1)

            pool.wait_ge(out_stored, 32 * CHUNKS)
            pool.wait_ge(spare_zero, 16)
            pool.wait_ge(off_ready, 1)
            pool.sem_inc(slot_free, 1)
            total = pool.value_load(OFFI[0:1, EXPERTS:EXPERTS + 1], min_val=1, max_val=SLOT_TILES - 1)
            with pool.Fori(0, total) as s:
                pool.wait_ge(slot_row, 2 * s + 3)
                pool.sem_inc(wait_carrier, 1)
                nc.gpsimd.indirect_dma_start(
                    out=out, out_offset=bass.IndirectOffsetOnAxis(ap=TOKEN[:, 0:1], axis=0),
                    in_=SLOTOUT, in_offset=None, compute_op=ALU.add).then_inc(slot_added, 16)
                pool.wait_ge(slot_added, 16 * (s + 1))
                pool.sem_inc(slot_free, 1)

        @block.scalar
        def _(act):
            act.dma_start(SRC, src).then_inc(edges_in, 16)
            act.dma_start(DSTI, dst).then_inc(edges_in, 16)
            act.dma_start(VEC[:, :, :], vecs).then_inc(vec_in, 16)
            for i, w in enumerate((w1a, w1b, w2a, w2b)):
                act.dma_start(W[i // 2][i % 2], w.rearrange("(k p) o -> p k o", p=128)).then_inc(gnnw_in, 16)
            act.dma_start(ROWS[:, :, :], rows.partition_broadcast(NODE)).then_inc(rows_in, 16)
            act.dma_start(WR[:, :, :], wr.rearrange("(k p) e -> p k e", p=128)).then_inc(ffn_small_in, 16)
            act.dma_start(B1[:, :, :], b1).then_inc(ffn_small_in, 16)
            act.wait_ge(const_ready, 3)
            half = SLOT_TILES // 2
            for i in range(2):
                n = half if i == 0 else SLOT_TILES - half
                act.dma_start(slots[i * half * 128:(i * half + n) * 128, :].rearrange("(s p) r -> p s r", p=128),
                              FILL[:, :].unsqueeze(1).to_broadcast([128, n, ROW])).then_inc(filled, 16)
            act.dma_start(out[N:N + 128, :], FILL[:, 0:D]).then_inc(spare_zero, 16)

            act.wait_ge(moments_in, 1)
            nc.scalar.activation(LN[:, 0, :], MV[:, :, 1], ACT.Sqrt, bias=EPST[0:NODE]).then_inc(ln_std, 1)
            act.wait_ge(ln_ready, 1)

            def normalise(c, p, turned_count, done):
                wait_count(act, turned_count, c - 1)
                for i in range(2):
                    t = 2 * c + i
                    nc.scalar.activation(STAGE[0:NODE, p, i, :].unsqueeze(1), X[:, ds(t, 1), :], ACT.Identity,
                                         scale=LN[:, 1, ds(t, 1)], bias=LN[:, 2, ds(t, 1)]).then_inc(done, 1)

            chunks(act, lambda c, p: normalise(c, p, turned0, staged0))

            def bn_sqrt(n):
                act.wait_ge(dve_bn, 2 * n + 2)
                nc.scalar.activation(BN[:, 2, :, 0], BN[:, 0, :, 1], ACT.Sqrt, bias=EPST).then_inc(bn_std, 1)

            bn_sqrt(0)
            act.wait_ge(spread_done, 1)
            nc.scalar.copy(SPREAD[0:NODE, :, :], PS[0:NODE, 4, :].rearrange("p (a d) -> p a d", a=2))\
                .then_inc(spread_ready, 1)

            for layer in range(2):
                if layer == 0:
                    act.wait_ge(edges_in, 32)

                def indices(i, layer=layer):
                    for r in range(RING):
                        wait_count(act, gathered[r], 16 * GROUP * (i + layer * ROUNDS))
                        nc.scalar.copy(IDX[:, r, :], SRC[:, ds(GROUP * (RING * i + r), GROUP)])\
                            .then_inc(index_ready, 1)

                indices(0)
                with act.Fori(1, ROUNDS) as i:
                    indices(i)

                act.wait_ge(agg_done, layer + 1)
                base = layer * CHUNKS

                def stage(c, p, base=base):
                    wait_count(act, turned, c + base - 1)
                    nc.scalar.copy(STAGE[0:NODE, p, :, :], H[:, ds(2 * c, 2), 0:D]).then_inc(staged, 1)

                def keep_z(c, p, base=base, layer=layer):
                    if not last(c):
                        stage(c + 1, 1 - p)
                    act.wait_ge(z_ready, c + base + 1)
                    for o in range(KD):
                        nc.scalar.activation(feat[:, o, ds(CH * c, CH)], z_psum[p][:, o, :], ACT.Identity,
                                             bias=VEC[:, 2 + 3 * layer, o:o + 1]).then_inc(z_kept, 1)

                act.wait_ge(vec_in, 16)
                stage(0, 0)
                chunks(act, keep_z)
                bn_sqrt(layer + 1)
                act.wait_ge(bn_ready, layer + 2)
                if layer == 0:
                    act.wait_ge(filled, 32)
                    act.wait_ge(spare_zero, 16)

                def relu_norm(c, p, base=base):
                    wait_count(act, y_ready, c + base - 1)
                    for k in range(KD):
                        nc.scalar.activation(RT[p][:, k, :], feat[:, k, ds(CH * c, CH)], ACT.Relu,
                                             scale=BN[:, 3, k, 0:1], bias=BN[:, 5, k, 0:1]).then_inc(relu_ready, 1)

                def keep_h1(c, p):
                    if not last(c):
                        relu_norm(c + 1, 1 - p)
                    act.wait_ge(y_taken, c + 1)
                    nc.scalar.activation(H[:, ds(2 * c, 2), 0:D], TMP[:, p, :, :], ACT.Relu).then_inc(h1_ready, 1)

                if layer == 0:
                    relu_norm(0, 0)
                    chunks(act, keep_h1)
                else:
                    chunks(act, relu_norm)

            act.wait_ge(moments_mid, 1)
            nc.scalar.activation(LN[:, 0, :], MV[:, :, 1], ACT.Sqrt, bias=EPST[0:NODE]).then_inc(ln2_std, 1)
            act.wait_ge(ln2_ready, 1)

            def turn_rows(c, p):
                if not last(c):
                    normalise(c + 1, 1 - p, turned2, staged2)
                act.wait_ge(turned2, c + 1)
                nc.scalar.copy(feat[:, :, ds(CH * c, CH)], turn_psum[p]).then_inc(feat2, 1)

            normalise(0, 0, turned2, staged2)
            chunks(act, turn_rows)
            act.wait_ge(logit_max, 1)
            nc.scalar.activation(LOGIT, LOGIT, ACT.Exp).then_inc(exp_ready, 1)

            act.wait_ge(ffn_small_in, 32)
            with act.Fori(0, CHUNKS) as c:
                for f in range(NF):
                    act.wait_ge(hidden, NF * c + f + 1)
                    nc.scalar.activation(GELU[:, f, :], hidden_psum[f], ACT.Gelu, bias=B1[:, 0, f:f + 1])\
                        .then_inc(gelu_done, 1)

            def expert(e):
                first = act.value_load(OFFI[0:1, ds(e, 1)], min_val=0, max_val=SLOT_TILES - 1)
                end = act.value_load(OFFI[0:1, ds(e + 1, 1)], min_val=1, max_val=SLOT_TILES - 1)
                with act.Fori(first, end) as s:
                    for f in range(NF):
                        act.wait_ge(slot_hidden, NF * s + f + 1)
                        nc.scalar.activation(SLOTGELU[:, f, :], slot_hidden_psum[f], ACT.Gelu,
                                             bias=B1[:, ds(e + 1, 1), f]).then_inc(slot_gelu, 1)

            act.wait_ge(off_ready, 1)
            with act.Fori(0, EXPERTS) as e:
                expert(e)

        @block.tensor
        def _(pe):
            for l in range(2):
                pe.sem_inc(multiplied[l], GROUP)
            pe.sem_inc(slot_ffn, 1)
            pe.wait_ge(const_ready, 2)

            def turn(c, p, ready, turned_count, taken, per, base=0):
                pe.wait_ge(ready, per * (c + base + 1))
                wait_count(pe, taken[0], taken[1] * (c + base - 1))
                for i in range(2):
                    for k in range(KD):
                        t = nc.tensor.transpose(turn_psum[p][:, k, i * NODE:(i + 1) * NODE],
                                                STAGE[0:NODE, p, i, k * 128:(k + 1) * 128],
                                                IDENT[0:NODE, 0:NODE])
                t.then_inc(turned_count, 1)

            chunks(pe, lambda c, p: turn(c, p, staged0, turned0, (bn0_counted, KD), 2))

            pe.wait_ge(range_ready, 2)
            for i in range(4):
                t = nc.tensor.transpose(PS[0:GROUPS // 2, 5, i * 128:(i + 1) * 128],
                                        RANGES[:, i // 2, (i % 2) * (GROUPS // 2):(i % 2 + 1) * (GROUPS // 2)],
                                        IDENT[:, :])
            t.then_inc(range_turned, 1)
            pe.wait_ge(row_ready, 2)
            for i in range(4):
                t = nc.tensor.transpose(PS[0:1, 6, i * (GROUPS // 2):(i + 1) * (GROUPS // 2)],
                                        EXTREMES[0:GROUPS // 2, i:i + 1], IDENT[0:GROUPS // 2, 0:GROUPS // 2])
            t.then_inc(row_turned, 1)

            pe.wait_ge(diag_ready, 2 * KD)
            for i in range(2 * KD):
                t = nc.tensor.matmul(PS[0:NODE, 4, i * 128:(i + 1) * 128], ONES[:, 0:NODE], DIAG[:, i, :],
                                     start=True, stop=True)
            t.then_inc(spread_done, 1)

            pe.wait_ge(table_ready, 3)
            pe.wait_ge(gnnw_in, 16 * 4)
            for layer in range(2):
                def multiply(i, layer=layer):
                    for r in range(RING):
                        g = RING * i + r
                        first = pe.value_load(TABLE[0:1, 0, ds(g, 1)], min_val=0, max_val=GROUPS * TILES)
                        end = pe.value_load(TABLE[0:1, 1, ds(g, 1)], min_val=1, max_val=GROUPS * TILES)
                        with pe.Fori(first, end) as s:
                            pe.wait_ge(gathered[r], 16 * GROUP * (i + 1 + layer * ROUNDS))
                            pe.wait_ge(added[layer], s + 1)
                            for k in range(GROUP):
                                pe.wait_ge(onehot_ready[layer], GROUP * s + k + 1)
                                nc.tensor.matmul(PS[0:NODE, 7, 0:D], ONEHOT[:, k, :], GATHERED[:, r, k, :],
                                                 start=k == 0, stop=k == GROUP - 1)\
                                    .then_inc(multiplied[layer], 1)

                with pe.Fori(0, ROUNDS) as i:
                    multiply(i)

                base = layer * CHUNKS

                def first_product(c, p, base=base, layer=layer):
                    if not last(c):
                        turn(c + 1, 1 - p, staged, turned, (feat_ready, 1), 1, base)
                    pe.wait_ge(feat_ready, c + base + 1)
                    wait_count(pe, z_kept, KD * (c + base - 1))
                    for o in range(KD):
                        for k in range(KD):
                            t = nc.tensor.matmul(z_psum[p][:, o, :], W[layer][0][:, k, o * 128:(o + 1) * 128],
                                                 feat[:, k, ds(CH * c, CH)], start=k == 0, stop=k == KD - 1)
                    t.then_inc(z_ready, 1)

                turn(0, 0, staged, turned, (feat_ready, 1), 1, base)
                chunks(pe, first_product)

                def second_product(c, p, base=base, layer=layer):
                    pe.wait_ge(relu_ready, KD * (c + base + 1))
                    wait_count(pe, y_taken, c + base - 1)
                    for i in range(2):
                        for k in range(KD):
                            t = nc.tensor.matmul(y_psum[p][:, i, :], RT[p][:, k, i * NODE:(i + 1) * NODE],
                                                 W[layer][1][:, k, :], start=k == 0, stop=k == KD - 1)
                    t.then_inc(y_ready, 1)

                chunks(pe, second_product)

            pe.wait_ge(ffn_small_in, 32)

            def router(c, p):
                if not last(c):
                    turn2(c + 1, 1 - p)
                pe.wait_ge(half2, c + 1)
                wait_count(pe, logit_kept, c - 1)
                for i in range(2):
                    for k in range(KD):
                        t = nc.tensor.matmul(logit_psum[p][:, i, :], RT[p][:, k, i * NODE:(i + 1) * NODE],
                                             WR[:, k, :], start=k == 0, stop=k == KD - 1)
                t.then_inc(logit_done, 1)

            def turn2(c, p):
                wait_count(pe, feat2, c - 1)
                turn(c, p, staged2, turned2, (half2, 1), 2)

            turn2(0, 0)
            chunks(pe, router)

            def shared(c):
                pe.wait_ge(feat2, CHUNKS)
                for f in range(NF):
                    if f >= 4:
                        pe.wait_ge(gelu_done, NF * c + f - 3)
                    for k in range(KD):
                        t = nc.tensor.matmul(hidden_psum[f], W1S[:, k, f * 128:(f + 1) * 128],
                                             feat[:, k, ds(CH * c, CH)], start=k == 0, stop=k == KD - 1)
                    t.then_inc(hidden, 1)
                wait_count(pe, ffn_taken, c)
                for i in range(2):
                    for f in range(NF):
                        if i == 0:
                            pe.wait_ge(gelu_done, NF * c + f + 1)
                        t = nc.tensor.matmul(ffn_psum[:, i, :], GELU[:, f, i * NODE:(i + 1) * NODE],
                                             W2S[:, f, :], start=f == 0, stop=f == NF - 1)
                t.then_inc(ffn_done, 1)

            pe.wait_ge(shared_in, 32)
            shared(0)
            pe.wait_ge(mask_ready, 1)
            mask = CUM.rearrange("p t e -> p (t e)")
            nc.tensor.matmul(PS[0:NODE, 6, 0:TE], TRI[:, :], mask, start=True, stop=True)
            nc.tensor.matmul(PS[:, 7, 0:TE], ONES[0:NODE, :], mask, start=True, stop=True).then_inc(counted, 1)
            with pe.Fori(1, CHUNKS) as c:
                shared(c)

            def turn_slots(s):
                pe.wait_ge(slot_in, 16 * (s + 1))
                for k in range(KD):
                    t = nc.tensor.transpose(slot_turn_psum[:, k, :], SLOTROW[:, k * 128:(k + 1) * 128],
                                            IDENT[:, :])
                t.then_inc(slot_turned, 1)

            turn_slots(0)

            def expert(e, q, i):
                first = pe.value_load(OFFI[0:1, ds(e, 1)], min_val=0, max_val=SLOT_TILES - 1)
                end = pe.value_load(OFFI[0:1, ds(e + 1, 1)], min_val=1, max_val=SLOT_TILES - 1)
                with pe.Fori(first, end) as s:
                    pe.wait_ge(expert_in[q], 32 * (i + 1))
                    pe.wait_ge(slot_feat, s + 1)
                    for f in range(NF):
                        if f >= 4:
                            pe.wait_ge(slot_gelu, NF * s + f - 3)
                        for k in range(KD):
                            t = nc.tensor.matmul(slot_hidden_psum[f], W1X[q][:, k, f * 128:(f + 1) * 128],
                                                 SLOTFEAT[:, k, :], start=k == 0, stop=k == KD - 1)
                        t.then_inc(slot_hidden, 1)
                    turn_slots(s + 1)
                    pe.wait_ge(slot_taken, s + 1)
                    for f in range(NF):
                        pe.wait_ge(slot_gelu, NF * s + f + 1)
                        t = nc.tensor.matmul(slot_ffn_psum, SLOTGELU[:, f, :], W2X[q][:, f, :],
                                             start=f == 0, stop=f == NF - 1)
                    t.then_inc(slot_ffn, 1)

            with pe.Fori(0, EXPERTS // 2) as i:
                expert(2 * i, 0, i)
                expert(2 * i + 1, 1, i)

        @block.vector
        def _(dve):
            chain = [0]

            def link(*instructions):
                for t in instructions:
                    t.then_inc(dve_chain, 1)
                chain[0] += len(instructions)
                dve.wait_ge(dve_chain, chain[0])

            v = nc.vector
            for one_ahead in (*added, out_ready, slot_taken, slot_row):
                dve.sem_inc(one_ahead, 1)
            dve.wait_ge(pool_const, 10)
            v.tensor_copy(FILL[:, D:D + 1], IOTAI[:, 180:181]).then_inc(const_ready, 1)
            link(v.tensor_copy(IOTA[:, :], IOTAI[:, 0:NODE]),
                 v.tensor_copy(NEG[:, :], IOTAI[:, 128:128 + TILES]),
                 v.tensor_copy(DOWN, IOTAI[0:NODE, 184:192]),
                 v.tensor_copy(LN[:, 3, :], IOTAI[0:NODE, 192:192 + TILES]))

            per = TILES // PIECES
            for i in range(PIECES):
                dve.wait_ge(x_in[i], 32)
                with dve.Fori(i * per, (i + 1) * per) as t:
                    v.bn_stats(LNSTAT[:, ds(t, 1), :], X[:, ds(t, 1), :]).then_inc(ln_stats, 1)

            def row_moments(ready):
                even, odd = LNSTAT[:, :, 1], LNSTAT[:, :, 4]
                link(v.tensor_tensor(LN[:, 0, :], even, odd, ALU.add),
                     v.tensor_tensor(LN[:, 1, :], even, odd, ALU.subtract),
                     v.tensor_tensor(MV[:, :, 1], LNSTAT[:, :, 2], LNSTAT[:, :, 5], ALU.add))
                link(v.scalar_tensor_tensor(out=LN[:, 2, :], in0=LN[:, 1, :], scalar=0.25, in1=LN[:, 1, :],
                                            op0=ALU.mult, op1=ALU.mult),
                     v.tensor_scalar(MV[:, :, 0], LN[:, 0, :], 0.5, None, ALU.mult))
                link(v.scalar_tensor_tensor(out=MV[:, :, 1], in0=MV[:, :, 1], scalar=1.0 / D, in1=LN[:, 2, :],
                                            op0=ALU.mult, op1=ALU.add))
                dve.sem_inc(ready, 1)

            dve.wait_ge(ln_stats, TILES)
            row_moments(moments_in)

            def layer_norm_scale(std, ready):
                dve.wait_ge(std, 1)
                link(v.reciprocal(LN[:, 1, :], LN[:, 0, :]))
                v.scalar_tensor_tensor(out=LN[:, 2, :], in0=MV[:, :, 0], scalar=-1.0, in1=LN[:, 1, :],
                                       op0=ALU.mult, op1=ALU.mult).then_inc(ready, 1)

            layer_norm_scale(ln_std, ln_ready)

            dve.wait_ge(edges_in, 32)
            link(v.tensor_copy(DST, DSTI))
            link(v.tensor_scalar(TILEOF, DST, 1.0 / NODE, 0.5 / NODE - 0.5, ALU.mult, ALU.add))
            link(v.tensor_scalar(TILEOF, TILEOF, ROUND, None, ALU.add))
            link(v.tensor_scalar(TILEOF, TILEOF, ROUND, None, ALU.subtract))
            by_group = TILEOF.rearrange("p (g k) -> p g k", k=GROUP)
            v.tensor_reduce(RANGES[:, 0, :], by_group, AX.X, ALU.max).then_inc(range_ready, 1)
            v.tensor_reduce(RANGES[:, 1, :], by_group, AX.X, ALU.min).then_inc(range_ready, 1)

            def count0(c, p):
                dve.wait_ge(turned0, c + 1)
                for k in range(KD):
                    v.bn_stats(BNSTAT[:, k, ds(c, 1), :], turn_psum[p][:, k, :].unsqueeze(1))\
                        .then_inc(bn0_counted, 1)

            chunks(dve, count0)
            dve.wait_ge(bn0_counted, KD * CHUNKS)

            def batch_norm(n, gamma, beta):
                for k in range(KD):
                    v.bn_aggr(BN[:, 0, k, :], BNSTAT[:, k, :, :].rearrange("p c s -> p (c s)"))\
                        .then_inc(dve_bn, 1)
                dve.wait_ge(bn_std, n + 1)
                link(v.reciprocal(BN[:, 1, :, 0], BN[:, 2, :, 0]))
                link(v.tensor_tensor(BN[:, 3, :, 0], BN[:, 1, :, 0], VEC[:, gamma, :], ALU.mult))
                link(v.tensor_tensor(BN[:, 4, :, 0], BN[:, 0, :, 0], BN[:, 3, :, 0], ALU.mult))
                v.tensor_tensor(BN[:, 5, :, 0], VEC[:, beta, :], BN[:, 4, :, 0], ALU.subtract)\
                    .then_inc(bn_ready, 1)
                dve.wait_ge(bn_ready, n + 1)

            dve.wait_ge(vec_in, 16)
            batch_norm(0, 0, 1)
            for i in range(2 * KD):
                v.tensor_scalar(DIAG[:, i, :], IDENT[:, :], BN[:, 3 if i < KD else 5, i % KD, 0:1], None,
                                ALU.mult).then_inc(diag_ready, 1)

            dve.wait_ge(range_turned, 1)
            turned_ranges = PS[0:GROUPS // 2, 5, :].rearrange("p (a q) -> p a q", a=4)
            v.tensor_reduce(EXTREMES[0:GROUPS // 2, 0:2], turned_ranges[:, 0:2, :], AX.X, ALU.max)\
                .then_inc(row_ready, 1)
            v.tensor_reduce(EXTREMES[0:GROUPS // 2, 2:4], turned_ranges[:, 2:4, :], AX.X, ALU.min)\
                .then_inc(row_ready, 1)
            dve.wait_ge(row_turned, 1)
            high, low, steps, ends, tile_less_step, firsts = [STEPS[:, i, :] for i in range(6)]
            link(v.tensor_scalar(high, PS[0:1, 6, 0:GROUPS], float(TILES - 1), None, ALU.min),
                 v.tensor_copy(low, PS[0:1, 6, GROUPS:2 * GROUPS]))
            link(v.scalar_tensor_tensor(out=steps, in0=high, scalar=1.0, in1=low, op0=ALU.add,
                                        op1=ALU.subtract))
            link(v.tensor_scalar(steps, steps, 1.0, None, ALU.max),
                 v.tensor_scalar(low, low, float(TILES - 1), None, ALU.min))
            link(v.tensor_tensor_scan(ends, ONES[0:1, 0:1].to_broadcast([1, GROUPS]), steps, 0.0, ALU.mult, ALU.add))
            link(v.tensor_tensor(firsts, ends, steps, ALU.subtract))
            link(v.tensor_tensor(tile_less_step, low, firsts, ALU.subtract))
            v.tensor_copy(TABLE[:, 0, :], firsts).then_inc(table_ready, 1)
            v.tensor_copy(TABLE[:, 1, :], ends).then_inc(table_ready, 1)
            v.tensor_copy(TABLE[:, 2, :], tile_less_step).then_inc(table_ready, 1)

            dve.wait_ge(spread_ready, 1)

            def h0(c, p):
                for i in range(2):
                    t = 2 * c + i
                    v.scalar_tensor_tensor(out=TMP[:, p, i, :].unsqueeze(1), in0=X[:, ds(t, 1), :], scalar=MV[:, ds(t, 1), 0],
                                           in1=SPREAD[0:NODE, 0:1, :], op0=ALU.subtract, op1=ALU.mult)\
                        .then_inc(centred, 1)
                dve.wait_ge(centred, 2 * c + 2)
                for i in range(2):
                    t = 2 * c + i
                    v.scalar_tensor_tensor(out=H[:, ds(t, 1), 0:D], in0=TMP[:, p, i, :].unsqueeze(1), scalar=LN[:, 1, ds(t, 1)],
                                           in1=SPREAD[0:NODE, 1:2, :], op0=ALU.mult, op1=ALU.add)\
                        .then_inc(h0_ready, 1)

            chunks(dve, h0)

            dve.wait_ge(table_ready, 3)
            dve.wait_ge(rows_in, 16)
            for layer in range(2):
                dve.wait_ge(stored[layer], 32 * CHUNKS)

                def neighbours(i, layer=layer):
                    for r in range(RING):
                        g = RING * i + r
                        first = dve.value_load(TABLE[0:1, 0, ds(g, 1)], min_val=0, max_val=GROUPS * TILES)
                        end = dve.value_load(TABLE[0:1, 1, ds(g, 1)], min_val=1, max_val=GROUPS * TILES)
                        shift = dve.value_load(TABLE[0:1, 2, ds(g, 1)], min_val=-GROUPS * TILES, max_val=TILES)
                        with dve.Fori(first, end) as s:
                            j = nc.s_assert_within(s + shift, 0, TILES - 1, skip_runtime_bounds_check_because=
                                                   "step + shift runs from a group's lowest to its highest node tile")
                            for k in range(GROUP):
                                dve.wait_ge(multiplied[layer], GROUP * s + k + 1)
                                v.tensor_scalar(ONEHOT[:, k, :], IOTA[:, :], DST[:, ds(GROUP * g + k, 1)],
                                                NEG[:, ds(j, 1)], ALU.subtract, ALU.is_equal)\
                                    .then_inc(onehot_ready[layer], 1)
                            dve.wait_ge(multiplied[layer], GROUP * s + 2 * GROUP)
                            dve.wait_ge(added[layer], s + 1)
                            v.tensor_tensor(H[:, ds(j, 1), 0:D], H[:, ds(j, 1), 0:D],
                                            PS[0:NODE, 7, 0:D].unsqueeze(1), ALU.add).then_inc(added[layer], 1)
                        dve.sem_inc(group_used, 1)

                with dve.Fori(0, ROUNDS) as i:
                    neighbours(i)
                total = dve.value_load(TABLE[0:1, 1, GROUPS - 1:GROUPS], min_val=1, max_val=GROUPS * TILES)
                dve.wait_ge(added[layer], total + 1)
                dve.sem_inc(agg_done, 1)

                base = layer * CHUNKS

                def keep_feat(c, p, base=base):
                    dve.wait_ge(turned, c + base + 1)
                    v.tensor_copy(feat[:, :, ds(CH * c, CH)], turn_psum[p]).then_inc(feat_ready, 1)

                def count(c, p, base=base):
                    if not last(c):
                        keep_feat(c + 1, 1 - p)
                    dve.wait_ge(z_kept, KD * (c + base + 1))
                    for k in range(KD):
                        v.bn_stats(BNSTAT[:, k, ds(c, 1), :], feat[:, k, ds(CH * c, CH)].unsqueeze(1))\
                            .then_inc(bn_counted, 1)

                keep_feat(0, 0)
                chunks(dve, count)
                dve.wait_ge(bn_counted, KD * CHUNKS * (layer + 1))
                batch_norm(layer + 1, 3 + 3 * layer, 4 + 3 * layer)

                def take_y(c, p, base=base, layer=layer):
                    dve.wait_ge(y_ready, c + base + 1)
                    if layer == 0:
                        wait_count(dve, h1_ready, c - 1)
                    v.tensor_tensor(TMP[:, p, :, :], y_psum[p],
                                    ROWS[:, layer:layer + 1, :].to_broadcast([NODE, 2, D]), ALU.add)\
                        .then_inc(y_taken, 1)
                    if layer == 1:
                        dve.wait_ge(y_taken, c + base + 1)
                        v.scalar_tensor_tensor(out=X[:, ds(2 * c, 2), :], in0=TMP[:, p, :, :], scalar=0.0,
                                               in1=X[:, ds(2 * c, 2), :], op0=ALU.max, op1=ALU.add)\
                            .then_inc(x2_ready, 1)
                        dve.wait_ge(x2_ready, c + 1)
                        for i in range(2):
                            t = 2 * c + i
                            v.bn_stats(LNSTAT[:, ds(t, 1), :], X[:, ds(t, 1), :]).then_inc(x2_stats, 1)

                chunks(dve, take_y)

            dve.wait_ge(x2_stats, TILES)
            row_moments(moments_mid)
            layer_norm_scale(ln2_std, ln2_ready)
            dve.wait_ge(ln2_ready, 1)

            def route_in(c, p):
                for i in range(2):
                    t = 2 * c + i
                    v.tensor_scalar(H[:, ds(t, 1), 0:D], X[:, ds(t, 1), :], MV[:, ds(t, 1), 0], LN[:, 1, ds(t, 1)],
                                    ALU.subtract, ALU.mult).then_inc(row_norm, 1)
                dve.wait_ge(feat2, c + 1)
                wait_count(dve, logit_done, c - 1)
                v.tensor_copy(RT[p], feat[:, :, ds(CH * c, CH)]).then_inc(half2, 1)
                dve.wait_ge(logit_done, c + 1)
                v.tensor_copy(LOGIT[:, ds(2 * c, 2), :], logit_psum[p]).then_inc(logit_kept, 1)

            chunks(dve, route_in)
            dve.wait_ge(logit_kept, CHUNKS)
            dve.wait_ge(row_norm, TILES)

            def over_experts(s):
                return s.unsqueeze(2).to_broadcast([NODE, TILES, EXPERTS])

            down = DOWN.unsqueeze(1).to_broadcast([NODE, TILES, EXPERTS])
            link(v.tensor_reduce(S0, LOGIT, AX.X, ALU.max))
            v.tensor_tensor(LOGIT, LOGIT, over_experts(S0), ALU.subtract).then_inc(logit_max, 1)
            dve.wait_ge(exp_ready, 1)
            link(v.tensor_reduce(S1, LOGIT, AX.X, ALU.add))
            link(v.reciprocal(S2, S1))
            link(v.tensor_tensor(LOGIT, LOGIT, over_experts(S2), ALU.mult))
            link(v.tensor_reduce(S0, LOGIT, AX.X, ALU.max))
            link(v.tensor_tensor(TOP1, LOGIT, over_experts(S0), ALU.is_equal))
            link(v.tensor_tensor(CAND, TOP1, down, ALU.mult))
            link(v.tensor_reduce(S1, CAND, AX.X, ALU.max))
            link(v.tensor_tensor(TOP1, down, over_experts(S1), ALU.is_equal))
            link(v.scalar_tensor_tensor(out=CAND, in0=TOP1, scalar=-4.0, in1=LOGIT, op0=ALU.mult, op1=ALU.add))
            link(v.tensor_reduce(S1, CAND, AX.X, ALU.max))
            link(v.tensor_tensor(TOP2, CAND, over_experts(S1), ALU.is_equal))
            link(v.tensor_tensor(CAND, TOP2, down, ALU.mult))
            link(v.tensor_reduce(S2, CAND, AX.X, ALU.max))
            link(v.tensor_tensor(TOP2, down, over_experts(S2), ALU.is_equal))
            link(v.tensor_tensor(CUM, TOP1, TOP2, ALU.add))
            dve.sem_inc(mask_ready, 1)
            link(v.tensor_tensor(S2, S0, S1, ALU.add))
            link(v.reciprocal(S3, S2))
            link(v.tensor_tensor(S0, S0, S3, ALU.mult), v.tensor_tensor(S1, S1, S3, ALU.mult))
            link(v.tensor_tensor(LOGIT, TOP1, over_experts(S0), ALU.mult),
                 v.tensor_tensor(CAND, TOP2, over_experts(S1), ALU.mult))
            link(v.tensor_tensor(H[:, :, D + 1:ROW], LOGIT, CAND, ALU.add),
                 v.tensor_copy(H[:, :, D:D + 1], LN[:, 3, :].unsqueeze(2)))
            dve.wait_ge(counted, 1)
            before = PS[0:NODE, 6, 0:TE].rearrange("p (t e) -> p t e", t=TILES)
            of_tile = PS[0:NODE, 7, 0:TE].rearrange("p (t e) -> p t e", t=TILES)
            link(*[v.tensor_tensor_scan(CUM2[:, :, e], ONES[0:NODE, 0:TILES], of_tile[:, :, e], 0.0,
                                        ALU.mult, ALU.add) for e in range(EXPERTS)])
            link(v.tensor_tensor(POS, CUM2, of_tile, ALU.subtract))
            link(v.tensor_tensor(POS, POS, before, ALU.add))
            tiles_of, ends_of, starts_of = [OFFF[0:NODE, i, :] for i in range(3)]
            link(v.tensor_scalar(tiles_of, CUM2[:, TILES - 1, :], 1.0 / 128, 127.0 / 256, ALU.mult, ALU.add))
            link(v.tensor_scalar(tiles_of, tiles_of, ROUND, None, ALU.add))
            link(v.tensor_scalar(tiles_of, tiles_of, ROUND, None, ALU.subtract))
            link(v.tensor_scalar(tiles_of, tiles_of, 1.0, None, ALU.max))
            link(v.tensor_tensor_scan(ends_of, ONES[0:NODE, 0:EXPERTS], tiles_of, 0.0, ALU.mult, ALU.add))
            link(v.tensor_tensor(starts_of, ends_of, tiles_of, ALU.subtract))
            link(v.tensor_copy(OFFI[:, 0:EXPERTS], starts_of[0:1, :]),
                 v.tensor_copy(OFFI[:, EXPERTS:EXPERTS + 1], ends_of[0:1, EXPERTS - 1:EXPERTS]))
            dve.sem_inc(off_ready, 1)
            link(v.scalar_tensor_tensor(out=POS, in0=starts_of.unsqueeze(1).to_broadcast([NODE, TILES, EXPERTS]),
                                        scalar=128.0, in1=POS, op0=ALU.mult, op1=ALU.add))
            link(v.tensor_tensor(CAND, TOP1, POS, ALU.mult), v.tensor_tensor(CUM2, TOP2, POS, ALU.mult))
            link(v.tensor_reduce(S0, CAND, AX.X, ALU.add), v.tensor_reduce(S1, CUM2, AX.X, ALU.add))
            link(v.tensor_copy(POSI[:, 0, :], S0), v.tensor_copy(POSI[:, 1, :], S1))
            dve.sem_inc(pos_ready, 1)

            with dve.Fori(0, CHUNKS) as c:
                dve.wait_ge(ffn_done, c + 1)
                dve.wait_ge(out_ready, c + 1)
                v.tensor_tensor(TMP[:, 0, :, :], ffn_psum, ROWS[:, 2:3, :].to_broadcast([NODE, 2, D]), ALU.add)\
                    .then_inc(ffn_taken, 1)
                dve.wait_ge(ffn_taken, c + 1)
                v.tensor_tensor(X[:, ds(2 * c, 2), :], X[:, ds(2 * c, 2), :], TMP[:, 0, :, :], ALU.add)\
                    .then_inc(out_ready, 1)

            def take_slots(s):
                dve.wait_ge(slot_turned, s + 1)
                v.tensor_copy(SLOTFEAT, slot_turn_psum).then_inc(slot_feat, 1)

            def keep_meta(s):
                v.tensor_copy(META[:, ds(s, 1), :], SLOTROW[:, D:ROW].unsqueeze(1)).then_inc(slot_meta, 1)

            take_slots(0)
            keep_meta(0)
            dve.wait_ge(b2_in, 16)
            with dve.Fori(0, EXPERTS) as e:
                first = dve.value_load(OFFI[0:1, ds(e, 1)], min_val=0, max_val=SLOT_TILES - 1)
                end = dve.value_load(OFFI[0:1, ds(e + 1, 1)], min_val=1, max_val=SLOT_TILES - 1)
                with dve.Fori(first, end) as s:
                    take_slots(s + 1)
                    keep_meta(s + 1)
                    dve.wait_ge(slot_ffn, s + 2)
                    dve.wait_ge(slot_row, 2 * s + 1)
                    v.tensor_tensor(SLOTSUM.unsqueeze(1), slot_ffn_psum.unsqueeze(1), B2X[:, ds(e, 1), :], ALU.add)\
                        .then_inc(slot_taken, 1)
                    dve.wait_ge(slot_taken, s + 2)
                    dve.wait_ge(slot_free, s + 1)
                    v.tensor_scalar(SLOTOUT.unsqueeze(1), SLOTSUM.unsqueeze(1), META[:, ds(s, 1), ds(e + 1, 1)], None, ALU.mult)\
                        .then_inc(slot_row, 1)
                    v.tensor_copy(TOKEN[:, 0:1].unsqueeze(1), META[:, ds(s, 1), 0:1]).then_inc(slot_row, 1)


def kernel(x, src, dst, L0_gnn_g0, L0_gnn_b0, L0_gnn_W1a, L0_gnn_b1a, L0_gnn_g1, L0_gnn_bt1, L0_gnn_W1b,
           L0_gnn_b1b, L0_gnn_W2a, L0_gnn_b2a, L0_gnn_g2, L0_gnn_bt2, L0_gnn_W2b, L0_gnn_b2b, L0_ffn_Wr,
           L0_ffn_W1s, L0_ffn_b1s, L0_ffn_W2s, L0_ffn_b2s, L0_ffn_W1p, L0_ffn_b1p, L0_ffn_W2p, L0_ffn_b2p):
    import numpy as np
    import concourse.bacc as bacc
    from concourse import mybir
    from concourse.bass_utils import run_bass_kernel_spmd

    def by_tile(a, fill):
        a = np.pad(np.asarray(a), (0, EDGE_TILES * 128 - E), constant_values=fill)
        return np.ascontiguousarray(a.reshape(EDGE_TILES, 128).T)

    def columns(*vectors):
        a = np.stack([np.asarray(v) for v in vectors])
        return np.ascontiguousarray(a.reshape(len(vectors), -1, 128).transpose(2, 0, 1))

    arrays = {
        "x": np.asarray(x), "src": by_tile(src, 0), "dst": by_tile(dst, FAR),
        "vecs": columns(L0_gnn_g0, L0_gnn_b0, L0_gnn_b1a, L0_gnn_g1, L0_gnn_bt1, L0_gnn_b2a, L0_gnn_g2,
                        L0_gnn_bt2),
        "w1a": np.asarray(L0_gnn_W1a), "w1b": np.asarray(L0_gnn_W1b),
        "w2a": np.asarray(L0_gnn_W2a), "w2b": np.asarray(L0_gnn_W2b),
        "rows": np.stack([np.asarray(v) for v in (L0_gnn_b1b, L0_gnn_b2b, L0_ffn_b2s)]),
        "wr": np.asarray(L0_ffn_Wr), "w1s": np.asarray(L0_ffn_W1s), "w2s": np.asarray(L0_ffn_W2s),
        "b1": columns(L0_ffn_b1s, *np.asarray(L0_ffn_b1p)),
        "w1p": np.asarray(L0_ffn_W1p), "w2p": np.asarray(L0_ffn_W2p), "b2p": np.asarray(L0_ffn_b2p),
    }
    nc = bacc.Bacc("TRN2", target_bir_lowering=False, num_devices=1)
    args = {n: nc.dram_tensor(f"in_{n}", a.shape, mybir.dt.from_np(a.dtype), kind="ExternalInput").ap()
            for n, a in arrays.items()}
    out = nc.dram_tensor("out", (N + 128, D), mybir.dt.float32, kind="ExternalOutput").ap()
    build(nc, out=out, **args)
    result = run_bass_kernel_spmd(nc, [{f"in_{n}": a for n, a in arrays.items()}], core_ids=[0])
    return result.results[0]["out"][0:N]
```

```python
N, D, E = 6250, 256, 106250
NODE = 125
TILES = N // NODE
KD = D // 128
CH = 2 * NODE
CHUNKS = N // CH
PIECES = 5
GROUP = 8
RING = 4
EDGE_TILES = -(-E // (128 * GROUP * RING)) * GROUP * RING
GROUPS = EDGE_TILES // GROUP
ROUNDS = GROUPS // RING
HALF = GROUP // 2
F, NF, EXPERTS, TOPK = 1024, 1024 // 128, 8, 2
ROW = D + 1 + EXPERTS
SLOT_TILES = (TOPK * N + EXPERTS * 127) // 128 + 1
EPS = 1e-5
ROUND = 12582912.0
FAR = 1 << 20
VECS = 8


def build(nc, x, src, dst, vecs, w1a, w1b, w2a, w2b, rows, wr, w1s, w2s, b1, w1p, w2p, b2p, out):
    from contextlib import ExitStack

    import concourse.bass as bass
    from concourse import mybir

    F32, I32 = mybir.dt.float32, mybir.dt.int32
    ACT, ALU, AX = mybir.ActivationFunctionType, mybir.AluOpType, mybir.AxisListType
    ds = bass.ds

    with ExitStack() as ctx:
        def sb(name, shape, dt=F32):
            return ctx.enter_context(nc.sbuf_tensor(name, shape, dt))

        def sem(name):
            return ctx.enter_context(nc.semaphore(name))

        tables = [nc.dram_tensor(f"table{l}", (N, D), F32).ap() for l in range(2)]
        slots = nc.dram_tensor("slots", (SLOT_TILES * 128, ROW), F32).ap()

        XA = sb("X", [128, TILES, D])
        X = XA[0:NODE]
        HA = sb("H", [128, TILES, ROW])
        H = HA[0:NODE]
        FT = sb("FT", [128, KD * N])
        feat = FT[:, :].rearrange("p (k n) -> p k n", k=KD)
        E_ = sb("edge_arena", [128, KD * F + NF * D + NF * CH])
        G_ = sb("gnn_arena", [128, 4 * KD * D + 2 * KD * CH])

        def cut(arena, at, shape):
            size = 1
            for s in shape:
                size *= s
            v = arena[:, at:at + size]
            names = "abcd"[:len(shape)]
            if len(shape) > 1:
                v = v.rearrange(f"p ({' '.join(names)}) -> p {' '.join(names)}",
                                **{n: s for n, s in zip(names, shape)})
            return v

        SRC = cut(E_, 0, [EDGE_TILES]).bitcast(I32)
        DST = cut(E_, EDGE_TILES, [EDGE_TILES])
        ONEHOT = [cut(E_, 2 * EDGE_TILES + i * HALF * NODE, [HALF, NODE]) for i in range(2)]
        SPREAD = cut(E_, 2 * EDGE_TILES, [2, D])
        W1S = cut(E_, 0, [KD, F])
        W2S = cut(E_, KD * F, [NF, D])
        GELU = cut(E_, KD * F + NF * D, [NF, CH])
        W = [[cut(G_, (2 * l + i) * KD * D, [KD, D]) for i in range(2)] for l in range(2)]
        RT = [cut(G_, 4 * KD * D + p * KD * CH, [KD, CH]) for p in range(2)]
        TE = TILES * EXPERTS
        LOGIT, TOP1, TOP2, CAND, POS, CUM, CUM2 = [
            cut(G_, i * TE, [TILES, EXPERTS])[0:NODE] for i in range(7)]
        HX = HA[:, :, :].rearrange("p t r -> p (t r)")
        DSTI = cut(HX, 0, [EDGE_TILES]).bitcast(I32)
        TILEOF = cut(HX, EDGE_TILES, [EDGE_TILES])
        RANGES = cut(HX, 2 * EDGE_TILES, [2, GROUPS])
        AT = 2 * EDGE_TILES + 2 * GROUPS
        EXTREMES = cut(HX, AT, [4])
        STEPS = cut(HX, AT + 4, [6, GROUPS])[0:1]
        DIAG = cut(HX, AT + 4 + 6 * GROUPS, [2 * KD, 128])
        IOTAI = cut(HX, AT + 4 + 6 * GROUPS + 512, [256]).bitcast(I32)
        GATHERED = cut(HX, 0, [RING, GROUP, D])
        at, hx = 0, {}
        for name, shape in (("w1_0", [KD, F]), ("w1_1", [KD, F]), ("w2_0", [NF, D]), ("w2_1", [NF, D]),
                            ("b2", [EXPERTS, D]), ("meta", [SLOT_TILES, 1 + EXPERTS]), ("row", [ROW]),
                            ("feat", [KD, 128]), ("gelu", [NF, 128]), ("out", [D])):
            hx[name] = cut(HX, at, shape)
            size = 1
            for n in shape:
                size *= n
            at += size
        assert at <= TILES * ROW
        W1X, W2X = [hx["w1_0"], hx["w1_1"]], [hx["w2_0"], hx["w2_1"]]
        B2X, META, SLOTROW, SLOTFEAT = hx["b2"], hx["meta"], hx["row"], hx["feat"]
        SLOTGELU, SLOTOUT = hx["gelu"], hx["out"]
        TABLE = sb("TABLE", [1, 3, GROUPS], I32)
        IDX = sb("IDX", [128, RING, GROUP], I32)
        STAGE = sb("STAGE", [128, 2, 2, D])
        TMP = sb("TMP", [NODE, 2, 2, D])
        ROWS = sb("ROWS", [NODE, 3, D])
        IDENT = sb("IDENT", [128, 128])
        ONES = sb("ONES", [128, 128])
        TRI = sb("TRI", [NODE, NODE])
        IOTA = sb("IOTA", [128, NODE])
        NEG = sb("NEG", [128, TILES])
        REL = sb("REL", [128, GROUP])
        MISC = sb("MISC", [128, 64])
        VEC = sb("VEC", [128, VECS, KD])
        B1 = sb("B1", [128, 1 + EXPERTS, NF])
        WR = sb("WR", [128, KD, EXPERTS])
        LNSTAT = sb("LNSTAT", [NODE, TILES, 6])
        LN = sb("LN", [NODE, 4, TILES])
        MV = sb("MV", [NODE, TILES, 2])
        BNSTAT = sb("BNSTAT", [128, KD, CHUNKS, 6])
        BN = sb("BN", [128, 6, KD, 2])
        FILL = cut(G_, 4 * KD * D, [ROW])
        POSI = sb("POSI", [NODE, TOPK, TILES], I32)
        OFFI = sb("OFFI", [1, 16], I32)
        EPST = MISC[:, 0:1]
        OFFF = MISC[:, 8:32].rearrange("p (a b) -> p a b", a=3)
        DOWN = MISC[0:NODE, 40:48]
        assert 7 * TE + 4 * TILES <= 4 * KD * D + 2 * KD * CH
        S0, S1, S2, S3 = [cut(G_, 7 * TE + i * TILES, [TILES])[0:NODE] for i in range(4)]
        POS32 = sb("POS32", [NODE, 2, TOPK], I32)
        TOKEN = sb("TOKEN", [128, 1], I32)
        SENDROW = [cut(STAGE[:, :, :, :].rearrange("p a b d -> p (a b d)"), p * 2 * D, [ROW])[0:NODE]
                   for p in range(2)]
        SLOTSUM = cut(STAGE[:, :, :, :].rearrange("p a b d -> p (a b d)"), 0, [D])

        PS = ctx.enter_context(nc.psum_tensor("PS", [128, 8, 512], F32))

        x_in = [sem(f"x_in{i}") for i in range(PIECES)]
        edges_in, vec_in, rows_in, gnnw_in, ffn_small_in = map(
            sem, ("edges_in", "vec_in", "rows_in", "gnnw_in", "ffn_small_in"))
        pool_const, const_ready, dve_chain = map(sem, ("pool_const", "const_ready", "dve_chain"))
        ln_stats, moments_in, ln_std, ln_ready = map(sem, ("ln_stats", "moments_in", "ln_std", "ln_ready"))
        staged0, turned0, feat0, bn0_counted = map(sem, ("staged0", "turned0", "feat0", "bn0_counted"))
        bn_std, bn_ready = map(sem, ("bn_std", "bn_ready"))
        dve_bn = sem("bn_moments")
        diag_ready, spread_done, spread_ready = map(sem, ("diag_ready", "spread_done", "spread_ready"))
        centred, h0_ready = map(sem, ("centred", "h0_ready"))
        range_ready, range_turned, row_ready, row_turned, table_ready = map(
            sem, ("range_ready", "range_turned", "row_ready", "row_turned", "table_ready"))
        stored = [sem(f"stored{l}") for l in range(2)]
        index_ready = sem("index_ready")
        gathered = [sem(f"gathered{r}") for r in range(RING)]
        group_used = sem("group_used")
        rel_ready = [sem(f"rel_ready{l}") for l in range(2)]
        onehot_ready = [sem(f"onehot_ready{l}") for l in range(2)]
        onehot_used = [sem(f"onehot_used{l}") for l in range(2)]
        summed = [sem(f"summed{l}") for l in range(2)]
        kept = [sem(f"kept{l}") for l in range(2)]
        h0_turned = sem("h0_turned")
        agg_done = sem("agg_done")
        staged, turned, h1_turned, z_ready, z_kept, bn_counted = map(
            sem, ("staged", "turned", "h1_turned", "z_ready", "z_kept", "bn_counted"))
        relu_ready, y_ready, y_taken, h1_ready, x2_ready, x2_stats = map(
            sem, ("relu_ready", "y_ready", "y_taken", "h1_ready", "x2_ready", "x2_stats"))
        moments_mid, ln2_std, ln2_ready, row_norm = map(sem, ("moments_mid", "ln2_std", "ln2_ready", "row_norm"))
        staged2, turned2, feat2, half2, logit_done, logit_kept = map(
            sem, ("staged2", "turned2", "feat2", "half2", "logit_done", "logit_kept"))
        logit_max, exp_ready, mask_ready, counted, pos_ready, off_ready = map(
            sem, ("logit_max", "exp_ready", "mask_ready", "counted", "pos_ready", "off_ready"))
        shared_in, hidden, gelu_done, ffn_done, ffn_taken, out_ready, out_stored, spare_zero = map(
            sem, ("shared_in", "hidden", "gelu_done", "ffn_done", "ffn_taken", "out_ready",
                  "out_stored", "spare_zero"))
        filled, row_copied = map(sem, ("filled", "row_copied"))
        scattered = [sem(f"scattered{p}") for p in range(2)]
        scatter_end = sem("scatter_end")
        wait_carrier = sem("wait_carrier")
        expert_in = [sem(f"expert_in{q}") for q in range(2)]
        b2_in, slot_in, slot_turned, slot_feat, slot_meta = map(
            sem, ("b2_in", "slot_in", "slot_turned", "slot_feat", "slot_meta"))
        slot_hidden, slot_gelu, slot_ffn, slot_taken, slot_row, slot_added = map(
            sem, ("slot_hidden", "slot_gelu", "slot_ffn", "slot_taken", "slot_row", "slot_added"))
        slot_free = sem("slot_free")

        def wait_count(eng, semaphore, value):
            if isinstance(value, int) and value <= 0:
                return
            eng.wait_ge(semaphore, value)

        def chunks(eng, body):
            body(0, 0)
            body(1, 1)
            with eng.Fori(1, CHUNKS // 2) as i:
                body(2 * i, 0)
                body(2 * i + 1, 1)
            body(CHUNKS - 1, 0)

        def last(c):
            return isinstance(c, int) and c == CHUNKS - 1

        PARTS = ((0, 112), (112, NODE))

        def by_tile(dram):
            return dram[0:N, :].rearrange("(t p) d -> p t d", p=NODE)

        turn_psum = [PS[:, p, 0:KD * CH].rearrange("q (k n) -> q k n", k=KD) for p in range(2)]
        z_psum = [PS[:, 2 + p, 0:KD * CH].rearrange("q (k n) -> q k n", k=KD) for p in range(2)]
        sum_psum = PS[:, 4:8, 0:NODE]
        y_psum = [PS[0:NODE, 4 + p, :].rearrange("q (i d) -> q i d", i=2) for p in range(2)]
        logit_psum = [PS[0:NODE, 6 + p, 0:2 * EXPERTS].rearrange("q (i e) -> q i e", i=2) for p in range(2)]
        hidden_psum = [PS[:, f % 4, 0:CH] for f in range(NF)]
        ffn_psum = PS[0:NODE, 4, :].rearrange("q (i d) -> q i d", i=2)
        slot_turn_psum = PS[:, 5, 0:KD * 128].rearrange("q (k n) -> q k n", k=KD)
        slot_hidden_psum = [PS[:, f % 4, 0:128] for f in range(NF)]
        slot_ffn_psum = PS[:, 6, 0:D]


        block = ctx.enter_context(nc.Block())

        @block.sync
        def _(sp):
            for i in range(PIECES):
                t = slice(i * TILES // PIECES, (i + 1) * TILES // PIECES)
                for a, b in PARTS:
                    sp.dma_start(X[a:b, t, :], by_tile(x)[a:b, t, :]).then_inc(x_in[i], 16)

            def store_table(layer, source_ready, base):
                def store(c, p):
                    wait_count(sp, source_ready, base * (c + 1))
                    for a, b in PARTS:
                        sp.dma_start(by_tile(tables[layer])[a:b, ds(2 * c, 2), :],
                                     H[a:b, ds(2 * c, 2), 0:D]).then_inc(stored[layer], 16)
                return store

            chunks(sp, store_table(0, h0_ready, 2))
            chunks(sp, store_table(1, h1_ready, 1))

            sp.wait_ge(agg_done, 2)
            sp.dma_start(W1S, w1s.rearrange("(k p) f -> p k f", p=128)).then_inc(shared_in, 16)
            sp.dma_start(W2S, w2s.rearrange("(f p) d -> p f d", p=128)).then_inc(shared_in, 16)

            def store_out(c, p):
                sp.wait_ge(out_ready, c + 2)
                for a, b in PARTS:
                    sp.dma_start(by_tile(out)[a:b, ds(2 * c, 2), :],
                                 X[a:b, ds(2 * c, 2), :]).then_inc(out_stored, 16)

            def load_expert(e, q):
                sp.dma_start(W1X[q], w1p[ds(e, 1)].rearrange("o (k p) f -> p (o k) f", p=128))\
                    .then_inc(expert_in[q], 16)
                sp.dma_start(W2X[q], w2p[ds(e, 1)].rearrange("o (f p) d -> p (o f) d", p=128))\
                    .then_inc(expert_in[q], 16)

            def load_slots(s):
                sp.dma_start(SLOTROW, slots[ds(128 * s, 128), :]).then_inc(slot_in, 16)

            with sp.Fori(0, CHUNKS) as c:
                store_out(c, 0)
            sp.wait_ge(scatter_end, 1)
            sp.dma_start(B2X, b2p.partition_broadcast(128)).then_inc(b2_in, 16)
            load_expert(0, 0)
            load_slots(0)

            def expert(e, q):
                first = sp.value_load(OFFI[0:1, ds(e, 1)], min_val=0, max_val=SLOT_TILES - 1)
                end = sp.value_load(OFFI[0:1, ds(e + 1, 1)], min_val=1, max_val=SLOT_TILES - 1)
                if not (isinstance(e, int) and e == EXPERTS - 1):
                    sp.wait_ge(slot_ffn, first + 1)
                    load_expert(e + 1, 1 - q)
                with sp.Fori(first, end) as s:
                    sp.wait_ge(slot_turned, s + 1)
                    sp.wait_ge(slot_meta, s + 1)
                    load_slots(s + 1)

            with sp.Fori(0, EXPERTS // 2 - 1) as i:
                expert(2 * i, 0)
                expert(2 * i + 1, 1)
            expert(EXPERTS - 2, 0)
            expert(EXPERTS - 1, 1)

        @block.gpsimd
        def _(pool):
            nc.gpsimd.memset(IDENT[:, :], 0.0).then_inc(pool_const, 1)
            nc.gpsimd.memset(TRI[:, :], 1.0).then_inc(pool_const, 1)
            nc.gpsimd.memset(ONES[:, :], 1.0).then_inc(pool_const, 1)
            nc.gpsimd.memset(FILL[:, :], 0.0).then_inc(pool_const, 1)
            nc.gpsimd.memset(EPST, EPS).then_inc(pool_const, 1)
            nc.gpsimd.iota(IOTAI[:, 0:NODE], [[1, NODE]], base=0, channel_multiplier=0)\
                .then_inc(pool_const, 1)
            nc.gpsimd.iota(IOTAI[:, 128:128 + TILES], [[-NODE, TILES]], base=0, channel_multiplier=0)\
                .then_inc(pool_const, 1)
            nc.gpsimd.iota(IOTAI[:, 180:181], [[1, 1]], base=N, channel_multiplier=1)\
                .then_inc(pool_const, 1)
            nc.gpsimd.iota(IOTAI[:, 184:192], [[-1, EXPERTS]], base=EXPERTS, channel_multiplier=0)\
                .then_inc(pool_const, 1)
            nc.gpsimd.iota(IOTAI[:, 192:192 + TILES], [[NODE, TILES]], base=0, channel_multiplier=1)\
                .then_inc(pool_const, 1)
            pool.wait_ge(pool_const, 10)
            nc.gpsimd.affine_select(out=IDENT[:, :], in_=IDENT[:, :], compare_op=ALU.not_equal, fill=1.0,
                                    base=0, pattern=[[-1, 128]], channel_multiplier=1)\
                .then_inc(const_ready, 1)
            nc.gpsimd.affine_select(out=TRI[:, :], in_=TRI[:, :], compare_op=ALU.is_gt, fill=0.0,
                                    base=0, pattern=[[1, NODE]], channel_multiplier=-1)\
                .then_inc(const_ready, 1)

            for layer in range(2):
                pool.wait_ge(stored[layer], 32 * CHUNKS)

                def gather(i, layer=layer):
                    for r in range(RING):
                        g = RING * i + r + layer * GROUPS
                        wait_count(pool, group_used, g - RING + 1)
                        pool.wait_ge(index_ready, g + 1)
                        pool.sem_inc(wait_carrier, 1)
                        for k in range(GROUP):
                            nc.gpsimd.indirect_dma_start(
                                out=GATHERED[:, r, k, :], out_offset=None, in_=tables[layer],
                                in_offset=bass.IndirectOffsetOnAxis(ap=IDX[:, r, k:k + 1], axis=0))\
                                .then_inc(gathered[r], 16)

                gather(0)
                with pool.Fori(1, ROUNDS) as i:
                    gather(i)

            pool.wait_ge(pos_ready, 1)
            pool.wait_ge(filled, 32)

            def scatter(t, p):
                wait_count(pool, scattered[p], 32 * (t // 2) if isinstance(t, int) else 16 * (t - p))
                nc.gpsimd.tensor_copy(SENDROW[p].unsqueeze(1), H[:, ds(t, 1), :]).then_inc(row_copied, 1)
                nc.gpsimd.tensor_copy(POS32[:, p, :].unsqueeze(2), POSI[:, :, ds(t, 1)])\
                    .then_inc(row_copied, 1)
                pool.wait_ge(row_copied, 2 * t + 2)
                pool.sem_inc(wait_carrier, 1)
                for k in range(TOPK):
                    nc.gpsimd.indirect_dma_start(
                        out=slots, out_offset=bass.IndirectOffsetOnAxis(ap=POS32[:, p, k:k + 1], axis=0),
                        in_=SENDROW[p], in_offset=None).then_inc(scattered[p], 16)

            scatter(0, 0)
            scatter(1, 1)
            with pool.Fori(1, TILES // 2) as i:
                scatter(2 * i, 0)
                scatter(2 * i + 1, 1)
            for p in range(2):
                pool.wait_ge(scattered[p], 32 * TILES // 2)
            pool.sem_inc(scatter_end, 1)

            pool.wait_ge(out_stored, 32 * CHUNKS)
            pool.wait_ge(spare_zero, 16)
            pool.wait_ge(off_ready, 1)
            pool.sem_inc(slot_free, 1)
            total = pool.value_load(OFFI[0:1, EXPERTS:EXPERTS + 1], min_val=1, max_val=SLOT_TILES - 1)
            with pool.Fori(0, total) as s:
                pool.wait_ge(slot_row, 2 * s + 3)
                pool.sem_inc(wait_carrier, 1)
                nc.gpsimd.indirect_dma_start(
                    out=out, out_offset=bass.IndirectOffsetOnAxis(ap=TOKEN[:, 0:1], axis=0),
                    in_=SLOTOUT, in_offset=None, compute_op=ALU.add).then_inc(slot_added, 16)
                pool.wait_ge(slot_added, 16 * (s + 1))
                pool.sem_inc(slot_free, 1)

        @block.scalar
        def _(act):
            act.dma_start(SRC, src).then_inc(edges_in, 16)
            act.dma_start(DSTI, dst).then_inc(edges_in, 16)
            act.dma_start(VEC[:, :, :], vecs).then_inc(vec_in, 16)
            for i, w in enumerate((w1a, w1b, w2a, w2b)):
                act.dma_start(W[i // 2][i % 2], w.rearrange("(k p) o -> p k o", p=128)).then_inc(gnnw_in, 16)
            act.dma_start(ROWS[:, :, :], rows.partition_broadcast(NODE)).then_inc(rows_in, 16)
            act.dma_start(WR[:, :, :], wr.rearrange("(k p) e -> p k e", p=128)).then_inc(ffn_small_in, 16)
            act.dma_start(B1[:, :, :], b1).then_inc(ffn_small_in, 16)
            act.wait_ge(const_ready, 3)
            half = SLOT_TILES // 2
            for i in range(2):
                n = half if i == 0 else SLOT_TILES - half
                act.dma_start(slots[i * half * 128:(i * half + n) * 128, :].rearrange("(s p) r -> p s r", p=128),
                              FILL[:, :].unsqueeze(1).to_broadcast([128, n, ROW])).then_inc(filled, 16)
            act.dma_start(out[N:N + 128, :], FILL[:, 0:D]).then_inc(spare_zero, 16)

            act.wait_ge(moments_in, 1)
            nc.scalar.activation(LN[:, 0, :], MV[:, :, 1], ACT.Sqrt, bias=EPST[0:NODE]).then_inc(ln_std, 1)
            act.wait_ge(ln_ready, 1)

            def normalise(c, p, turned_count, done):
                wait_count(act, turned_count, c - 1)
                for i in range(2):
                    t = 2 * c + i
                    nc.scalar.activation(STAGE[0:NODE, p, i, :].unsqueeze(1), X[:, ds(t, 1), :], ACT.Identity,
                                         scale=LN[:, 1, ds(t, 1)], bias=LN[:, 2, ds(t, 1)]).then_inc(done, 1)

            chunks(act, lambda c, p: normalise(c, p, turned0, staged0))

            def bn_sqrt(n):
                act.wait_ge(dve_bn, 2 * n + 2)
                nc.scalar.activation(BN[:, 2, :, 0], BN[:, 0, :, 1], ACT.Sqrt, bias=EPST).then_inc(bn_std, 1)

            bn_sqrt(0)
            act.wait_ge(bn_ready, 1)
            for k in range(KD):
                for i in range(PIECES):
                    part = feat[:, k, i * (N // PIECES):(i + 1) * (N // PIECES)]
                    nc.scalar.activation(part, part, ACT.Identity, scale=BN[:, 3, k, 0:1],
                                         bias=BN[:, 5, k, 0:1]).then_inc(h0_turned, 1)
            act.wait_ge(spread_done, 1)
            nc.scalar.copy(SPREAD[0:NODE, :, :], PS[0:NODE, 4, :].rearrange("p (a d) -> p a d", a=2))\
                .then_inc(spread_ready, 1)

            for layer in range(2):
                if layer == 0:
                    act.wait_ge(edges_in, 32)
                    act.wait_ge(table_ready, 3)

                def keep_sums(i, layer=layer):
                    for r in range(RING):
                        g = RING * i + r
                        first = act.value_load(TABLE[0:1, 0, ds(g, 1)], min_val=0, max_val=GROUPS * TILES)
                        end = act.value_load(TABLE[0:1, 1, ds(g, 1)], min_val=1, max_val=GROUPS * TILES)
                        shift = act.value_load(TABLE[0:1, 2, ds(g, 1)], min_val=-GROUPS * TILES, max_val=TILES)
                        with act.Fori(first, end) as s:
                            j = nc.s_assert_within(s + shift, 0, TILES - 1, skip_runtime_bounds_check_because=
                                                   "step + shift runs from a group's lowest to its highest node tile")
                            act.wait_ge(summed[layer], s + 1)
                            nc.scalar.copy(feat[:, :, ds(NODE * j, NODE)], sum_psum[:, ds(2 * (s % 2), 2), :])\
                                .then_inc(kept[layer], 1)
                        act.sem_inc(group_used, 1)
                        if not (isinstance(i, int) and i == ROUNDS - 1):
                            act.wait_ge(gathered[r], 16 * GROUP * (i + 1 + layer * ROUNDS))
                            nc.scalar.copy(IDX[:, r, :], SRC[:, ds(GROUP * (g + RING), GROUP)])\
                                .then_inc(index_ready, 1)

                if layer == 1:
                    for r in range(RING):
                        act.wait_ge(gathered[r], 16 * GROUP * ROUNDS)
                for r in range(RING):
                    nc.scalar.copy(IDX[:, r, :], SRC[:, GROUP * r:GROUP * (r + 1)]).then_inc(index_ready, 1)
                with act.Fori(0, ROUNDS - 1) as i:
                    keep_sums(i)
                keep_sums(ROUNDS - 1)
                total = act.value_load(TABLE[0:1, 1, GROUPS - 1:GROUPS], min_val=1, max_val=GROUPS * TILES)
                act.wait_ge(kept[layer], total + 2)
                act.sem_inc(agg_done, 1)

                base = layer * CHUNKS

                def keep_z(c, p, base=base, layer=layer):
                    act.wait_ge(z_ready, c + base + 1)
                    for o in range(KD):
                        nc.scalar.activation(feat[:, o, ds(CH * c, CH)], z_psum[p][:, o, :], ACT.Identity,
                                             bias=VEC[:, 2 + 3 * layer, o:o + 1]).then_inc(z_kept, 1)

                act.wait_ge(vec_in, 16)
                chunks(act, keep_z)
                bn_sqrt(layer + 1)
                act.wait_ge(bn_ready, layer + 2)
                if layer == 0:
                    act.wait_ge(filled, 32)
                    act.wait_ge(spare_zero, 16)

                def relu_norm(c, p, base=base):
                    wait_count(act, y_ready, c + base - 1)
                    for k in range(KD):
                        nc.scalar.activation(RT[p][:, k, :], feat[:, k, ds(CH * c, CH)], ACT.Relu,
                                             scale=BN[:, 3, k, 0:1], bias=BN[:, 5, k, 0:1]).then_inc(relu_ready, 1)

                def keep_h1(c, p):
                    if not last(c):
                        relu_norm(c + 1, 1 - p)
                    act.wait_ge(y_taken, c + 1)
                    wait_count(act, turned, c - 1)
                    nc.scalar.activation(STAGE[0:NODE, p, :, :], TMP[:, p, :, :], ACT.Relu).then_inc(staged, 1)
                    nc.scalar.activation(H[:, ds(2 * c, 2), 0:D], TMP[:, p, :, :], ACT.Relu).then_inc(h1_ready, 1)

                if layer == 0:
                    relu_norm(0, 0)
                    chunks(act, keep_h1)
                else:
                    chunks(act, relu_norm)

            act.wait_ge(moments_mid, 1)
            nc.scalar.activation(LN[:, 0, :], MV[:, :, 1], ACT.Sqrt, bias=EPST[0:NODE]).then_inc(ln2_std, 1)
            act.wait_ge(ln2_ready, 1)

            def turn_rows(c, p):
                if not last(c):
                    normalise(c + 1, 1 - p, turned2, staged2)
                act.wait_ge(turned2, c + 1)
                nc.scalar.copy(feat[:, :, ds(CH * c, CH)], turn_psum[p]).then_inc(feat2, 1)

            normalise(0, 0, turned2, staged2)
            chunks(act, turn_rows)
            act.wait_ge(logit_max, 1)
            nc.scalar.activation(LOGIT, LOGIT, ACT.Exp).then_inc(exp_ready, 1)

            act.wait_ge(ffn_small_in, 32)
            with act.Fori(0, CHUNKS) as c:
                for f in range(NF):
                    act.wait_ge(hidden, NF * c + f + 1)
                    nc.scalar.activation(GELU[:, f, :], hidden_psum[f], ACT.Gelu, bias=B1[:, 0, f:f + 1])\
                        .then_inc(gelu_done, 1)

            def expert(e):
                first = act.value_load(OFFI[0:1, ds(e, 1)], min_val=0, max_val=SLOT_TILES - 1)
                end = act.value_load(OFFI[0:1, ds(e + 1, 1)], min_val=1, max_val=SLOT_TILES - 1)
                with act.Fori(first, end) as s:
                    for f in range(NF):
                        act.wait_ge(slot_hidden, NF * s + f + 1)
                        nc.scalar.activation(SLOTGELU[:, f, :], slot_hidden_psum[f], ACT.Gelu,
                                             bias=B1[:, ds(e + 1, 1), f]).then_inc(slot_gelu, 1)

            act.wait_ge(off_ready, 1)
            with act.Fori(0, EXPERTS) as e:
                expert(e)

        @block.tensor
        def _(pe):
            for l in range(2):
                pe.sem_inc(onehot_used[l], 2)
            pe.sem_inc(slot_ffn, 1)
            pe.wait_ge(const_ready, 2)

            def turn(c, p, ready, turned_count, taken, per, base=0):
                pe.wait_ge(ready, per * (c + base + 1))
                wait_count(pe, taken[0], taken[1] * (c + base - 1))
                for i in range(2):
                    for k in range(KD):
                        t = nc.tensor.transpose(turn_psum[p][:, k, i * NODE:(i + 1) * NODE],
                                                STAGE[0:NODE, p, i, k * 128:(k + 1) * 128],
                                                IDENT[0:NODE, 0:NODE])
                t.then_inc(turned_count, 1)

            chunks(pe, lambda c, p: turn(c, p, staged0, turned0, (feat0, 1), 2))

            pe.wait_ge(range_ready, 2)
            for i in range(2):
                t = nc.tensor.transpose(PS[0:GROUPS, 5, i * 128:(i + 1) * 128], RANGES[:, i, :], IDENT[:, :])
            t.then_inc(range_turned, 1)
            pe.wait_ge(row_ready, 2)
            for i in range(2):
                t = nc.tensor.transpose(PS[0:1, 6, i * GROUPS:(i + 1) * GROUPS], EXTREMES[0:GROUPS, i:i + 1],
                                        IDENT[0:GROUPS, 0:GROUPS])
            t.then_inc(row_turned, 1)

            pe.wait_ge(diag_ready, 2 * KD)
            for i in range(2 * KD):
                t = nc.tensor.matmul(PS[0:NODE, 4, i * 128:(i + 1) * 128], ONES[:, 0:NODE], DIAG[:, i, :],
                                     start=True, stop=True)
            t.then_inc(spread_done, 1)

            pe.wait_ge(table_ready, 3)
            pe.wait_ge(gnnw_in, 16 * 4)
            for layer in range(2):
                def multiply(i, layer=layer):
                    for r in range(RING):
                        g = RING * i + r
                        first = pe.value_load(TABLE[0:1, 0, ds(g, 1)], min_val=0, max_val=GROUPS * TILES)
                        end = pe.value_load(TABLE[0:1, 1, ds(g, 1)], min_val=1, max_val=GROUPS * TILES)
                        shift = pe.value_load(TABLE[0:1, 2, ds(g, 1)], min_val=-GROUPS * TILES, max_val=TILES)
                        with pe.Fori(first, end) as s:
                            j = nc.s_assert_within(s + shift, 0, TILES - 1, skip_runtime_bounds_check_because=
                                                   "step + shift runs from a group's lowest to its highest node tile")
                            bank = 2 * (s % 2)
                            pe.wait_ge(gathered[r], 16 * GROUP * (i + 1 + layer * ROUNDS))
                            pe.wait_ge(kept[layer], s + 1)
                            for half in range(2):
                                pe.wait_ge(onehot_ready[layer], 2 * s + half + 2)
                                for m in range(HALF):
                                    for k in range(KD):
                                        t = nc.tensor.matmul(
                                            sum_psum[:, ds(bank + k, 1), :],
                                            GATHERED[:, r, half * HALF + m, k * 128:(k + 1) * 128],
                                            ONEHOT[half][:, m, :].unsqueeze(1),
                                            start=half == 0 and m == 0, stop=False)
                                t.then_inc(onehot_used[layer], 1)
                            pe.wait_ge(kept[layer], s + 2)
                            for k in range(KD):
                                t = nc.tensor.matmul(sum_psum[:, ds(bank + k, 1), :], IDENT[:, :],
                                                     feat[:, k:k + 1, ds(NODE * j, NODE)], start=False, stop=True)
                            t.then_inc(summed[layer], 1)

                if layer == 0:
                    pe.wait_ge(h0_turned, KD * PIECES)
                else:
                    pe.wait_ge(h1_turned, CHUNKS)
                with pe.Fori(0, ROUNDS) as i:
                    multiply(i)

                base = layer * CHUNKS
                pe.wait_ge(agg_done, layer + 1)

                def first_product(c, p, base=base, layer=layer):
                    wait_count(pe, z_kept, KD * (c + base - 1))
                    for o in range(KD):
                        for k in range(KD):
                            t = nc.tensor.matmul(z_psum[p][:, o, :], W[layer][0][:, k, o * 128:(o + 1) * 128],
                                                 feat[:, k, ds(CH * c, CH)], start=k == 0, stop=k == KD - 1)
                    t.then_inc(z_ready, 1)

                chunks(pe, first_product)

                def second_product(c, p, base=base, layer=layer):
                    pe.wait_ge(relu_ready, KD * (c + base + 1))
                    wait_count(pe, y_taken, c + base - 1)
                    for i in range(2):
                        for k in range(KD):
                            t = nc.tensor.matmul(y_psum[p][:, i, :], RT[p][:, k, i * NODE:(i + 1) * NODE],
                                                 W[layer][1][:, k, :], start=k == 0, stop=k == KD - 1)
                    t.then_inc(y_ready, 1)
                    if layer == 0 and not (isinstance(c, int) and c == 0):
                        turn(c - 1, 1 - p, staged, turned, (h1_turned, 1), 1)

                chunks(pe, second_product)
                if layer == 0:
                    turn(CHUNKS - 1, 0, staged, turned, (h1_turned, 1), 1)

            pe.wait_ge(ffn_small_in, 32)

            def router(c, p):
                if not last(c):
                    turn2(c + 1, 1 - p)
                pe.wait_ge(half2, c + 1)
                wait_count(pe, logit_kept, c - 1)
                for i in range(2):
                    for k in range(KD):
                        t = nc.tensor.matmul(logit_psum[p][:, i, :], RT[p][:, k, i * NODE:(i + 1) * NODE],
                                             WR[:, k, :], start=k == 0, stop=k == KD - 1)
                t.then_inc(logit_done, 1)

            def turn2(c, p):
                wait_count(pe, feat2, c - 1)
                turn(c, p, staged2, turned2, (half2, 1), 2)

            turn2(0, 0)
            chunks(pe, router)

            def shared(c):
                pe.wait_ge(feat2, CHUNKS)
                for f in range(NF):
                    if f >= 4:
                        pe.wait_ge(gelu_done, NF * c + f - 3)
                    for k in range(KD):
                        t = nc.tensor.matmul(hidden_psum[f], W1S[:, k, f * 128:(f + 1) * 128],
                                             feat[:, k, ds(CH * c, CH)], start=k == 0, stop=k == KD - 1)
                    t.then_inc(hidden, 1)
                wait_count(pe, ffn_taken, c)
                for i in range(2):
                    for f in range(NF):
                        if i == 0:
                            pe.wait_ge(gelu_done, NF * c + f + 1)
                        t = nc.tensor.matmul(ffn_psum[:, i, :], GELU[:, f, i * NODE:(i + 1) * NODE],
                                             W2S[:, f, :], start=f == 0, stop=f == NF - 1)
                t.then_inc(ffn_done, 1)

            pe.wait_ge(shared_in, 32)
            shared(0)
            pe.wait_ge(mask_ready, 1)
            mask = CUM.rearrange("p t e -> p (t e)")
            nc.tensor.matmul(PS[0:NODE, 6, 0:TE], TRI[:, :], mask, start=True, stop=True)
            nc.tensor.matmul(PS[:, 7, 0:TE], ONES[0:NODE, :], mask, start=True, stop=True).then_inc(counted, 1)
            with pe.Fori(1, CHUNKS) as c:
                shared(c)

            def turn_slots(s):
                pe.wait_ge(slot_in, 16 * (s + 1))
                for k in range(KD):
                    t = nc.tensor.transpose(slot_turn_psum[:, k, :], SLOTROW[:, k * 128:(k + 1) * 128],
                                            IDENT[:, :])
                t.then_inc(slot_turned, 1)

            turn_slots(0)

            def expert(e, q, i):
                first = pe.value_load(OFFI[0:1, ds(e, 1)], min_val=0, max_val=SLOT_TILES - 1)
                end = pe.value_load(OFFI[0:1, ds(e + 1, 1)], min_val=1, max_val=SLOT_TILES - 1)
                with pe.Fori(first, end) as s:
                    pe.wait_ge(expert_in[q], 32 * (i + 1))
                    pe.wait_ge(slot_feat, s + 1)
                    for f in range(NF):
                        if f >= 4:
                            pe.wait_ge(slot_gelu, NF * s + f - 3)
                        for k in range(KD):
                            t = nc.tensor.matmul(slot_hidden_psum[f], W1X[q][:, k, f * 128:(f + 1) * 128],
                                                 SLOTFEAT[:, k, :], start=k == 0, stop=k == KD - 1)
                        t.then_inc(slot_hidden, 1)
                    turn_slots(s + 1)
                    pe.wait_ge(slot_taken, s + 1)
                    for f in range(NF):
                        pe.wait_ge(slot_gelu, NF * s + f + 1)
                        t = nc.tensor.matmul(slot_ffn_psum, SLOTGELU[:, f, :], W2X[q][:, f, :],
                                             start=f == 0, stop=f == NF - 1)
                    t.then_inc(slot_ffn, 1)

            with pe.Fori(0, EXPERTS // 2) as i:
                expert(2 * i, 0, i)
                expert(2 * i + 1, 1, i)

        @block.vector
        def _(dve):
            chain = [0]

            def link(*instructions):
                for t in instructions:
                    t.then_inc(dve_chain, 1)
                chain[0] += len(instructions)
                dve.wait_ge(dve_chain, chain[0])

            v = nc.vector
            for one_ahead in (*kept, *kept, *onehot_ready, out_ready, slot_taken, slot_row):
                dve.sem_inc(one_ahead, 1)
            dve.wait_ge(pool_const, 10)
            v.tensor_copy(FILL[:, D:D + 1], IOTAI[:, 180:181]).then_inc(const_ready, 1)
            link(v.tensor_copy(IOTA[:, :], IOTAI[:, 0:NODE]),
                 v.tensor_copy(NEG[:, :], IOTAI[:, 128:128 + TILES]),
                 v.tensor_copy(DOWN, IOTAI[0:NODE, 184:192]),
                 v.tensor_copy(LN[:, 3, :], IOTAI[0:NODE, 192:192 + TILES]))

            per = TILES // PIECES
            for i in range(PIECES):
                dve.wait_ge(x_in[i], 32)
                with dve.Fori(i * per, (i + 1) * per) as t:
                    v.bn_stats(LNSTAT[:, ds(t, 1), :], X[:, ds(t, 1), :]).then_inc(ln_stats, 1)

            def row_moments(ready):
                even, odd = LNSTAT[:, :, 1], LNSTAT[:, :, 4]
                link(v.tensor_tensor(LN[:, 0, :], even, odd, ALU.add),
                     v.tensor_tensor(LN[:, 1, :], even, odd, ALU.subtract),
                     v.tensor_tensor(MV[:, :, 1], LNSTAT[:, :, 2], LNSTAT[:, :, 5], ALU.add))
                link(v.scalar_tensor_tensor(out=LN[:, 2, :], in0=LN[:, 1, :], scalar=0.25, in1=LN[:, 1, :],
                                            op0=ALU.mult, op1=ALU.mult),
                     v.tensor_scalar(MV[:, :, 0], LN[:, 0, :], 0.5, None, ALU.mult))
                link(v.scalar_tensor_tensor(out=MV[:, :, 1], in0=MV[:, :, 1], scalar=1.0 / D, in1=LN[:, 2, :],
                                            op0=ALU.mult, op1=ALU.add))
                dve.sem_inc(ready, 1)

            dve.wait_ge(ln_stats, TILES)
            row_moments(moments_in)

            def layer_norm_scale(std, ready):
                dve.wait_ge(std, 1)
                link(v.reciprocal(LN[:, 1, :], LN[:, 0, :]))
                v.scalar_tensor_tensor(out=LN[:, 2, :], in0=MV[:, :, 0], scalar=-1.0, in1=LN[:, 1, :],
                                       op0=ALU.mult, op1=ALU.mult).then_inc(ready, 1)

            layer_norm_scale(ln_std, ln_ready)

            dve.wait_ge(edges_in, 32)
            link(v.tensor_copy(DST, DSTI))
            link(v.tensor_scalar(TILEOF, DST, 1.0 / NODE, 0.5 / NODE - 0.5, ALU.mult, ALU.add))
            link(v.tensor_scalar(TILEOF, TILEOF, ROUND, None, ALU.add))
            link(v.tensor_scalar(TILEOF, TILEOF, ROUND, None, ALU.subtract))
            by_group = TILEOF.rearrange("p (g k) -> p g k", k=GROUP)
            v.tensor_reduce(RANGES[:, 0, :], by_group, AX.X, ALU.max).then_inc(range_ready, 1)
            v.tensor_reduce(RANGES[:, 1, :], by_group, AX.X, ALU.min).then_inc(range_ready, 1)

            def count0(c, p):
                dve.wait_ge(turned0, c + 1)
                v.tensor_copy(feat[:, :, ds(CH * c, CH)], turn_psum[p]).then_inc(feat0, 1)
                dve.wait_ge(feat0, c + 1)
                for k in range(KD):
                    v.bn_stats(BNSTAT[:, k, ds(c, 1), :], feat[:, k, ds(CH * c, CH)].unsqueeze(1))\
                        .then_inc(bn0_counted, 1)

            chunks(dve, count0)
            dve.wait_ge(bn0_counted, KD * CHUNKS)

            def batch_norm(n, gamma, beta):
                for k in range(KD):
                    v.bn_aggr(BN[:, 0, k, :], BNSTAT[:, k, :, :].rearrange("p c s -> p (c s)"))\
                        .then_inc(dve_bn, 1)
                dve.wait_ge(bn_std, n + 1)
                link(v.reciprocal(BN[:, 1, :, 0], BN[:, 2, :, 0]))
                link(v.tensor_tensor(BN[:, 3, :, 0], BN[:, 1, :, 0], VEC[:, gamma, :], ALU.mult))
                link(v.tensor_tensor(BN[:, 4, :, 0], BN[:, 0, :, 0], BN[:, 3, :, 0], ALU.mult))
                v.tensor_tensor(BN[:, 5, :, 0], VEC[:, beta, :], BN[:, 4, :, 0], ALU.subtract)\
                    .then_inc(bn_ready, 1)
                dve.wait_ge(bn_ready, n + 1)

            dve.wait_ge(vec_in, 16)
            batch_norm(0, 0, 1)
            for i in range(2 * KD):
                v.tensor_scalar(DIAG[:, i, :], IDENT[:, :], BN[:, 3 if i < KD else 5, i % KD, 0:1], None,
                                ALU.mult).then_inc(diag_ready, 1)

            dve.wait_ge(range_turned, 1)
            turned_ranges = PS[0:GROUPS, 5, 0:256].rearrange("p (a q) -> p a q", a=2)
            v.tensor_reduce(EXTREMES[0:GROUPS, 0:1], turned_ranges[:, 0:1, :], AX.X, ALU.max).then_inc(row_ready, 1)
            v.tensor_reduce(EXTREMES[0:GROUPS, 1:2], turned_ranges[:, 1:2, :], AX.X, ALU.min).then_inc(row_ready, 1)
            dve.wait_ge(row_turned, 1)
            high, low, steps, ends, tile_less_step, firsts = [STEPS[:, i, :] for i in range(6)]
            link(v.tensor_scalar(high, PS[0:1, 6, 0:GROUPS], float(TILES - 1), None, ALU.min),
                 v.tensor_copy(low, PS[0:1, 6, GROUPS:2 * GROUPS]))
            link(v.scalar_tensor_tensor(out=steps, in0=high, scalar=1.0, in1=low, op0=ALU.add,
                                        op1=ALU.subtract))
            link(v.tensor_scalar(steps, steps, 1.0, None, ALU.max),
                 v.tensor_scalar(low, low, float(TILES - 1), None, ALU.min))
            link(v.tensor_tensor_scan(ends, ONES[0:1, 0:1].to_broadcast([1, GROUPS]), steps, 0.0, ALU.mult, ALU.add))
            link(v.tensor_tensor(firsts, ends, steps, ALU.subtract))
            link(v.tensor_tensor(tile_less_step, low, firsts, ALU.subtract))
            v.tensor_copy(TABLE[:, 0, :], firsts).then_inc(table_ready, 1)
            v.tensor_copy(TABLE[:, 1, :], ends).then_inc(table_ready, 1)
            v.tensor_copy(TABLE[:, 2, :], tile_less_step).then_inc(table_ready, 1)

            dve.wait_ge(spread_ready, 1)

            def h0(c, p):
                for i in range(2):
                    t = 2 * c + i
                    v.scalar_tensor_tensor(out=TMP[:, p, i, :].unsqueeze(1), in0=X[:, ds(t, 1), :], scalar=MV[:, ds(t, 1), 0],
                                           in1=SPREAD[0:NODE, 0:1, :], op0=ALU.subtract, op1=ALU.mult)\
                        .then_inc(centred, 1)
                dve.wait_ge(centred, 2 * c + 2)
                for i in range(2):
                    t = 2 * c + i
                    v.scalar_tensor_tensor(out=H[:, ds(t, 1), 0:D], in0=TMP[:, p, i, :].unsqueeze(1), scalar=LN[:, 1, ds(t, 1)],
                                           in1=SPREAD[0:NODE, 1:2, :], op0=ALU.mult, op1=ALU.add)\
                        .then_inc(h0_ready, 1)

            chunks(dve, h0)

            dve.wait_ge(table_ready, 3)
            dve.wait_ge(rows_in, 16)
            for layer in range(2):
                def onehots(i, layer=layer):
                    for r in range(RING):
                        g = RING * i + r
                        first = dve.value_load(TABLE[0:1, 0, ds(g, 1)], min_val=0, max_val=GROUPS * TILES)
                        end = dve.value_load(TABLE[0:1, 1, ds(g, 1)], min_val=1, max_val=GROUPS * TILES)
                        shift = dve.value_load(TABLE[0:1, 2, ds(g, 1)], min_val=-GROUPS * TILES, max_val=TILES)
                        with dve.Fori(first, end) as s:
                            j = nc.s_assert_within(s + shift, 0, TILES - 1, skip_runtime_bounds_check_because=
                                                   "step + shift runs from a group's lowest to its highest node tile")
                            dve.wait_ge(onehot_ready[layer], 2 * s + 1)
                            v.tensor_scalar(REL[:, :], DST[:, ds(GROUP * g, GROUP)], NEG[:, ds(j, 1)], None,
                                            ALU.add).then_inc(rel_ready[layer], 1)
                            dve.wait_ge(rel_ready[layer], s + 1)
                            for half in range(2):
                                dve.wait_ge(onehot_used[layer], 2 * s + half + 1)
                                v.tensor_tensor(ONEHOT[half],
                                                IOTA[:, :].unsqueeze(1).to_broadcast([128, HALF, NODE]),
                                                REL[:, half * HALF:(half + 1) * HALF].unsqueeze(2)
                                                .to_broadcast([128, HALF, NODE]), ALU.is_equal)\
                                    .then_inc(onehot_ready[layer], 1)

                with dve.Fori(0, ROUNDS) as i:
                    onehots(i)

                base = layer * CHUNKS

                def count(c, p, base=base):
                    dve.wait_ge(z_kept, KD * (c + base + 1))
                    for k in range(KD):
                        v.bn_stats(BNSTAT[:, k, ds(c, 1), :], feat[:, k, ds(CH * c, CH)].unsqueeze(1))\
                            .then_inc(bn_counted, 1)

                chunks(dve, count)
                dve.wait_ge(bn_counted, KD * CHUNKS * (layer + 1))
                batch_norm(layer + 1, 3 + 3 * layer, 4 + 3 * layer)

                def keep_turned(c, p):
                    dve.wait_ge(turned, c + 1)
                    v.tensor_copy(feat[:, :, ds(CH * c, CH)], turn_psum[p]).then_inc(h1_turned, 1)

                def take_y(c, p, base=base, layer=layer):
                    dve.wait_ge(y_ready, c + base + 1)
                    if layer == 0:
                        wait_count(dve, h1_ready, c - 1)
                    v.tensor_tensor(TMP[:, p, :, :], y_psum[p],
                                    ROWS[:, layer:layer + 1, :].to_broadcast([NODE, 2, D]), ALU.add)\
                        .then_inc(y_taken, 1)
                    if layer == 0 and not (isinstance(c, int) and c == 0):
                        keep_turned(c - 1, 1 - p)
                    if layer == 1:
                        dve.wait_ge(y_taken, c + base + 1)
                        v.scalar_tensor_tensor(out=X[:, ds(2 * c, 2), :], in0=TMP[:, p, :, :], scalar=0.0,
                                               in1=X[:, ds(2 * c, 2), :], op0=ALU.max, op1=ALU.add)\
                            .then_inc(x2_ready, 1)
                        dve.wait_ge(x2_ready, c + 1)
                        for i in range(2):
                            t = 2 * c + i
                            v.bn_stats(LNSTAT[:, ds(t, 1), :], X[:, ds(t, 1), :]).then_inc(x2_stats, 1)

                chunks(dve, take_y)
                if layer == 0:
                    keep_turned(CHUNKS - 1, 0)

            dve.wait_ge(x2_stats, TILES)
            row_moments(moments_mid)
            layer_norm_scale(ln2_std, ln2_ready)
            dve.wait_ge(ln2_ready, 1)

            def route_in(c, p):
                for i in range(2):
                    t = 2 * c + i
                    v.tensor_scalar(H[:, ds(t, 1), 0:D], X[:, ds(t, 1), :], MV[:, ds(t, 1), 0], LN[:, 1, ds(t, 1)],
                                    ALU.subtract, ALU.mult).then_inc(row_norm, 1)
                dve.wait_ge(feat2, c + 1)
                wait_count(dve, logit_done, c - 1)
                v.tensor_copy(RT[p], feat[:, :, ds(CH * c, CH)]).then_inc(half2, 1)
                dve.wait_ge(logit_done, c + 1)
                v.tensor_copy(LOGIT[:, ds(2 * c, 2), :], logit_psum[p]).then_inc(logit_kept, 1)

            chunks(dve, route_in)
            dve.wait_ge(logit_kept, CHUNKS)
            dve.wait_ge(row_norm, TILES)

            def over_experts(s):
                return s.unsqueeze(2).to_broadcast([NODE, TILES, EXPERTS])

            down = DOWN.unsqueeze(1).to_broadcast([NODE, TILES, EXPERTS])
            link(v.tensor_reduce(S0, LOGIT, AX.X, ALU.max))
            v.tensor_tensor(LOGIT, LOGIT, over_experts(S0), ALU.subtract).then_inc(logit_max, 1)
            dve.wait_ge(exp_ready, 1)
            link(v.tensor_reduce(S1, LOGIT, AX.X, ALU.add))
            link(v.reciprocal(S2, S1))
            link(v.tensor_tensor(LOGIT, LOGIT, over_experts(S2), ALU.mult))
            link(v.tensor_reduce(S0, LOGIT, AX.X, ALU.max))
            link(v.tensor_tensor(TOP1, LOGIT, over_experts(S0), ALU.is_equal))
            link(v.tensor_tensor(CAND, TOP1, down, ALU.mult))
            link(v.tensor_reduce(S1, CAND, AX.X, ALU.max))
            link(v.tensor_tensor(TOP1, down, over_experts(S1), ALU.is_equal))
            link(v.scalar_tensor_tensor(out=CAND, in0=TOP1, scalar=-4.0, in1=LOGIT, op0=ALU.mult, op1=ALU.add))
            link(v.tensor_reduce(S1, CAND, AX.X, ALU.max))
            link(v.tensor_tensor(TOP2, CAND, over_experts(S1), ALU.is_equal))
            link(v.tensor_tensor(CAND, TOP2, down, ALU.mult))
            link(v.tensor_reduce(S2, CAND, AX.X, ALU.max))
            link(v.tensor_tensor(TOP2, down, over_experts(S2), ALU.is_equal))
            link(v.tensor_tensor(CUM, TOP1, TOP2, ALU.add))
            dve.sem_inc(mask_ready, 1)
            link(v.tensor_tensor(S2, S0, S1, ALU.add))
            link(v.reciprocal(S3, S2))
            link(v.tensor_tensor(S0, S0, S3, ALU.mult), v.tensor_tensor(S1, S1, S3, ALU.mult))
            link(v.tensor_tensor(LOGIT, TOP1, over_experts(S0), ALU.mult),
                 v.tensor_tensor(CAND, TOP2, over_experts(S1), ALU.mult))
            link(v.tensor_tensor(H[:, :, D + 1:ROW], LOGIT, CAND, ALU.add),
                 v.tensor_copy(H[:, :, D:D + 1], LN[:, 3, :].unsqueeze(2)))
            dve.wait_ge(counted, 1)
            before = PS[0:NODE, 6, 0:TE].rearrange("p (t e) -> p t e", t=TILES)
            of_tile = PS[0:NODE, 7, 0:TE].rearrange("p (t e) -> p t e", t=TILES)
            link(*[v.tensor_tensor_scan(CUM2[:, :, e], ONES[0:NODE, 0:TILES], of_tile[:, :, e], 0.0,
                                        ALU.mult, ALU.add) for e in range(EXPERTS)])
            link(v.tensor_tensor(POS, CUM2, of_tile, ALU.subtract))
            link(v.tensor_tensor(POS, POS, before, ALU.add))
            tiles_of, ends_of, starts_of = [OFFF[0:NODE, i, :] for i in range(3)]
            link(v.tensor_scalar(tiles_of, CUM2[:, TILES - 1, :], 1.0 / 128, 127.0 / 256, ALU.mult, ALU.add))
            link(v.tensor_scalar(tiles_of, tiles_of, ROUND, None, ALU.add))
            link(v.tensor_scalar(tiles_of, tiles_of, ROUND, None, ALU.subtract))
            link(v.tensor_scalar(tiles_of, tiles_of, 1.0, None, ALU.max))
            link(v.tensor_tensor_scan(ends_of, ONES[0:NODE, 0:EXPERTS], tiles_of, 0.0, ALU.mult, ALU.add))
            link(v.tensor_tensor(starts_of, ends_of, tiles_of, ALU.subtract))
            link(v.tensor_copy(OFFI[:, 0:EXPERTS], starts_of[0:1, :]),
                 v.tensor_copy(OFFI[:, EXPERTS:EXPERTS + 1], ends_of[0:1, EXPERTS - 1:EXPERTS]))
            dve.sem_inc(off_ready, 1)
            link(v.scalar_tensor_tensor(out=POS, in0=starts_of.unsqueeze(1).to_broadcast([NODE, TILES, EXPERTS]),
                                        scalar=128.0, in1=POS, op0=ALU.mult, op1=ALU.add))
            link(v.tensor_tensor(CAND, TOP1, POS, ALU.mult), v.tensor_tensor(CUM2, TOP2, POS, ALU.mult))
            link(v.tensor_reduce(S0, CAND, AX.X, ALU.add), v.tensor_reduce(S1, CUM2, AX.X, ALU.add))
            link(v.tensor_copy(POSI[:, 0, :], S0), v.tensor_copy(POSI[:, 1, :], S1))
            dve.sem_inc(pos_ready, 1)

            with dve.Fori(0, CHUNKS) as c:
                dve.wait_ge(ffn_done, c + 1)
                dve.wait_ge(out_ready, c + 1)
                v.tensor_tensor(TMP[:, 0, :, :], ffn_psum, ROWS[:, 2:3, :].to_broadcast([NODE, 2, D]), ALU.add)\
                    .then_inc(ffn_taken, 1)
                dve.wait_ge(ffn_taken, c + 1)
                v.tensor_tensor(X[:, ds(2 * c, 2), :], X[:, ds(2 * c, 2), :], TMP[:, 0, :, :], ALU.add)\
                    .then_inc(out_ready, 1)

            def take_slots(s):
                dve.wait_ge(slot_turned, s + 1)
                v.tensor_copy(SLOTFEAT, slot_turn_psum).then_inc(slot_feat, 1)

            def keep_meta(s):
                v.tensor_copy(META[:, ds(s, 1), :], SLOTROW[:, D:ROW].unsqueeze(1)).then_inc(slot_meta, 1)

            take_slots(0)
            keep_meta(0)
            dve.wait_ge(b2_in, 16)
            with dve.Fori(0, EXPERTS) as e:
                first = dve.value_load(OFFI[0:1, ds(e, 1)], min_val=0, max_val=SLOT_TILES - 1)
                end = dve.value_load(OFFI[0:1, ds(e + 1, 1)], min_val=1, max_val=SLOT_TILES - 1)
                with dve.Fori(first, end) as s:
                    take_slots(s + 1)
                    keep_meta(s + 1)
                    dve.wait_ge(slot_ffn, s + 2)
                    dve.wait_ge(slot_row, 2 * s + 1)
                    v.tensor_tensor(SLOTSUM.unsqueeze(1), slot_ffn_psum.unsqueeze(1), B2X[:, ds(e, 1), :], ALU.add)\
                        .then_inc(slot_taken, 1)
                    dve.wait_ge(slot_taken, s + 2)
                    dve.wait_ge(slot_free, s + 1)
                    v.tensor_scalar(SLOTOUT.unsqueeze(1), SLOTSUM.unsqueeze(1), META[:, ds(s, 1), ds(e + 1, 1)], None, ALU.mult)\
                        .then_inc(slot_row, 1)
                    v.tensor_copy(TOKEN[:, 0:1].unsqueeze(1), META[:, ds(s, 1), 0:1]).then_inc(slot_row, 1)


def kernel(x, src, dst, L0_gnn_g0, L0_gnn_b0, L0_gnn_W1a, L0_gnn_b1a, L0_gnn_g1, L0_gnn_bt1, L0_gnn_W1b,
           L0_gnn_b1b, L0_gnn_W2a, L0_gnn_b2a, L0_gnn_g2, L0_gnn_bt2, L0_gnn_W2b, L0_gnn_b2b, L0_ffn_Wr,
           L0_ffn_W1s, L0_ffn_b1s, L0_ffn_W2s, L0_ffn_b2s, L0_ffn_W1p, L0_ffn_b1p, L0_ffn_W2p, L0_ffn_b2p):
    import numpy as np
    import concourse.bacc as bacc
    from concourse import mybir
    from concourse.bass_utils import run_bass_kernel_spmd

    def by_tile(a, fill):
        a = np.pad(np.asarray(a), (0, EDGE_TILES * 128 - E), constant_values=fill)
        return np.ascontiguousarray(a.reshape(EDGE_TILES, 128).T)

    def columns(*vectors):
        a = np.stack([np.asarray(v) for v in vectors])
        return np.ascontiguousarray(a.reshape(len(vectors), -1, 128).transpose(2, 0, 1))

    arrays = {
        "x": np.asarray(x), "src": by_tile(src, 0), "dst": by_tile(dst, FAR),
        "vecs": columns(L0_gnn_g0, L0_gnn_b0, L0_gnn_b1a, L0_gnn_g1, L0_gnn_bt1, L0_gnn_b2a, L0_gnn_g2,
                        L0_gnn_bt2),
        "w1a": np.asarray(L0_gnn_W1a), "w1b": np.asarray(L0_gnn_W1b),
        "w2a": np.asarray(L0_gnn_W2a), "w2b": np.asarray(L0_gnn_W2b),
        "rows": np.stack([np.asarray(v) for v in (L0_gnn_b1b, L0_gnn_b2b, L0_ffn_b2s)]),
        "wr": np.asarray(L0_ffn_Wr), "w1s": np.asarray(L0_ffn_W1s), "w2s": np.asarray(L0_ffn_W2s),
        "b1": columns(L0_ffn_b1s, *np.asarray(L0_ffn_b1p)),
        "w1p": np.asarray(L0_ffn_W1p), "w2p": np.asarray(L0_ffn_W2p), "b2p": np.asarray(L0_ffn_b2p),
    }
    nc = bacc.Bacc("TRN2", target_bir_lowering=False, num_devices=1)
    args = {n: nc.dram_tensor(f"in_{n}", a.shape, mybir.dt.from_np(a.dtype), kind="ExternalInput").ap()
            for n, a in arrays.items()}
    out = nc.dram_tensor("out", (N + 128, D), mybir.dt.float32, kind="ExternalOutput").ap()
    build(nc, out=out, **args)
    result = run_bass_kernel_spmd(nc, [{f"in_{n}": a for n, a in arrays.items()}], core_ids=[0])
    return result.results[0]["out"][0:N]
```

```python
N, D, E = 6250, 256, 106250
NODE = 125
TILES = N // NODE
KD = D // 128
CH = 2 * NODE
CHUNKS = N // CH
PIECE = (0, 4, 8, 16, CHUNKS)
PIECES = len(PIECE) - 1
GROUP = 8
RING = 4
EDGE_TILES = -(-E // (128 * GROUP * RING)) * GROUP * RING
GROUPS = EDGE_TILES // GROUP
ROUNDS = GROUPS // RING
HALF = GROUP // 2
F, NF, EXPERTS, TOPK = 1024, 1024 // 128, 8, 2
ROW = D + 1 + EXPERTS
BLOCK = 256
SLOT_BLOCKS = (TOPK * N + EXPERTS * (BLOCK - 1)) // BLOCK + 1
HB = BLOCK // 128
EPS = 1e-5
ROUND = 12582912.0
FAR = 1 << 20
VECS = 8


def build(nc, x, src, dst, vecs, w1a, w1b, w2a, w2b, rows, wr, w1s, w2s, b1, w1p, w2p, b2p, out):
    from contextlib import ExitStack

    import concourse.bass as bass
    from concourse import mybir

    F32, I32, F32R = mybir.dt.float32, mybir.dt.int32, mybir.dt.float32r
    ACT, ALU, AX = mybir.ActivationFunctionType, mybir.AluOpType, mybir.AxisListType
    ds = bass.ds

    with ExitStack() as ctx:
        def sb(name, shape, dt=F32):
            return ctx.enter_context(nc.sbuf_tensor(name, shape, dt))

        def sem(name):
            return ctx.enter_context(nc.semaphore(name))

        tables = [nc.dram_tensor(f"table{l}", (N, D), F32).ap() for l in range(2)]
        slots = nc.dram_tensor("slots", (SLOT_BLOCKS * BLOCK, ROW), F32).ap()

        XA = sb("X", [128, TILES, D])
        X = XA[0:NODE]
        HA = sb("H", [128, TILES, ROW])
        H_AT = nc.sbuf_base - 4 * TILES * ROW
        H = HA[0:NODE]
        FT = sb("FT", [128, KD * N])
        FT_AT = nc.sbuf_base - 4 * KD * N
        feat = FT[:, :].rearrange("p (k n) -> p k n", k=KD)
        WORDS, FEAT_WORDS = 4 * KD * F, 2 * KD * BLOCK
        G_WORDS = 4 * KD * D + 2 * KD * CH + 72
        E_ = sb("edge_arena", [128, WORDS + FEAT_WORDS - G_WORDS])
        E_AT = nc.sbuf_base - 4 * (WORDS + FEAT_WORDS - G_WORDS)
        G_ = sb("gnn_arena", [128, G_WORDS])
        assert nc.sbuf_base == E_AT + 4 * (WORDS + FEAT_WORDS)

        def cut(arena, at, shape):
            size = 1
            for s in shape:
                size *= s
            v = arena[:, at:at + size]
            names = "abcd"[:len(shape)]
            if len(shape) > 1:
                v = v.rearrange(f"p ({' '.join(names)}) -> p {' '.join(names)}",
                                **{n: s for n, s in zip(names, shape)})
            return v

        SRC = cut(E_, 0, [EDGE_TILES]).bitcast(I32)
        DST = cut(E_, EDGE_TILES, [EDGE_TILES])
        ONEHOT = [cut(E_, 2 * EDGE_TILES + i * HALF * NODE, [HALF, NODE]) for i in range(2)]
        FILL = cut(E_, 2 * EDGE_TILES + 3 * HALF * NODE, [HB, ROW])
        W = [[cut(G_, (2 * l + i) * KD * D, [KD, D]) for i in range(2)] for l in range(2)]
        RT = [cut(G_, 4 * KD * D + p * KD * CH, [KD, CH]) for p in range(2)]
        TE = TILES * EXPERTS
        LOGIT, TOP1, TOP2, CAND, POS, CUM, CUM2 = [
            cut(E_, i * TE, [TILES, EXPERTS])[0:NODE] for i in range(7)]
        HX = HA[:, :, :].rearrange("p t r -> p (t r)")
        DSTI = cut(HX, 0, [EDGE_TILES]).bitcast(I32)
        TILEOF = cut(HX, EDGE_TILES, [EDGE_TILES])
        RANGES = cut(HX, 2 * EDGE_TILES, [2, GROUPS])
        AT = 2 * EDGE_TILES + 2 * GROUPS
        EXTREMES = cut(HX, AT, [4])
        STEPS = cut(HX, AT + 4, [8, GROUPS])[0:1]
        IOTAI = cut(HX, AT + 4 + 8 * GROUPS + 512, [256]).bitcast(I32)
        GATHERED = cut(HX, 0, [RING, GROUP, D])
        assert KD * F == NF * D
        SLOTROW = cut(HX, WORDS + 2 * NF * CH, [HB, ROW])
        AT = WORDS + 2 * NF * CH + HB * ROW
        TOKENS = cut(HX, AT, [TILES, 1 + EXPERTS])[0:NODE]
        assert AT + TILES * (1 + EXPERTS) <= TILES * ROW
        B2X, SLOTOUT = cut(HX, 0, [EXPERTS, D]), cut(HX, EXPERTS * D, [HB, D])
        LOADED = [nc.alloc_sbuf_tensor_at(f"loaded{q}", [128, 2, KD * F], F32, offset=at + 2 * WORDS)
                  for q, at in enumerate((E_AT, FT_AT))]
        SHARED_LOADED = cut(HX, WORDS // 2, [2, KD * F])
        GELU_ALL = cut(FT, WORDS + NF * BLOCK, [NF, BLOCK])
        SHARED_GELU_ALL = cut(HX, WORDS + NF * CH, [NF, CH])
        WEIGHT = [nc.alloc_sbuf_tensor_at(f"weight{q}", [128, 2, 2, KD * F], F32R, offset=at)
                  for q, at in enumerate((E_AT, FT_AT))]
        SHARED_W = nc.alloc_sbuf_tensor_at("shared_weight", [128, 2, 2, KD * F], F32R, offset=H_AT)
        SHARED_GELU = nc.alloc_sbuf_tensor_at("shared_gelu_parts", [128, 2, NF, CH], F32R, offset=H_AT + 4 * WORDS)
        SHARED_FEAT = nc.alloc_sbuf_tensor_at("shared_feat_parts", [128, 2, KD, CH], F32R, offset=E_AT + 4 * WORDS)
        W1X = [[WEIGHT[q][:, part, 0, :].rearrange("p (k f) -> p k f", k=KD) for part in range(2)] for q in range(2)]
        W2X = [[WEIGHT[q][:, part, 1, :].rearrange("p (f d) -> p f d", f=NF) for part in range(2)] for q in range(2)]
        W1S = [SHARED_W[:, part, 0, :].rearrange("p (k f) -> p k f", k=KD) for part in range(2)]
        W2S = [SHARED_W[:, part, 1, :].rearrange("p (f d) -> p f d", f=NF) for part in range(2)]
        SLOTGELU = nc.alloc_sbuf_tensor_at("slot_gelu_parts", [128, 2, NF, BLOCK], F32R, offset=FT_AT + 4 * WORDS)
        SLOTFEAT = nc.alloc_sbuf_tensor_at("slot_feat_parts", [128, 2, KD, BLOCK], F32R, offset=E_AT + 4 * WORDS)
        TABLE = sb("TABLE", [1, 3, GROUPS], I32)
        FINAL = sb("FINAL", [1, ROUNDS + 2], I32)
        IDX = sb("IDX", [128, RING, GROUP], I32)
        STAGE = sb("STAGE", [128, 2, 2, D])
        TMP = sb("TMP", [NODE, 2, 2, D])
        ROWS = sb("ROWS", [NODE, 3, D])
        IDENT = sb("IDENT", [128, 128])
        ONES = sb("ONES", [128, 128])
        TRI = sb("TRI", [NODE, NODE])
        IOTA = sb("IOTA", [128, NODE])
        NEG = sb("NEG", [128, TILES])
        REL = sb("REL", [128, GROUP])
        MISC = sb("MISC", [128, 64])
        VEC = sb("VEC", [128, VECS, KD])
        B1 = sb("B1", [128, 1 + EXPERTS, NF])
        WR = sb("WR", [128, KD, EXPERTS])
        LNSTAT = sb("LNSTAT", [NODE, TILES, 6])
        LN = sb("LN", [NODE, 4, TILES])
        MV = sb("MV", [NODE, TILES, 2])
        BNSTAT = sb("BNSTAT", [128, KD, CHUNKS, 6])
        BN = sb("BN", [128, 6, KD, 2])
        POSI = sb("POSI", [NODE, TOPK, TILES], I32)
        OFFI = sb("OFFI", [1, 16], I32)
        EPST = MISC[:, 0:1]
        OFFF = MISC[:, 8:32].rearrange("p (a b) -> p a b", a=3)
        DOWN = MISC[0:NODE, 40:48]
        assert 7 * TE + 4 * TILES <= WORDS // 2
        S0, S1, S2, S3 = [cut(E_, 7 * TE + i * TILES, [TILES])[0:NODE] for i in range(4)]
        SEND = 4
        POS32 = sb("POS32", [NODE, SEND, TOPK], I32)
        META = sb("META", [128, 2 * HB, 1 + EXPERTS])
        TOKEN = sb("TOKEN", [128, HB], I32)
        SENDROW = [cut(STAGE[:, :, :, :].rearrange("p a b d -> p (a b d)"), q * ROW, [ROW])[0:NODE]
                   for q in range(SEND - 1)]
        SENDROW.append(TMP[:, 1, :, :].rearrange("p i d -> p (i d)")[:, 0:ROW])
        SLOTSUM = cut(STAGE[:, :, :, :].rearrange("p a b d -> p (a b d)"), 0, [HB, D])

        PS = ctx.enter_context(nc.psum_tensor("PS", [128, 8, 512], F32))

        x_in = [sem(f"x_in{i}") for i in range(PIECES)]
        edges_in, vec_in, rows_in, gnnw_in, ffn_small_in = map(
            sem, ("edges_in", "vec_in", "rows_in", "gnnw_in", "ffn_small_in"))
        pool_const, const_ready, dve_chain = map(sem, ("pool_const", "const_ready", "dve_chain"))
        ln_stats, moments_in, ln_std, ln_ready = map(sem, ("ln_stats", "moments_in", "ln_std", "ln_ready"))
        staged0, turned0, feat0, bn0_counted = map(sem, ("staged0", "turned0", "feat0", "bn0_counted"))
        bn_std, bn_ready = map(sem, ("bn_std", "bn_ready"))
        dve_bn = sem("bn_moments")
        h0_staged, turned_back, h0_ready = map(sem, ("h0_staged", "turned_back", "h0_ready"))
        range_ready, range_turned, row_ready, row_turned, table_ready = map(
            sem, ("range_ready", "range_turned", "row_ready", "row_turned", "table_ready"))
        stored = [sem(f"stored{l}") for l in range(2)]
        index_ready = sem("index_ready")
        gathered = [sem(f"gathered{r}") for r in range(RING)]
        group_used = sem("group_used")
        rel_ready = [sem(f"rel_ready{l}") for l in range(2)]
        onehot_ready = [sem(f"onehot_ready{l}") for l in range(2)]
        onehot_used = [sem(f"onehot_used{l}") for l in range(2)]
        summed = [sem(f"summed{l}") for l in range(2)]
        kept = [sem(f"kept{l}") for l in range(2)]
        h0_turned = sem("h0_turned")
        agg_done = sem("agg_done")
        staged, turned, h1_turned, z_ready, z_kept, bn_counted = map(
            sem, ("staged", "turned", "h1_turned", "z_ready", "z_kept", "bn_counted"))
        relu_ready, y_ready, y_taken, h1_ready, x2_ready, x2_stats = map(
            sem, ("relu_ready", "y_ready", "y_taken", "h1_ready", "x2_ready", "x2_stats"))
        moments_mid, ln2_std, ln2_ready = map(sem, ("moments_mid", "ln2_std", "ln2_ready"))
        staged2, turned2, feat2, half2, logit_done, logit_kept = map(
            sem, ("staged2", "turned2", "feat2", "half2", "logit_done", "logit_kept"))
        logit_max, exp_ready, mask_ready, counted, pos_ready, off_ready = map(
            sem, ("logit_max", "exp_ready", "mask_ready", "counted", "pos_ready", "off_ready"))
        shared_in, hidden, gelu_done, ffn_done, ffn_taken, out_ready, out_stored, spare_zero = map(
            sem, ("shared_in", "hidden", "gelu_done", "ffn_done", "ffn_taken", "out_ready",
                  "out_stored", "spare_zero"))
        filled = sem("filled")
        scattered = [sem(f"scattered{q}") for q in range(SEND)]
        send_ready, shared_high_w, shared_split, first_high, first_feat, first_low = map(
            sem, ("send_ready", "shared_high_w", "shared_split", "first_high", "first_feat", "first_low"))
        shared_high, feat_high, shared_feat, shared_low = map(
            sem, ("shared_high", "feat_high", "shared_feat", "shared_low"))
        act_carrier = sem("act_carrier")
        wait_carrier = sem("wait_carrier")
        expert_in = [sem(f"expert_in{q}") for q in range(2)]
        first_slots_in = sem("first_slots_in")
        w_high = [sem(f"w_high{q}") for q in range(2)]
        w_split = [sem(f"w_split{q}") for q in range(2)]
        b2_in, slot_in, slot_turned, slot_high, slot_feat, slot_meta = map(
            sem, ("b2_in", "slot_in", "slot_turned", "slot_high", "slot_feat", "slot_meta"))
        slot_hidden, slot_gelu, gelu_high, gelu_low, slot_ffn, slot_taken, slot_row, slot_added = map(
            sem, ("slot_hidden", "slot_gelu", "gelu_high", "gelu_low", "slot_ffn", "slot_taken",
                  "slot_row", "slot_added"))
        slot_free = sem("slot_free")

        def wait_count(eng, semaphore, value):
            if isinstance(value, int) and value <= 0:
                return
            eng.wait_ge(semaphore, value)

        def chunks(eng, body, start=0, stop=CHUNKS):
            if start == 0:
                body(0, 0)
                body(1, 1)
                start = 2
            if stop // 2 > start // 2:
                with eng.Fori(start // 2, stop // 2) as i:
                    body(2 * i, 0)
                    body(2 * i + 1, 1)
            if stop % 2:
                body(stop - 1, 0)

        def piece_tiles(i):
            return slice(2 * PIECE[i], 2 * PIECE[i + 1])

        def final_chunks(eng, i, body, lag=0):
            most = CHUNKS - 1
            start = eng.value_load(FINAL[0:1, ds(i + 1 - lag, 1)], min_val=0, max_val=most)
            stop = eng.value_load(FINAL[0:1, ds(i + 2 - lag, 1)], min_val=0, max_val=most)
            with eng.If(start < stop), eng.Fori(start, stop) as c:
                body(c)

        def remaining_chunks(eng, body, lag=0):
            start = eng.value_load(FINAL[0:1, ROUNDS + 1 - lag:ROUNDS + 2 - lag], min_val=0, max_val=CHUNKS - 1)
            with eng.Fori(start, CHUNKS) as c:
                body(c)

        def last(c):
            return isinstance(c, int) and c == CHUNKS - 1

        PARTS = ((0, 112), (112, NODE))

        def by_tile(dram):
            return dram[0:N, :].rearrange("(t p) d -> p t d", p=NODE)

        turn_psum = [PS[:, p, 0:KD * CH].rearrange("q (k n) -> q k n", k=KD) for p in range(2)]
        back_psum = [PS[0:NODE, 2 + p, :].rearrange("q (i d) -> q i d", i=2) for p in range(2)]
        z_psum = PS[:, 2:4, 0:KD * CH].rearrange("q b (k n) -> q b k n", k=KD)
        sum_psum = PS[:, 4:8, 0:NODE]
        y_psum = [PS[0:NODE, 4 + p, :].rearrange("q (i d) -> q i d", i=2) for p in range(2)]
        logit_psum = [PS[0:NODE, 6 + p, 0:2 * EXPERTS].rearrange("q (i e) -> q i e", i=2) for p in range(2)]
        hidden_psum = [PS[:, f // 2, (f % 2) * BLOCK:(f % 2) * BLOCK + CH] for f in range(NF)]
        ffn_psum = PS[0:NODE, 4:6, :].rearrange("q b (i d) -> q b i d", i=2)
        slot_turn_psum = PS[:, 7, 0:KD * BLOCK].rearrange("q (k n) -> q k n", k=KD)
        slot_hidden_psum = [PS[:, f // 2, (f % 2) * BLOCK:(f % 2 + 1) * BLOCK] for f in range(NF)]
        slot_ffn_psum = PS[:, 5:5 + HB, 0:D]


        def load_expert(eng, e, q, done):
            eng.dma_start(LOADED[q][:, 0, :].rearrange("p (k f) -> p k f", k=KD), w1p[ds(e, 1)].rearrange("o (k p) f -> p (o k) f", p=128))\
                .then_inc(done, 16)
            eng.dma_start(LOADED[q][:, 1, :].rearrange("p (f d) -> p f d", f=NF), w2p[ds(e, 1)].rearrange("o (f p) d -> p (o f) d", p=128))\
                .then_inc(done, 16)

        def load_slots(eng, s, done):
            eng.dma_start(SLOTROW, slots[ds(BLOCK * s, BLOCK), :].rearrange("(h p) r -> p h r", p=128))\
                .then_inc(done, 16)

        block = ctx.enter_context(nc.Block())

        @block.sync
        def _(sp):
            for i in range(PIECES):
                t = piece_tiles(i)
                for a, b in PARTS:
                    sp.dma_start(X[a:b, t, :], by_tile(x)[a:b, t, :]).then_inc(x_in[i], 16)

            def store_table(layer, source_ready):
                def store(c, p):
                    sp.wait_ge(source_ready, c + 1)
                    for a, b in PARTS:
                        sp.dma_start(by_tile(tables[layer])[a:b, ds(2 * c, 2), :],
                                     H[a:b, ds(2 * c, 2), 0:D]).then_inc(stored[layer], 16)
                return store

            chunks(sp, store_table(0, h0_ready))
            chunks(sp, store_table(1, h1_ready))

            sp.wait_ge(agg_done, 2)
            sp.dma_start(SHARED_LOADED[:, 0, :].rearrange("p (k f) -> p k f", k=KD),
                         w1s.rearrange("(k p) f -> p k f", p=128)).then_inc(shared_in, 16)
            sp.dma_start(SHARED_LOADED[:, 1, :].rearrange("p (f d) -> p f d", f=NF),
                         w2s.rearrange("(f p) d -> p f d", p=128)).then_inc(shared_in, 16)
            sp.wait_ge(pos_ready, 1)
            load_expert(sp, 0, 0, expert_in[0])

            def store_out(c, p):
                sp.wait_ge(out_ready, c + 2)
                for a, b in PARTS:
                    sp.dma_start(by_tile(out)[a:b, ds(2 * c, 2), :],
                                 X[a:b, ds(2 * c, 2), :]).then_inc(out_stored, 16)

            with sp.Fori(0, CHUNKS) as c:
                store_out(c, 0)
            sp.wait_ge(off_ready, 1)
            total = sp.value_load(OFFI[0:1, EXPERTS:EXPERTS + 1], min_val=EXPERTS, max_val=SLOT_BLOCKS - 1)
            with sp.Fori(1, total) as s:
                sp.wait_ge(slot_turned, s + 1)
                sp.wait_ge(slot_meta, s + 1)
                load_slots(sp, s + 1, slot_in)

        @block.gpsimd
        def _(pool):
            nc.gpsimd.memset(IDENT[:, :], 0.0).then_inc(pool_const, 1)
            nc.gpsimd.memset(TRI[:, :], 1.0).then_inc(pool_const, 1)
            nc.gpsimd.memset(ONES[:, :], 1.0).then_inc(pool_const, 1)
            nc.gpsimd.memset(FILL, 0.0).then_inc(pool_const, 1)
            nc.gpsimd.memset(EPST, EPS).then_inc(pool_const, 1)
            nc.gpsimd.iota(IOTAI[:, 0:NODE], [[1, NODE]], base=0, channel_multiplier=0)\
                .then_inc(pool_const, 1)
            nc.gpsimd.iota(IOTAI[:, 128:128 + TILES], [[-NODE, TILES]], base=0, channel_multiplier=0)\
                .then_inc(pool_const, 1)
            nc.gpsimd.iota(IOTAI[:, 180:182], [[128, HB]], base=N, channel_multiplier=1)\
                .then_inc(pool_const, 1)
            nc.gpsimd.iota(IOTAI[:, 184:192], [[-1, EXPERTS]], base=EXPERTS, channel_multiplier=0)\
                .then_inc(pool_const, 1)
            nc.gpsimd.iota(IOTAI[:, 192:192 + TILES], [[NODE, TILES]], base=0, channel_multiplier=1)\
                .then_inc(pool_const, 1)
            pool.wait_ge(pool_const, 10)
            nc.gpsimd.affine_select(out=IDENT[:, :], in_=IDENT[:, :], compare_op=ALU.not_equal, fill=1.0,
                                    base=0, pattern=[[-1, 128]], channel_multiplier=1)\
                .then_inc(const_ready, 1)
            nc.gpsimd.affine_select(out=TRI[:, :], in_=TRI[:, :], compare_op=ALU.is_gt, fill=0.0,
                                    base=0, pattern=[[1, NODE]], channel_multiplier=-1)\
                .then_inc(const_ready, 1)

            for layer in range(2):
                pool.wait_ge(stored[layer], 32 * CHUNKS)

                def gather(i, layer=layer):
                    for r in range(RING):
                        g = RING * i + r + layer * GROUPS
                        wait_count(pool, group_used, g - RING + 1)
                        pool.wait_ge(index_ready, g + 1)
                        pool.sem_inc(wait_carrier, 1)
                        for k in range(GROUP):
                            nc.gpsimd.indirect_dma_start(
                                out=GATHERED[:, r, k, :], out_offset=None, in_=tables[layer],
                                in_offset=bass.IndirectOffsetOnAxis(ap=IDX[:, r, k:k + 1], axis=0))\
                                .then_inc(gathered[r], 16)

                gather(0)
                with pool.Fori(1, ROUNDS) as i:
                    gather(i)

                def table_rows(c, p):
                    pool.wait_ge(staged, c + 1)
                    nc.gpsimd.tensor_copy(H[:, ds(2 * c, 2), 0:D], STAGE[0:NODE, p, :, :]).then_inc(h1_ready, 1)

                if layer == 0:
                    chunks(pool, table_rows)

            def split_parts(weight, loaded, high, low):
                for product in range(2):
                    nc.gpsimd.tensor_copy(weight[:, 0, product, :], loaded[:, product, :]).then_inc(high, 1)
                for product in range(2):
                    pool.wait_ge(high, product + 1)
                    nc.gpsimd.tensor_tensor(weight[:, 1, product, :], loaded[:, product, :],
                                            weight[:, 0, product, :].bitcast(F32), ALU.subtract).then_inc(low, 1)

            pool.wait_ge(shared_in, 32)
            split_parts(SHARED_W, SHARED_LOADED, shared_high_w, shared_split)

            def first_parts(c):
                pool.wait_ge(feat2, CHUNKS)
                pool.wait_ge(logit_kept, CHUNKS)
                if c:
                    pool.wait_ge(hidden, NF // 2 * c)
                nc.gpsimd.tensor_copy(SHARED_FEAT[:, 0, :, :], feat[:, :, CH * c:CH * (c + 1)]).then_inc(first_high, 1)
                pool.wait_ge(first_high, c + 1)
                nc.gpsimd.tensor_tensor(SHARED_FEAT[:, 1, :, :], feat[:, :, CH * c:CH * (c + 1)],
                                        SHARED_FEAT[:, 0, :, :].bitcast(F32), ALU.subtract).then_inc(first_feat, 1)

            def first_gelu(c, j):
                pool.wait_ge(shared_high, NF // 2 * c + j + 1)
                pair = slice(2 * j, 2 * j + 2)
                nc.gpsimd.tensor_tensor(SHARED_GELU[:, 1, pair, :], SHARED_GELU_ALL[:, pair, :],
                                        SHARED_GELU[:, 0, pair, :].bitcast(F32), ALU.subtract).then_inc(first_low, 1)

            first_parts(0)
            for c in range(2):
                for j in range(NF // 2):
                    first_gelu(c, j)
                if c == 0:
                    first_parts(1)

            pool.wait_ge(filled, 16 * HB * ROUNDS)

            def scatter(t, q):
                pool.wait_ge(send_ready, 3 * t + 3)
                pool.sem_inc(wait_carrier, 1)
                for k in range(TOPK):
                    nc.gpsimd.indirect_dma_start(
                        out=slots, out_offset=bass.IndirectOffsetOnAxis(ap=POS32[:, q, k:k + 1], axis=0),
                        in_=SENDROW[q], in_offset=None).then_inc(scattered[q], 16)

            with pool.Fori(0, TILES // SEND) as i:
                for q in range(SEND):
                    scatter(SEND * i + q, q)
            for q in range(TILES % SEND):
                scatter(TILES // SEND * SEND + q, q)
            for q in range(SEND):
                pool.wait_ge(scattered[q], 32 * (TILES // SEND + (q < TILES % SEND)))
            load_slots(pool, 0, first_slots_in)
            pool.wait_ge(expert_in[0], 32)
            split_parts(WEIGHT[0], LOADED[0], w_high[0], w_split[0])
            pool.wait_ge(ffn_done, CHUNKS)
            pool.dma_start(B2X, b2p.partition_broadcast(128)).then_inc(b2_in, 16)

            pool.wait_ge(out_stored, 32 * CHUNKS)
            pool.wait_ge(spare_zero, 16)
            pool.wait_ge(off_ready, 1)
            pool.sem_inc(slot_free, 1)
            total = pool.value_load(OFFI[0:1, EXPERTS:EXPERTS + 1], min_val=1, max_val=SLOT_BLOCKS - 1)
            with pool.Fori(0, total) as s:
                pool.wait_ge(slot_row, 3 * s + 4)
                pool.sem_inc(wait_carrier, 1)
                for h in range(HB):
                    nc.gpsimd.indirect_dma_start(
                        out=out, out_offset=bass.IndirectOffsetOnAxis(ap=TOKEN[:, h:h + 1], axis=0),
                        in_=SLOTOUT[:, h, :], in_offset=None, compute_op=ALU.add).then_inc(slot_added, 16)
                pool.wait_ge(slot_added, 32 * (s + 1))
                pool.sem_inc(slot_free, 1)

        @block.scalar
        def _(act):
            act.dma_start(SRC, src).then_inc(edges_in, 16)
            act.dma_start(DSTI, dst).then_inc(edges_in, 16)
            act.dma_start(VEC[:, :, :], vecs).then_inc(vec_in, 16)
            for i, w in enumerate((w1a, w1b, w2a, w2b)):
                act.dma_start(W[i // 2][i % 2], w.rearrange("(k p) o -> p k o", p=128)).then_inc(gnnw_in, 16)
            act.dma_start(ROWS[:, :, :], rows.partition_broadcast(NODE)).then_inc(rows_in, 16)
            act.dma_start(WR[:, :, :], wr.rearrange("(k p) e -> p k e", p=128)).then_inc(ffn_small_in, 16)
            act.dma_start(B1[:, :, :], b1).then_inc(ffn_small_in, 16)
            def ln_sqrt(i):
                act.wait_ge(moments_in, i + 1)
                t = piece_tiles(i)
                nc.scalar.activation(LN[:, 0, t], MV[:, t, 1], ACT.Sqrt, bias=EPST[0:NODE]).then_inc(ln_std, 1)

            def normalise(c, p, done):
                for i in range(2):
                    t = 2 * c + i
                    nc.scalar.activation(STAGE[0:NODE, p, i, :].unsqueeze(1), X[:, ds(t, 1), :], ACT.Identity,
                                         scale=LN[:, 1, ds(t, 1)], bias=LN[:, 2, ds(t, 1)]).then_inc(done, 1)

            def keep_turned0(c, p):
                act.wait_ge(turned0, c + 1)
                nc.scalar.copy(feat[:, :, ds(CH * c, CH)], turn_psum[p]).then_inc(feat0, 1)

            def normalise0(c, p):
                normalise(c + 1, 1 - p, staged0)
                keep_turned0(c, p)

            for i in range(PIECES):
                ln_sqrt(i)
                act.wait_ge(ln_ready, i + 1)
                normalise(PIECE[i], 0, staged0)
                chunks(act, normalise0, PIECE[i], PIECE[i + 1] - 1)
                keep_turned0(PIECE[i + 1] - 1, (PIECE[i + 1] - 1) % 2)

            def bn_sqrt(n):
                act.wait_ge(dve_bn, 2 * n + 2)
                nc.scalar.activation(BN[:, 2, :, 0], BN[:, 0, :, 1], ACT.Sqrt, bias=EPST).then_inc(bn_std, 1)

            bn_sqrt(0)
            act.wait_ge(bn_ready, 1)

            def stage_h0(c, p):
                wait_count(act, turned_back, c - 1)
                for k in range(KD):
                    nc.scalar.activation(RT[p][:, k, :], feat[:, k, ds(CH * c, CH)], ACT.Identity,
                                         scale=BN[:, 3, k, 0:1], bias=BN[:, 5, k, 0:1]).then_inc(h0_staged, 1)

            chunks(act, stage_h0)
            act.wait_ge(edges_in, 32)
            for r in range(RING):
                nc.scalar.copy(IDX[:, r, :], SRC[:, GROUP * r:GROUP * (r + 1)]).then_inc(index_ready, 1)
            act.wait_ge(h0_staged, KD * CHUNKS)
            for k in range(KD):
                for i in range(5):
                    part = feat[:, k, i * (N // 5):(i + 1) * (N // 5)]
                    nc.scalar.activation(part, part, ACT.Identity, scale=BN[:, 3, k, 0:1],
                                         bias=BN[:, 5, k, 0:1]).then_inc(h0_turned, 1)
            def fill_slots(start, count):
                for h in range(HB):
                    act.dma_start(slots.rearrange("(s h p) r -> p h s r", h=HB, p=128)[:, h, ds(start, count), :],
                                  FILL[:, h:h + 1, :].to_broadcast([128, count, ROW])).then_inc(filled, 16)

            per_round = SLOT_BLOCKS // (ROUNDS - 1)
            last_fill = SLOT_BLOCKS - per_round * (ROUNDS - 1)
            act.wait_ge(const_ready, 3)
            act.dma_start(out[N:N + BLOCK, :].rearrange("(h p) d -> p h d", p=128), FILL[:, :, 0:D])\
                .then_inc(spare_zero, 16)
            act.wait_ge(vec_in, 16)
            act.sem_inc(z_kept, 2 * KD)
            for layer in range(2):
                if layer == 0:
                    act.wait_ge(edges_in, 32)
                    act.wait_ge(table_ready, 3)

                base = layer * CHUNKS

                def keep_z(c, base=base, layer=layer):
                    act.wait_ge(z_ready, c + base + 1)
                    act.sem_inc(act_carrier, 1)
                    for o in range(KD):
                        nc.scalar.activation(feat[:, o:o + 1, ds(CH * c, CH)], z_psum[:, ds(c % 2, 1), o, :],
                                             ACT.Identity, bias=VEC[:, 2 + 3 * layer, o:o + 1]).then_inc(z_kept, 1)

                def keep_sums(i, layer=layer):
                    for r in range(RING):
                        g = RING * i + r
                        first = act.value_load(TABLE[0:1, 0, ds(g, 1)], min_val=0, max_val=GROUPS * TILES)
                        end = act.value_load(TABLE[0:1, 1, ds(g, 1)], min_val=1, max_val=GROUPS * TILES)
                        shift = act.value_load(TABLE[0:1, 2, ds(g, 1)], min_val=-GROUPS * TILES, max_val=TILES)
                        with act.Fori(first, end) as s:
                            j = nc.s_assert_within(s + shift, 0, TILES - 1, skip_runtime_bounds_check_because=
                                                   "step + shift runs from a group's lowest to its highest node tile")
                            act.wait_ge(summed[layer], s + 1)
                            nc.scalar.copy(feat[:, :, ds(NODE * j, NODE)], sum_psum[:, ds(2 * (s % 2), 2), :])\
                                .then_inc(kept[layer], 1)
                        act.sem_inc(group_used, 1)
                        if not (isinstance(i, int) and i == ROUNDS - 1):
                            act.wait_ge(gathered[r], 16 * GROUP * (i + 1 + layer * ROUNDS))
                            nc.scalar.copy(IDX[:, r, :], SRC[:, ds(GROUP * (g + RING), GROUP)])\
                                .then_inc(index_ready, 1)

                if layer == 1:
                    for r in range(RING):
                        act.wait_ge(gathered[r], 16 * GROUP * ROUNDS)
                    for r in range(RING):
                        nc.scalar.copy(IDX[:, r, :], SRC[:, GROUP * r:GROUP * (r + 1)]).then_inc(index_ready, 1)
                with act.Fori(0, ROUNDS - 1) as i:
                    keep_sums(i)
                    final_chunks(act, i, keep_z)
                    if layer == 0:
                        fill_slots(i * per_round, per_round)
                if layer == 0:
                    fill_slots((ROUNDS - 1) * per_round, last_fill)
                keep_sums(ROUNDS - 1)
                final_chunks(act, ROUNDS - 1, keep_z)
                total = act.value_load(TABLE[0:1, 1, GROUPS - 1:GROUPS], min_val=1, max_val=GROUPS * TILES)
                act.wait_ge(kept[layer], total + 2)
                act.sem_inc(agg_done, 1)

                remaining_chunks(act, keep_z)
                bn_sqrt(layer + 1)
                act.wait_ge(bn_ready, layer + 2)
                def relu_norm(c, p, base=base):
                    wait_count(act, y_ready, c + base - 1)
                    for k in range(KD):
                        nc.scalar.activation(RT[p][:, k, :], feat[:, k, ds(CH * c, CH)], ACT.Relu,
                                             scale=BN[:, 3, k, 0:1], bias=BN[:, 5, k, 0:1]).then_inc(relu_ready, 1)

                def keep_h1(c, p):
                    if not last(c):
                        relu_norm(c + 1, 1 - p)
                    act.wait_ge(y_taken, c + 1)
                    wait_count(act, turned, c - 1)
                    wait_count(act, h1_ready, c - 1)
                    nc.scalar.activation(STAGE[0:NODE, p, :, :], TMP[:, p, :, :], ACT.Relu).then_inc(staged, 1)

                if layer == 0:
                    relu_norm(0, 0)
                    chunks(act, keep_h1)
                else:
                    chunks(act, relu_norm)

            act.wait_ge(moments_mid, 1)
            nc.scalar.activation(LN[:, 0, :], MV[:, :, 1], ACT.Sqrt, bias=EPST[0:NODE]).then_inc(ln2_std, 1)
            act.wait_ge(ln2_ready, 1)

            def turn_rows(c, p):
                if not last(c):
                    normalise(c + 1, 1 - p, staged2)
                act.wait_ge(turned2, c + 1)
                wait_count(act, feat2, c - 1)
                nc.scalar.copy(RT[p], turn_psum[p]).then_inc(half2, 1)

            normalise(0, 0, staged2)
            chunks(act, turn_rows)
            act.wait_ge(logit_max, 1)
            nc.scalar.activation(LOGIT, LOGIT, ACT.Exp).then_inc(exp_ready, 1)

            act.wait_ge(ffn_small_in, 32)
            with act.Fori(0, CHUNKS) as c:
                def shared_gelu_high(j):
                    act.wait_ge(gelu_done, NF * c + 2 * j + 2)
                    nc.scalar.copy(SHARED_GELU[:, 0, 2 * j:2 * j + 2, :], SHARED_GELU_ALL[:, 2 * j:2 * j + 2, :])\
                        .then_inc(shared_high, 1)

                for j in range(NF // 2):
                    act.wait_ge(hidden, NF // 2 * c + j + 1)
                    for f in (2 * j, 2 * j + 1):
                        nc.scalar.activation(SHARED_GELU_ALL[:, f, :], hidden_psum[f], ACT.Gelu,
                                             bias=B1[:, 0, f:f + 1]).then_inc(gelu_done, 1)
                    if j:
                        shared_gelu_high(j - 1)
                shared_gelu_high(NF // 2 - 1)

            act.wait_ge(slot_turned, 1)
            act.wait_ge(slot_meta, 1)
            load_slots(act, 1, slot_in)

            def gelu_block(e, s, load_next=None):
                def high(j):
                    act.wait_ge(slot_gelu, NF * s + 2 * j + 2)
                    nc.scalar.copy(SLOTGELU[:, 0, 2 * j:2 * j + 2, :], GELU_ALL[:, 2 * j:2 * j + 2, :])\
                        .then_inc(gelu_high, 1)

                for j in range(NF // 2):
                    act.wait_ge(slot_hidden, NF // 2 * s + j + 1)
                    act.sem_inc(act_carrier, 1)
                    for f in (2 * j, 2 * j + 1):
                        nc.scalar.activation(GELU_ALL[:, f, :], slot_hidden_psum[f], ACT.Gelu,
                                             bias=B1[:, ds(e + 1, 1), f]).then_inc(slot_gelu, 1)
                    if j == 0 and load_next is not None:
                        load_next()
                    if j:
                        high(j - 1)
                high(NF // 2 - 1)

            def expert(e, q, count):
                first = act.value_load(OFFI[0:1, ds(e, 1)], min_val=0, max_val=SLOT_BLOCKS - 2)
                end = act.value_load(OFFI[0:1, ds(e + 1, 1)], min_val=1, max_val=SLOT_BLOCKS - 1)
                if count is None:
                    gelu_block(e, first)
                else:
                    gelu_block(e, first, lambda: load_expert(act, e + 1, 1 - q, expert_in[1 - q]))
                    act.wait_ge(expert_in[1 - q], 32 * (count + 1))
                    for product in range(2):
                        nc.scalar.copy(WEIGHT[1 - q][:, 0, product, :], LOADED[1 - q][:, product, :])\
                            .then_inc(w_high[1 - q], 1)
                second = act.snap(first + 1)
                with act.If(second < end), act.Fori(second, end) as s:
                    gelu_block(e, s)

            act.wait_ge(off_ready, 1)
            with act.Fori(0, EXPERTS // 2 - 1) as i:
                expert(2 * i, 0, i)
                expert(2 * i + 1, 1, i + 1)
            expert(EXPERTS - 2, 0, EXPERTS // 2 - 1)
            expert(EXPERTS - 1, 1, None)

        @block.tensor
        def _(pe):
            for l in range(2):
                pe.sem_inc(onehot_used[l], 2)
            pe.sem_inc(slot_ffn, 1)
            pe.wait_ge(const_ready, 2)

            def turn(c, p, ready, turned_count, taken, per, base=0):
                pe.wait_ge(ready, per * (c + base + 1))
                wait_count(pe, taken[0], taken[1] * (c + base - 1))
                for i in range(2):
                    for k in range(KD):
                        t = nc.tensor.transpose(turn_psum[p][:, k, i * NODE:(i + 1) * NODE],
                                                STAGE[0:NODE, p, i, k * 128:(k + 1) * 128],
                                                IDENT[0:NODE, 0:NODE])
                t.then_inc(turned_count, 1)

            chunks(pe, lambda c, p: turn(c, p, staged0, turned0, (feat0, 1), 2))

            pe.wait_ge(range_ready, 2)
            for i in range(2):
                t = nc.tensor.transpose(PS[0:GROUPS, 5, i * 128:(i + 1) * 128], RANGES[:, i, :], IDENT[:, :])
            t.then_inc(range_turned, 1)
            pe.wait_ge(row_ready, 2)
            for i in range(2):
                t = nc.tensor.transpose(PS[0:1, 6, i * GROUPS:(i + 1) * GROUPS], EXTREMES[0:GROUPS, i:i + 1],
                                        IDENT[0:GROUPS, 0:GROUPS])
            t.then_inc(row_turned, 1)

            def turn_back(c, p):
                pe.wait_ge(h0_staged, KD * (c + 1))
                wait_count(pe, h0_ready, c - 1)
                for i in range(2):
                    for k in range(KD):
                        t = nc.tensor.transpose(back_psum[p][:, i, k * 128:(k + 1) * 128],
                                                RT[p][:, k, i * NODE:(i + 1) * NODE], IDENT[:, :])
                t.then_inc(turned_back, 1)

            chunks(pe, turn_back)

            pe.wait_ge(table_ready, 3)
            pe.wait_ge(gnnw_in, 16 * 4)
            for layer in range(2):
                def multiply(i, layer=layer):
                    for r in range(RING):
                        g = RING * i + r
                        first = pe.value_load(TABLE[0:1, 0, ds(g, 1)], min_val=0, max_val=GROUPS * TILES)
                        end = pe.value_load(TABLE[0:1, 1, ds(g, 1)], min_val=1, max_val=GROUPS * TILES)
                        shift = pe.value_load(TABLE[0:1, 2, ds(g, 1)], min_val=-GROUPS * TILES, max_val=TILES)
                        with pe.Fori(first, end) as s:
                            j = nc.s_assert_within(s + shift, 0, TILES - 1, skip_runtime_bounds_check_because=
                                                   "step + shift runs from a group's lowest to its highest node tile")
                            bank = 2 * (s % 2)
                            pe.wait_ge(gathered[r], 16 * GROUP * (i + 1 + layer * ROUNDS))
                            pe.wait_ge(kept[layer], s + 1)
                            for half in range(2):
                                pe.wait_ge(onehot_ready[layer], 2 * s + half + 2)
                                for m in range(HALF):
                                    for k in range(KD):
                                        t = nc.tensor.matmul(
                                            sum_psum[:, ds(bank + k, 1), :],
                                            GATHERED[:, r, half * HALF + m, k * 128:(k + 1) * 128],
                                            ONEHOT[half][:, m, :].unsqueeze(1),
                                            start=half == 0 and m == 0, stop=False)
                                t.then_inc(onehot_used[layer], 1)
                            pe.wait_ge(kept[layer], s + 2)
                            for k in range(KD):
                                t = nc.tensor.matmul(sum_psum[:, ds(bank + k, 1), :], IDENT[:, :],
                                                     feat[:, k:k + 1, ds(NODE * j, NODE)], start=False, stop=True)
                            t.then_inc(summed[layer], 1)

                if layer == 0:
                    pe.wait_ge(h0_turned, KD * 5)
                else:
                    pe.wait_ge(h1_turned, CHUNKS)
                base = layer * CHUNKS

                def first_product(c, base=base, layer=layer):
                    pe.wait_ge(z_kept, KD * (c + base + 1))
                    for o in range(KD):
                        for k in range(KD):
                            t = nc.tensor.matmul(z_psum[:, ds(c % 2, 1), o, :], W[layer][0][:, k, o * 128:(o + 1) * 128],
                                                 feat[:, k:k + 1, ds(CH * c, CH)], start=k == 0, stop=k == KD - 1)
                    t.then_inc(z_ready, 1)

                with pe.Fori(0, ROUNDS) as i:
                    multiply(i)
                    final_chunks(pe, i, first_product)
                pe.wait_ge(agg_done, layer + 1)
                remaining_chunks(pe, first_product)

                def second_product(c, p, base=base, layer=layer):
                    pe.wait_ge(relu_ready, KD * (c + base + 1))
                    wait_count(pe, y_taken, c + base - 1)
                    for i in range(2):
                        for k in range(KD):
                            t = nc.tensor.matmul(y_psum[p][:, i, :], RT[p][:, k, i * NODE:(i + 1) * NODE],
                                                 W[layer][1][:, k, :], start=k == 0, stop=k == KD - 1)
                    t.then_inc(y_ready, 1)
                    if layer == 0 and not (isinstance(c, int) and c == 0):
                        turn(c - 1, 1 - p, staged, turned, (h1_turned, 1), 1)

                chunks(pe, second_product)
                if layer == 0:
                    turn(CHUNKS - 1, 0, staged, turned, (h1_turned, 1), 1)

            pe.wait_ge(ffn_small_in, 32)

            def router(c, p):
                if not last(c):
                    turn2(c + 1, 1 - p)
                pe.wait_ge(half2, c + 1)
                wait_count(pe, logit_kept, c - 1)
                for i in range(2):
                    for k in range(KD):
                        t = nc.tensor.matmul(logit_psum[p][:, i, :], RT[p][:, k, i * NODE:(i + 1) * NODE],
                                             WR[:, k, :], start=k == 0, stop=k == KD - 1)
                t.then_inc(logit_done, 1)

            def turn2(c, p):
                turn(c, p, staged2, turned2, (half2, 1), 2)

            turn2(0, 0)
            chunks(pe, router)

            terms = ((0, 0), (0, 1), (1, 0))

            def shared(c):
                first = isinstance(c, int) and c < 2
                if first:
                    pe.wait_ge(first_feat, c + 1)
                else:
                    pe.wait_ge(shared_feat, c - 1)
                wait_count(pe, ffn_taken, c - 1)
                for f in range(NF):
                    for k in range(KD):
                        for n, (wp, xp) in enumerate(terms):
                            t = nc.tensor.matmul(hidden_psum[f], W1S[wp][:, k, f * 128:(f + 1) * 128],
                                                 SHARED_FEAT[:, xp, k, :], start=k == 0 and n == 0,
                                                 stop=k == KD - 1 and n == len(terms) - 1)
                    if f % 2:
                        t.then_inc(hidden, 1)
                if last(c):
                    turn_slots(0)
                for i in range(2):
                    for f in range(NF):
                        if i == 0 and f % 2 == 0:
                            if first:
                                pe.wait_ge(first_low, NF // 2 * c + f // 2 + 1)
                            else:
                                pe.wait_ge(shared_low, NF // 2 * (c - 2) + f // 2 + 1)
                        for n, (wp, xp) in enumerate(terms):
                            t = nc.tensor.matmul(ffn_psum[:, ds(c % 2, 1), i, :],
                                                 SHARED_GELU[:, xp, f, i * NODE:(i + 1) * NODE],
                                                 W2S[wp][:, f:f + 1, :], start=f == 0 and n == 0,
                                                 stop=f == NF - 1 and n == len(terms) - 1)
                t.then_inc(ffn_done, 1)

            pe.wait_ge(shared_split, 2)
            shared(0)
            pe.wait_ge(mask_ready, 1)
            mask = CUM.rearrange("p t e -> p (t e)")
            nc.tensor.matmul(PS[0:NODE, 6, 0:TE], TRI[:, :], mask, start=True, stop=True)
            nc.tensor.matmul(PS[:, 7, 0:TE], ONES[0:NODE, :], mask, start=True, stop=True).then_inc(counted, 1)
            shared(1)

            def turn_slots(s):
                if isinstance(s, int):
                    pe.wait_ge(first_slots_in, 16)
                else:
                    pe.wait_ge(slot_in, 16 * s)
                for h in range(HB):
                    for k in range(KD):
                        t = nc.tensor.transpose(slot_turn_psum[:, k, h * 128:(h + 1) * 128],
                                                SLOTROW[:, h, k * 128:(k + 1) * 128], IDENT[:, :])
                t.then_inc(slot_turned, 1)

            with pe.Fori(2, CHUNKS - 1) as c:
                shared(c)
            shared(CHUNKS - 1)

            def expert(e, q, i):
                first = pe.value_load(OFFI[0:1, ds(e, 1)], min_val=0, max_val=SLOT_BLOCKS - 2)
                end = pe.value_load(OFFI[0:1, ds(e + 1, 1)], min_val=1, max_val=SLOT_BLOCKS - 1)
                with pe.Fori(first, end) as s:
                    pe.wait_ge(w_split[q], 2 * (i + 1))
                    pe.wait_ge(slot_feat, s + 1)
                    for f in range(NF):
                        for k in range(KD):
                            for n, (wp, xp) in enumerate(terms):
                                t = nc.tensor.matmul(slot_hidden_psum[f],
                                                     W1X[q][wp][:, k, f * 128:(f + 1) * 128],
                                                     SLOTFEAT[:, xp, k, :], start=k == 0 and n == 0,
                                                     stop=k == KD - 1 and n == len(terms) - 1)
                        if f % 2:
                            t.then_inc(slot_hidden, 1)
                        if f == 3:
                            pe.wait_ge(slot_taken, s + 1)
                    turn_slots(s + 1)
                    for j in range(NF // 2):
                        pe.wait_ge(gelu_low, NF // 2 * s + j + 1)
                        for h in range(HB):
                            for f in (2 * j, 2 * j + 1):
                                for n, (wp, xp) in enumerate(terms):
                                    t = nc.tensor.matmul(slot_ffn_psum[:, h, :],
                                                         SLOTGELU[:, xp, f, h * 128:(h + 1) * 128],
                                                         W2X[q][wp][:, f, :], start=f == 0 and n == 0,
                                                         stop=f == NF - 1 and n == len(terms) - 1)
                    t.then_inc(slot_ffn, 1)

            with pe.Fori(0, EXPERTS // 2) as i:
                expert(2 * i, 0, i)
                expert(2 * i + 1, 1, i)

        @block.vector
        def _(dve):
            chain = [0]

            def link(*instructions):
                for t in instructions:
                    t.then_inc(dve_chain, 1)
                chain[0] += len(instructions)
                dve.wait_ge(dve_chain, chain[0])

            v = nc.vector
            for one_ahead in (*kept, *kept, *onehot_ready, out_ready, slot_taken, slot_row):
                dve.sem_inc(one_ahead, 1)
            dve.wait_ge(pool_const, 10)
            v.tensor_copy(FILL[:, :, D:D + 1], IOTAI[:, 180:182].unsqueeze(2)).then_inc(const_ready, 1)
            link(v.tensor_copy(IOTA[:, :], IOTAI[:, 0:NODE]),
                 v.tensor_copy(NEG[:, :], IOTAI[:, 128:128 + TILES]),
                 v.tensor_copy(DOWN, IOTAI[0:NODE, 184:192]),
                 v.tensor_copy(LN[:, 3, :], IOTAI[0:NODE, 192:192 + TILES]))

            def row_moments(ready, t=slice(0, TILES)):
                even, odd = LNSTAT[:, t, 1], LNSTAT[:, t, 4]
                link(v.tensor_tensor(LN[:, 0, t], even, odd, ALU.add),
                     v.tensor_tensor(LN[:, 1, t], even, odd, ALU.subtract),
                     v.tensor_tensor(MV[:, t, 1], LNSTAT[:, t, 2], LNSTAT[:, t, 5], ALU.add))
                link(v.scalar_tensor_tensor(out=LN[:, 2, t], in0=LN[:, 1, t], scalar=0.25, in1=LN[:, 1, t],
                                            op0=ALU.mult, op1=ALU.mult),
                     v.tensor_scalar(MV[:, t, 0], LN[:, 0, t], 0.5, None, ALU.mult))
                link(v.scalar_tensor_tensor(out=MV[:, t, 1], in0=MV[:, t, 1], scalar=1.0 / D, in1=LN[:, 2, t],
                                            op0=ALU.mult, op1=ALU.add))
                dve.sem_inc(ready, 1)

            def layer_norm_scale(std, ready, count=1, t=slice(0, TILES)):
                dve.wait_ge(std, count)
                link(v.reciprocal(LN[:, 1, t], LN[:, 0, t]))
                v.scalar_tensor_tensor(out=LN[:, 2, t], in0=MV[:, t, 0], scalar=-1.0, in1=LN[:, 1, t],
                                       op0=ALU.mult, op1=ALU.mult).then_inc(ready, 1)

            def layer_norm_piece(i):
                t = piece_tiles(i)
                dve.wait_ge(x_in[i], 32)

                def stats(tile, count):
                    for j in range(count):
                        v.bn_stats(LNSTAT[:, ds(tile + j, 1), :], X[:, ds(tile + j, 1), :]).then_inc(ln_stats, 1)

                with dve.Fori(t.start // 4, t.stop // 4) as quad:
                    stats(4 * quad, 4)
                stats(t.stop // 4 * 4, t.stop % 4)
                dve.wait_ge(ln_stats, t.stop)
                row_moments(moments_in, t)

            def scale_piece(i):
                layer_norm_scale(ln_std, ln_ready, i + 1, piece_tiles(i))

            def count0(c, p):
                dve.wait_ge(feat0, c + 1)
                for k in range(KD):
                    v.bn_stats(BNSTAT[:, k, ds(c, 1), :], feat[:, k, ds(CH * c, CH)].unsqueeze(1))\
                        .then_inc(bn0_counted, 1)

            layer_norm_piece(0)
            scale_piece(0)
            for i in range(PIECES - 1):
                layer_norm_piece(i + 1)
                chunks(dve, count0, PIECE[i], PIECE[i + 1])
                scale_piece(i + 1)

            dve.wait_ge(edges_in, 32)
            link(v.tensor_copy(DST, DSTI))
            link(v.tensor_scalar(TILEOF, DST, 1.0 / NODE, 0.5 / NODE - 0.5, ALU.mult, ALU.add))
            link(v.tensor_scalar(TILEOF, TILEOF, ROUND, None, ALU.add))
            link(v.tensor_scalar(TILEOF, TILEOF, ROUND, None, ALU.subtract))
            by_group = TILEOF.rearrange("p (g k) -> p g k", k=GROUP)
            v.tensor_reduce(RANGES[:, 0, :], by_group, AX.X, ALU.max).then_inc(range_ready, 1)
            v.tensor_reduce(RANGES[:, 1, :], by_group, AX.X, ALU.min).then_inc(range_ready, 1)

            chunks(dve, count0, PIECE[PIECES - 1], CHUNKS)
            dve.wait_ge(bn0_counted, KD * CHUNKS)

            def batch_norm(n, gamma, beta):
                for k in range(KD):
                    v.bn_aggr(BN[:, 0, k, :], BNSTAT[:, k, :, :].rearrange("p c s -> p (c s)"))\
                        .then_inc(dve_bn, 1)
                dve.wait_ge(bn_std, n + 1)
                link(v.reciprocal(BN[:, 1, :, 0], BN[:, 2, :, 0]))
                link(v.tensor_tensor(BN[:, 3, :, 0], BN[:, 1, :, 0], VEC[:, gamma, :], ALU.mult))
                link(v.tensor_tensor(BN[:, 4, :, 0], BN[:, 0, :, 0], BN[:, 3, :, 0], ALU.mult))
                v.tensor_tensor(BN[:, 5, :, 0], VEC[:, beta, :], BN[:, 4, :, 0], ALU.subtract)\
                    .then_inc(bn_ready, 1)
                dve.wait_ge(bn_ready, n + 1)

            dve.wait_ge(vec_in, 16)
            batch_norm(0, 0, 1)

            dve.wait_ge(range_turned, 1)
            turned_ranges = PS[0:GROUPS, 5, 0:256].rearrange("p (a q) -> p a q", a=2)
            v.tensor_reduce(EXTREMES[0:GROUPS, 0:1], turned_ranges[:, 0:1, :], AX.X, ALU.max).then_inc(row_ready, 1)
            v.tensor_reduce(EXTREMES[0:GROUPS, 1:2], turned_ranges[:, 1:2, :], AX.X, ALU.min).then_inc(row_ready, 1)
            dve.wait_ge(row_turned, 1)
            high, low, steps, ends, tile_less_step, firsts = [STEPS[:, i, :] for i in range(6)]
            link(v.tensor_scalar(high, PS[0:1, 6, 0:GROUPS], float(TILES - 1), None, ALU.min),
                 v.tensor_copy(low, PS[0:1, 6, GROUPS:2 * GROUPS]))
            link(v.scalar_tensor_tensor(out=steps, in0=high, scalar=1.0, in1=low, op0=ALU.add,
                                        op1=ALU.subtract))
            link(v.tensor_scalar(steps, steps, 1.0, None, ALU.max),
                 v.tensor_scalar(low, low, float(TILES - 1), None, ALU.min))
            link(v.tensor_tensor_scan(ends, ONES[0:1, 0:1].to_broadcast([1, GROUPS]), steps, 0.0, ALU.mult, ALU.add))
            link(v.tensor_tensor(firsts, ends, steps, ALU.subtract))
            link(v.tensor_tensor(tile_less_step, low, firsts, ALU.subtract))
            lowest, other = STEPS[:, 6, 0:ROUNDS], STEPS[:, 7, 0:ROUNDS]
            link(v.tensor_reduce(lowest, low.rearrange("o (i r) -> o i r", r=RING), AX.X, ALU.min),
                 v.memset(FINAL[:, 0:2], 0))
            span = 1
            while span < ROUNDS:
                link(v.tensor_tensor(other[:, 0:ROUNDS - span], lowest[:, 0:ROUNDS - span],
                                     lowest[:, span:ROUNDS], ALU.min),
                     v.tensor_copy(other[:, ROUNDS - span:ROUNDS], lowest[:, ROUNDS - span:ROUNDS]))
                lowest, other, span = other, lowest, 2 * span
            link(v.tensor_scalar(other, lowest, 0.5, -0.25, ALU.mult, ALU.add))
            link(v.tensor_scalar(other, other, ROUND, None, ALU.add))
            link(v.tensor_scalar(other, other, ROUND, None, ALU.subtract))
            link(v.tensor_copy(FINAL[:, 2:ROUNDS + 2], other))
            v.tensor_copy(TABLE[:, 0, :], firsts).then_inc(table_ready, 1)
            v.tensor_copy(TABLE[:, 1, :], ends).then_inc(table_ready, 1)
            v.tensor_copy(TABLE[:, 2, :], tile_less_step).then_inc(table_ready, 1)

            dve.wait_ge(table_ready, 3)

            def h0(c, p):
                dve.wait_ge(turned_back, c + 1)
                v.tensor_copy(H[:, ds(2 * c, 2), 0:D], back_psum[p]).then_inc(h0_ready, 1)

            chunks(dve, h0)

            dve.wait_ge(table_ready, 3)
            dve.wait_ge(rows_in, 16)
            for layer in range(2):
                def onehots(i, layer=layer):
                    for r in range(RING):
                        g = RING * i + r
                        first = dve.value_load(TABLE[0:1, 0, ds(g, 1)], min_val=0, max_val=GROUPS * TILES)
                        end = dve.value_load(TABLE[0:1, 1, ds(g, 1)], min_val=1, max_val=GROUPS * TILES)
                        shift = dve.value_load(TABLE[0:1, 2, ds(g, 1)], min_val=-GROUPS * TILES, max_val=TILES)
                        with dve.Fori(first, end) as s:
                            j = nc.s_assert_within(s + shift, 0, TILES - 1, skip_runtime_bounds_check_because=
                                                   "step + shift runs from a group's lowest to its highest node tile")
                            dve.wait_ge(onehot_ready[layer], 2 * s + 1)
                            v.tensor_scalar(REL[:, :], DST[:, ds(GROUP * g, GROUP)], NEG[:, ds(j, 1)], None,
                                            ALU.add).then_inc(rel_ready[layer], 1)
                            dve.wait_ge(rel_ready[layer], s + 1)
                            for half in range(2):
                                dve.wait_ge(onehot_used[layer], 2 * s + half + 1)
                                v.tensor_tensor(ONEHOT[half],
                                                IOTA[:, :].unsqueeze(1).to_broadcast([128, HALF, NODE]),
                                                REL[:, half * HALF:(half + 1) * HALF].unsqueeze(2)
                                                .to_broadcast([128, HALF, NODE]), ALU.is_equal)\
                                    .then_inc(onehot_ready[layer], 1)

                base = layer * CHUNKS

                def count(c, base=base):
                    dve.wait_ge(z_kept, KD * (c + base + 3))
                    for k in range(KD):
                        v.bn_stats(BNSTAT[:, k, ds(c, 1), :], feat[:, k, ds(CH * c, CH)].unsqueeze(1))\
                            .then_inc(bn_counted, 1)

                with dve.Fori(0, ROUNDS) as i:
                    onehots(i)
                    final_chunks(dve, i, count, lag=1)
                remaining_chunks(dve, count, lag=1)
                dve.wait_ge(bn_counted, KD * CHUNKS * (layer + 1))
                batch_norm(layer + 1, 3 + 3 * layer, 4 + 3 * layer)

                def keep_turned(c, p):
                    dve.wait_ge(turned, c + 1)
                    v.tensor_copy(feat[:, :, ds(CH * c, CH)], turn_psum[p]).then_inc(h1_turned, 1)

                def row_stats(c):
                    dve.wait_ge(x2_ready, c + 1)
                    for i in range(2):
                        t = 2 * c + i
                        v.bn_stats(LNSTAT[:, ds(t, 1), :], X[:, ds(t, 1), :]).then_inc(x2_stats, 1)

                def take_y(c, p, base=base, layer=layer):
                    dve.wait_ge(y_ready, c + base + 1)
                    if layer == 0:
                        wait_count(dve, staged, c - 1)
                    v.tensor_tensor(TMP[:, p, :, :], y_psum[p],
                                    ROWS[:, layer:layer + 1, :].to_broadcast([NODE, 2, D]), ALU.add)\
                        .then_inc(y_taken, 1)
                    if layer == 0 and not (isinstance(c, int) and c == 0):
                        keep_turned(c - 1, 1 - p)
                    if layer == 1:
                        if not (isinstance(c, int) and c == 0):
                            row_stats(c - 1)
                        dve.wait_ge(y_taken, c + base + 1)
                        v.scalar_tensor_tensor(out=X[:, ds(2 * c, 2), :], in0=TMP[:, p, :, :], scalar=0.0,
                                               in1=X[:, ds(2 * c, 2), :], op0=ALU.max, op1=ALU.add)\
                            .then_inc(x2_ready, 1)

                chunks(dve, take_y)
                if layer == 0:
                    keep_turned(CHUNKS - 1, 0)
                else:
                    row_stats(CHUNKS - 1)

            dve.wait_ge(x2_stats, TILES)
            row_moments(moments_mid)
            layer_norm_scale(ln2_std, ln2_ready)
            dve.wait_ge(ln2_ready, 1)

            def route_in(c, p):
                dve.wait_ge(logit_done, c + 1)
                v.tensor_copy(feat[:, :, ds(CH * c, CH)], RT[p]).then_inc(feat2, 1)
                v.tensor_copy(LOGIT[:, ds(2 * c, 2), :], logit_psum[p]).then_inc(logit_kept, 1)

            chunks(dve, route_in)
            dve.wait_ge(logit_kept, CHUNKS)

            def over_experts(s):
                return s.unsqueeze(2).to_broadcast([NODE, TILES, EXPERTS])

            down = DOWN.unsqueeze(1).to_broadcast([NODE, TILES, EXPERTS])
            link(v.tensor_reduce(S0, LOGIT, AX.X, ALU.max))
            v.tensor_tensor(LOGIT, LOGIT, over_experts(S0), ALU.subtract).then_inc(logit_max, 1)
            dve.wait_ge(exp_ready, 1)
            link(v.tensor_reduce(S1, LOGIT, AX.X, ALU.add))
            link(v.reciprocal(S2, S1))
            link(v.tensor_tensor(LOGIT, LOGIT, over_experts(S2), ALU.mult))
            link(v.tensor_reduce(S0, LOGIT, AX.X, ALU.max))
            link(v.tensor_tensor(TOP1, LOGIT, over_experts(S0), ALU.is_equal))
            link(v.tensor_tensor(CAND, TOP1, down, ALU.mult))
            link(v.tensor_reduce(S1, CAND, AX.X, ALU.max))
            link(v.tensor_tensor(TOP1, down, over_experts(S1), ALU.is_equal))
            link(v.scalar_tensor_tensor(out=CAND, in0=TOP1, scalar=-4.0, in1=LOGIT, op0=ALU.mult, op1=ALU.add))
            link(v.tensor_reduce(S1, CAND, AX.X, ALU.max))
            link(v.tensor_tensor(TOP2, CAND, over_experts(S1), ALU.is_equal))
            link(v.tensor_tensor(CAND, TOP2, down, ALU.mult))
            link(v.tensor_reduce(S2, CAND, AX.X, ALU.max))
            link(v.tensor_tensor(TOP2, down, over_experts(S2), ALU.is_equal))
            link(v.tensor_tensor(CUM, TOP1, TOP2, ALU.add))
            dve.sem_inc(mask_ready, 1)
            link(v.tensor_tensor(S2, S0, S1, ALU.add))
            link(v.reciprocal(S3, S2))
            link(v.tensor_tensor(S0, S0, S3, ALU.mult), v.tensor_tensor(S1, S1, S3, ALU.mult))
            link(v.tensor_tensor(LOGIT, TOP1, over_experts(S0), ALU.mult),
                 v.tensor_tensor(CAND, TOP2, over_experts(S1), ALU.mult))
            link(v.tensor_tensor(TOKENS[:, :, 1:1 + EXPERTS], LOGIT, CAND, ALU.add),
                 v.tensor_copy(TOKENS[:, :, 0:1], LN[:, 3, :].unsqueeze(2)))
            dve.wait_ge(counted, 1)
            before = PS[0:NODE, 6, 0:TE].rearrange("p (t e) -> p t e", t=TILES)
            of_tile = PS[0:NODE, 7, 0:TE].rearrange("p (t e) -> p t e", t=TILES)
            link(*[v.tensor_tensor_scan(CUM2[:, :, e], ONES[0:NODE, 0:TILES], of_tile[:, :, e], 0.0,
                                        ALU.mult, ALU.add) for e in range(EXPERTS)])
            link(v.tensor_tensor(POS, CUM2, of_tile, ALU.subtract))
            link(v.tensor_tensor(POS, POS, before, ALU.add))
            blocks_of, ends_of, starts_of = [OFFF[0:NODE, i, :] for i in range(3)]
            link(v.tensor_scalar(blocks_of, CUM2[:, TILES - 1, :], 1.0 / BLOCK, (BLOCK - 1) / (2 * BLOCK),
                                 ALU.mult, ALU.add))
            link(v.tensor_scalar(blocks_of, blocks_of, ROUND, None, ALU.add))
            link(v.tensor_scalar(blocks_of, blocks_of, ROUND, None, ALU.subtract))
            link(v.tensor_scalar(blocks_of, blocks_of, 1.0, None, ALU.max))
            link(v.tensor_tensor_scan(ends_of, ONES[0:NODE, 0:EXPERTS], blocks_of, 0.0, ALU.mult, ALU.add))
            link(v.tensor_tensor(starts_of, ends_of, blocks_of, ALU.subtract))
            link(v.tensor_copy(OFFI[:, 0:EXPERTS], starts_of[0:1, :]),
                 v.tensor_copy(OFFI[:, EXPERTS:EXPERTS + 1], ends_of[0:1, EXPERTS - 1:EXPERTS]))
            dve.sem_inc(off_ready, 1)
            link(v.scalar_tensor_tensor(out=POS, in0=starts_of.unsqueeze(1).to_broadcast([NODE, TILES, EXPERTS]),
                                        scalar=float(BLOCK), in1=POS, op0=ALU.mult, op1=ALU.add))
            link(v.tensor_tensor(CAND, TOP1, POS, ALU.mult), v.tensor_tensor(CUM2, TOP2, POS, ALU.mult))
            link(v.tensor_reduce(S0, CAND, AX.X, ALU.add), v.tensor_reduce(S1, CUM2, AX.X, ALU.add))
            link(v.tensor_copy(POSI[:, 0, :], S0), v.tensor_copy(POSI[:, 1, :], S1))
            dve.sem_inc(pos_ready, 1)

            def add_shared(c):
                dve.wait_ge(ffn_done, c + 1)
                dve.wait_ge(out_ready, c + 1)
                v.tensor_tensor(TMP[:, 0:1, :, :], ffn_psum[:, ds(c % 2, 1), :, :], ROWS[:, 2:3, :].to_broadcast([NODE, 2, D]).unsqueeze(1), ALU.add)\
                    .then_inc(ffn_taken, 1)
                dve.wait_ge(ffn_taken, c + 1)
                v.tensor_tensor(X[:, ds(2 * c, 2), :], X[:, ds(2 * c, 2), :], TMP[:, 0, :, :], ALU.add)\
                    .then_inc(out_ready, 1)

            def take_slots(s):
                dve.wait_ge(slot_turned, s + 1)
                v.tensor_copy(SLOTFEAT[:, 0, :, :], slot_turn_psum).then_inc(slot_high, 1)
                dve.wait_ge(slot_high, s + 1)
                v.tensor_tensor(SLOTFEAT[:, 1, :, :], slot_turn_psum, SLOTFEAT[:, 0, :, :].bitcast(F32), ALU.subtract)\
                    .then_inc(slot_feat, 1)

            def keep_meta(s):
                v.tensor_copy(META[:, ds(HB * (s % 2), HB), :], SLOTROW[:, :, D:ROW]).then_inc(slot_meta, 1)

            def feat_parts(c):
                dve.wait_ge(hidden, NF // 2 * c)
                v.tensor_copy(SHARED_FEAT[:, 0, :, :], feat[:, :, ds(CH * c, CH)]).then_inc(feat_high, 1)
                dve.wait_ge(feat_high, c - 1)
                v.tensor_tensor(SHARED_FEAT[:, 1, :, :], feat[:, :, ds(CH * c, CH)],
                                SHARED_FEAT[:, 0, :, :].bitcast(F32), ALU.subtract).then_inc(shared_feat, 1)

            def shared_gelu_low(c, j):
                dve.wait_ge(shared_high, NF // 2 * c + j + 1)
                pair = slice(2 * j, 2 * j + 2)
                v.tensor_tensor(SHARED_GELU[:, 1, pair, :], SHARED_GELU_ALL[:, pair, :],
                                SHARED_GELU[:, 0, pair, :].bitcast(F32), ALU.subtract).then_inc(shared_low, 1)

            def send(i, count):
                for q in range(count):
                    t = SEND * i + q
                    wait_count(dve, scattered[q], 32 * i)
                    v.tensor_scalar(SENDROW[q][:, 0:D].unsqueeze(1), X[:, ds(t, 1), :], MV[:, ds(t, 1), 0],
                                    LN[:, 1, ds(t, 1)], ALU.subtract, ALU.mult).then_inc(send_ready, 1)
                    v.tensor_copy(SENDROW[q][:, D:ROW].unsqueeze(1), TOKENS[:, ds(t, 1), :]).then_inc(send_ready, 1)
                    v.tensor_copy(POS32[:, q, :].unsqueeze(2), POSI[:, :, ds(t, 1)]).then_inc(send_ready, 1)
                dve.wait_ge(send_ready, 3 * (SEND * i + count))

            def shared_chunk(c, tiles=0):
                if tiles:
                    send(c - 1, tiles)
                for j in range(NF // 2):
                    shared_gelu_low(c, j)
                if last(c):
                    take_slots(0)
                    keep_meta(0)
                else:
                    feat_parts(c + 1)
                add_shared(c)

            feat_parts(2)
            send(0, SEND)
            add_shared(0)
            add_shared(1)
            sends = TILES // SEND
            with dve.Fori(2, sends + 1) as c:
                shared_chunk(c, SEND)
            shared_chunk(sends + 1, TILES % SEND)
            with dve.Fori(sends + 2, CHUNKS - 1) as c:
                shared_chunk(c)
            shared_chunk(CHUNKS - 1)
            dve.wait_ge(b2_in, 16)

            def low(s, j):
                dve.wait_ge(gelu_high, NF // 2 * s + j + 1)
                pair = slice(2 * j, 2 * j + 2)
                v.tensor_tensor(SLOTGELU[:, 1, pair, :], GELU_ALL[:, pair, :], SLOTGELU[:, 0, pair, :].bitcast(F32),
                                ALU.subtract).then_inc(gelu_low, 1)

            def finish_block(e, s):
                for j in range(NF // 2):
                    low(s, j)
                take_slots(s + 1)
                keep_meta(s + 1)
                dve.wait_ge(slot_ffn, s + 2)
                dve.wait_ge(slot_row, 3 * s + 1)
                v.tensor_tensor(SLOTSUM, slot_ffn_psum, B2X[:, ds(e, 1), :].to_broadcast([128, HB, D]), ALU.add)\
                    .then_inc(slot_taken, 1)
                dve.wait_ge(slot_taken, s + 2)
                dve.wait_ge(slot_free, s + 1)
                for h in range(HB):
                    v.tensor_scalar(SLOTOUT[:, h:h + 1, :], SLOTSUM[:, h:h + 1, :],
                                    META[:, ds(HB * (s % 2) + h, 1), ds(e + 1, 1)], None, ALU.mult)\
                        .then_inc(slot_row, 1)
                v.tensor_copy(TOKEN[:, :].unsqueeze(2), META[:, ds(HB * (s % 2), HB), 0:1]).then_inc(slot_row, 1)

            def finish_expert(e, q, count):
                first = dve.value_load(OFFI[0:1, ds(e, 1)], min_val=0, max_val=SLOT_BLOCKS - 2)
                end = dve.value_load(OFFI[0:1, ds(e + 1, 1)], min_val=1, max_val=SLOT_BLOCKS - 1)
                finish_block(e, first)
                if count is not None:
                    for product in range(2):
                        dve.wait_ge(w_high[1 - q], 2 * count + product + 1)
                        v.tensor_tensor(WEIGHT[1 - q][:, 1, product, :], LOADED[1 - q][:, product, :],
                                        WEIGHT[1 - q][:, 0, product, :].bitcast(F32), ALU.subtract)\
                            .then_inc(w_split[1 - q], 1)
                second = dve.snap(first + 1)
                with dve.If(second < end), dve.Fori(second, end) as s:
                    finish_block(e, s)

            with dve.Fori(0, EXPERTS // 2 - 1) as i:
                finish_expert(2 * i, 0, i)
                finish_expert(2 * i + 1, 1, i + 1)
            finish_expert(EXPERTS - 2, 0, EXPERTS // 2 - 1)
            finish_expert(EXPERTS - 1, 1, None)


def kernel(x, src, dst, L0_gnn_g0, L0_gnn_b0, L0_gnn_W1a, L0_gnn_b1a, L0_gnn_g1, L0_gnn_bt1, L0_gnn_W1b,
           L0_gnn_b1b, L0_gnn_W2a, L0_gnn_b2a, L0_gnn_g2, L0_gnn_bt2, L0_gnn_W2b, L0_gnn_b2b, L0_ffn_Wr,
           L0_ffn_W1s, L0_ffn_b1s, L0_ffn_W2s, L0_ffn_b2s, L0_ffn_W1p, L0_ffn_b1p, L0_ffn_W2p, L0_ffn_b2p):
    import numpy as np
    import concourse.bacc as bacc
    from concourse import mybir
    from concourse.bass_utils import run_bass_kernel_spmd

    def by_tile(a, fill):
        a = np.pad(np.asarray(a), (0, EDGE_TILES * 128 - E), constant_values=fill)
        return np.ascontiguousarray(a.reshape(EDGE_TILES, 128).T)

    def columns(*vectors):
        a = np.stack([np.asarray(v) for v in vectors])
        return np.ascontiguousarray(a.reshape(len(vectors), -1, 128).transpose(2, 0, 1))

    arrays = {
        "x": np.asarray(x), "src": by_tile(src, 0), "dst": by_tile(dst, FAR),
        "vecs": columns(L0_gnn_g0, L0_gnn_b0, L0_gnn_b1a, L0_gnn_g1, L0_gnn_bt1, L0_gnn_b2a, L0_gnn_g2,
                        L0_gnn_bt2),
        "w1a": np.asarray(L0_gnn_W1a), "w1b": np.asarray(L0_gnn_W1b),
        "w2a": np.asarray(L0_gnn_W2a), "w2b": np.asarray(L0_gnn_W2b),
        "rows": np.stack([np.asarray(v) for v in (L0_gnn_b1b, L0_gnn_b2b, L0_ffn_b2s)]),
        "wr": np.asarray(L0_ffn_Wr), "w1s": np.asarray(L0_ffn_W1s), "w2s": np.asarray(L0_ffn_W2s),
        "b1": columns(L0_ffn_b1s, *np.asarray(L0_ffn_b1p)),
        "w1p": np.asarray(L0_ffn_W1p), "w2p": np.asarray(L0_ffn_W2p), "b2p": np.asarray(L0_ffn_b2p),
    }
    nc = bacc.Bacc("TRN2", target_bir_lowering=False, num_devices=1)
    args = {n: nc.dram_tensor(f"in_{n}", a.shape, mybir.dt.from_np(a.dtype), kind="ExternalInput").ap()
            for n, a in arrays.items()}
    out = nc.dram_tensor("out", (N + BLOCK, D), mybir.dt.float32, kind="ExternalOutput").ap()
    build(nc, out=out, **args)
    result = run_bass_kernel_spmd(nc, [{f"in_{n}": a for n, a in arrays.items()}], core_ids=[0])
    return result.results[0]["out"][0:N]
```
